# Optimizing a Trainium2 kernel written in Bass

```python
import numpy as np
import jax
import jax.numpy as jnp

def _softmax(x, axis=-1):
    return jax.nn.softmax(x, axis=axis)

def _gelu(x):
    return jax.nn.gelu(x, approximate=True)

def _silu(x):
    return jax.nn.silu(x)

def _sigmoid(x):
    return jax.nn.sigmoid(x)

def _layernorm(x, axis=-1, eps=1e-05):
    m = jnp.mean(x, axis=axis, keepdims=True)
    v = jnp.var(x, axis=axis, keepdims=True)
    return (x - m) / jnp.sqrt(v + eps)

def _scatter_add(tgt, idx, src, axis=0):
    return tgt.at[idx].add(src)

def _segment_sum(src, seg, n):
    return jax.ops.segment_sum(src, seg, n)
kernel_name = 'mk_vit_tower_d1_tok_img1024_r4_9976d6'

def setup_inputs(seed: int=0):
    np.random.seed(seed)
    _w = jnp.asarray

    def _rec_inputs():
        import jax
        import jax.numpy as jnp
        _rk = jax.random.key(seed)
        x = -0.000222058 + 0.999998 * jax.random.normal(jax.random.fold_in(_rk, 1), (64, 3, 64, 64), jnp.float32)
        return x
    x = _rec_inputs()

    def _L0_tok_setup():
        import jax, jax.numpy as jnp
        import numpy as np
        P = 16
        key = jax.random.key(seed)
        kx, kw, kb = jax.random.split(key, 3)
        B, C, H, W_ = (32, 3, 128, 128)
        in_dim, embed_dim = (C * P * P, 256)
        x = jax.random.normal(kx, (B, C, H, W_), dtype=jnp.float32)
        bound = 1.0 / np.sqrt(in_dim)
        W = jax.random.uniform(kw, (embed_dim, in_dim), minval=-bound, maxval=bound, dtype=jnp.float32)
        b = jax.random.uniform(kb, (embed_dim,), minval=-bound, maxval=bound, dtype=jnp.float32)
        return {'x': x, 'W': W, 'b': b}
    _L0_tok_all = _L0_tok_setup()
    _L0_tok_in = {k: v for k, v in _L0_tok_all.items() if k in ('W', 'b')}
    del _L0_tok_all

    def _L0_attn_setup():
        import jax, jax.numpy as jnp
        import numpy as np
        D = 256
        H = 4
        DK = 64
        DV = 128
        B, T = (4, 512)

        def _l2norm(t):
            return t * jax.lax.rsqrt(jnp.sum(t * t, axis=-1, keepdims=True) + 1e-06)
        key = jax.random.key(seed)
        ks = jax.random.split(key, 6)
        rn = lambda k, shape, scale: jax.random.normal(k, shape, jnp.float32) * scale
        return {'x': rn(ks[0], (B, T, D), 1.0), 'ln_w': jnp.ones((D,), jnp.float32), 'ln_b': jnp.zeros((D,), jnp.float32), 'Wq': rn(ks[1], (D, H * DK), D ** (-0.5)), 'Wk': rn(ks[2], (D, H * DK), D ** (-0.5)), 'Wv': rn(ks[3], (D, H * DV), D ** (-0.5)), 'Wb': rn(ks[4], (D, H), D ** (-0.5)), 'o_norm_w': jnp.ones((DV,), jnp.float32), 'Wo': rn(ks[5], (H * DV, D), (H * DV) ** (-0.5))}
    _L0_attn_all = _L0_attn_setup()
    _L0_attn_in = {k: v for k, v in _L0_attn_all.items() if k in ('ln_w', 'ln_b', 'Wq', 'Wk', 'Wv', 'Wb', 'o_norm_w', 'Wo')}
    del _L0_attn_all

    def _L0_ffn_setup():
        import jax, jax.numpy as jnp
        import numpy as np
        from math import sqrt
        B, S, D, H, E, K, FF = (2, 256, 256, 16, 8, 2, 1024)
        HD = D // H
        EPS = 1e-05

        def _rope_cache(seq_len, hd):
            inv_freq = 1.0 / 10000.0 ** (jnp.arange(0, hd, 2, dtype=jnp.float32) / hd)
            t = jnp.arange(seq_len, dtype=jnp.float32)
            freqs = t[:, None] * inv_freq[None, :]
            emb = jnp.concatenate([freqs, freqs], axis=-1)
            return (jnp.cos(emb), jnp.sin(emb))

        def _rotate_half(x):
            x1, x2 = jnp.split(x, 2, axis=-1)
            return jnp.concatenate([-x2, x1], axis=-1)

        def _layernorm(x, g, b):
            m = jnp.mean(x, axis=-1, keepdims=True)
            v = jnp.var(x, axis=-1, keepdims=True)
            return (x - m) * jax.lax.rsqrt(v + EPS) * g + b

        def _forward(x, Wq, bq, Wk, bk, Wv, bv, Wo, bo, Wg, bg, W1, b1, W2, b2, g1, be1, g2, be2):
            bsz, seq, d = x.shape
            q = (x @ Wq + bq).reshape(bsz, seq, H, HD).transpose(0, 2, 1, 3)
            k = (x @ Wk + bk).reshape(bsz, seq, H, HD).transpose(0, 2, 1, 3)
            v = (x @ Wv + bv).reshape(bsz, seq, H, HD).transpose(0, 2, 1, 3)
            cos, sin = _rope_cache(seq, HD)
            cos = cos[None, None]
            sin = sin[None, None]
            q = q * cos + _rotate_half(q) * sin
            k = k * cos + _rotate_half(k) * sin
            scores = jnp.einsum('bhqd,bhkd->bhqk', q, k) / sqrt(HD)
            attn = jax.nn.softmax(scores, axis=-1)
            ao = jnp.einsum('bhqk,bhkd->bhqd', attn, v)
            ao = ao.transpose(0, 2, 1, 3).reshape(bsz, seq, d)
            attn_out = ao @ Wo + bo
            x1 = _layernorm(x + attn_out, g1, be1)
            gate_logits = x1 @ Wg + bg
            gate_probs = jax.nn.softmax(gate_logits, axis=-1)
            topk_p, topk_i = jax.lax.top_k(gate_probs, K)
            topk_p = topk_p / jnp.sum(topk_p, axis=-1, keepdims=True)
            comb = jnp.sum(jax.nn.one_hot(topk_i, E, dtype=x.dtype) * topk_p[..., None], axis=-2)
            h = jax.nn.gelu(jnp.einsum('bsd,edf->bsef', x1, W1) + b1, approximate=False)
            y = jnp.einsum('bsef,efd->bsed', h, W2) + b2
            moe_out = jnp.einsum('bse,bsed->bsd', comb, y)
            return _layernorm(x1 + moe_out, g2, be2)
        key = jax.random.key(seed)
        ks = jax.random.split(key, 20)
        std = 0.02
        p = lambda k, sh: jax.random.normal(k, sh, dtype=jnp.float32) * std
        return {'x': jax.random.normal(ks[0], (B, S, D), dtype=jnp.float32), 'Wq': p(ks[1], (D, D)), 'bq': jnp.zeros((D,), jnp.float32), 'Wk': p(ks[2], (D, D)), 'bk': jnp.zeros((D,), jnp.float32), 'Wv': p(ks[3], (D, D)), 'bv': jnp.zeros((D,), jnp.float32), 'Wo': p(ks[4], (D, D)), 'bo': jnp.zeros((D,), jnp.float32), 'Wg': p(ks[5], (D, E)), 'bg': jnp.zeros((E,), jnp.float32), 'W1': p(ks[6], (E, D, FF)), 'b1': jnp.zeros((E, FF), jnp.float32), 'W2': p(ks[7], (E, FF, D)), 'b2': jnp.zeros((E, D), jnp.float32), 'g1': jnp.ones((D,), jnp.float32), 'be1': jnp.zeros((D,), jnp.float32), 'g2': jnp.ones((D,), jnp.float32), 'be2': jnp.zeros((D,), jnp.float32)}
    _L0_ffn_all = _L0_ffn_setup()
    _L0_ffn_in = {k: v for k, v in _L0_ffn_all.items() if k in ('Wq', 'bq', 'Wk', 'bk', 'Wv', 'bv', 'Wo', 'bo', 'Wg', 'bg', 'W1', 'b1', 'W2', 'b2', 'g1', 'be1', 'g2', 'be2')}
    del _L0_ffn_all
    return {'x': x, 'L0_tok_W': _L0_tok_in['W'], 'L0_tok_b': _L0_tok_in['b'], 'L0_attn_ln_w': _L0_attn_in['ln_w'], 'L0_attn_ln_b': _L0_attn_in['ln_b'], 'L0_attn_Wq': _L0_attn_in['Wq'], 'L0_attn_Wk': _L0_attn_in['Wk'], 'L0_attn_Wv': _L0_attn_in['Wv'], 'L0_attn_Wb': _L0_attn_in['Wb'], 'L0_attn_o_norm_w': _L0_attn_in['o_norm_w'], 'L0_attn_Wo': _L0_attn_in['Wo'], 'L0_ffn_Wq': _L0_ffn_in['Wq'], 'L0_ffn_bq': _L0_ffn_in['bq'], 'L0_ffn_Wk': _L0_ffn_in['Wk'], 'L0_ffn_bk': _L0_ffn_in['bk'], 'L0_ffn_Wv': _L0_ffn_in['Wv'], 'L0_ffn_bv': _L0_ffn_in['bv'], 'L0_ffn_Wo': _L0_ffn_in['Wo'], 'L0_ffn_bo': _L0_ffn_in['bo'], 'L0_ffn_Wg': _L0_ffn_in['Wg'], 'L0_ffn_bg': _L0_ffn_in['bg'], 'L0_ffn_W1': _L0_ffn_in['W1'], 'L0_ffn_b1': _L0_ffn_in['b1'], 'L0_ffn_W2': _L0_ffn_in['W2'], 'L0_ffn_b2': _L0_ffn_in['b2'], 'L0_ffn_g1': _L0_ffn_in['g1'], 'L0_ffn_be1': _L0_ffn_in['be1'], 'L0_ffn_g2': _L0_ffn_in['g2'], 'L0_ffn_be2': _L0_ffn_in['be2']}

def reference(x, L0_tok_W, L0_tok_b, L0_attn_ln_w, L0_attn_ln_b, L0_attn_Wq, L0_attn_Wk, L0_attn_Wv, L0_attn_Wb, L0_attn_o_norm_w, L0_attn_Wo, L0_ffn_Wq, L0_ffn_bq, L0_ffn_Wk, L0_ffn_bk, L0_ffn_Wv, L0_ffn_bv, L0_ffn_Wo, L0_ffn_bo, L0_ffn_Wg, L0_ffn_bg, L0_ffn_W1, L0_ffn_b1, L0_ffn_W2, L0_ffn_b2, L0_ffn_g1, L0_ffn_be1, L0_ffn_g2, L0_ffn_be2):
    import jax
    import jax.numpy as jnp

    def _L0_tok_ref(x, W, b):
        import jax, jax.numpy as jnp
        import numpy as np
        P = 16
        B, C, H, Wd = x.shape
        h, w = (H // P, Wd // P)
        patches = x.reshape(B, C, h, P, w, P).transpose(0, 2, 4, 1, 3, 5)
        patches = patches.reshape(B, h * w, C * P * P)
        return jnp.einsum('bld,ed->ble', patches, W) + b

    def _L0_attn_ref(x, ln_w, ln_b, Wq, Wk, Wv, Wb, o_norm_w, Wo):
        import jax, jax.numpy as jnp
        import numpy as np
        D = 256
        H = 4
        DK = 64
        DV = 128
        B, T = (4, 512)

        def _l2norm(t):
            return t * jax.lax.rsqrt(jnp.sum(t * t, axis=-1, keepdims=True) + 1e-06)
        Bx, Tx, _ = x.shape
        mu = jnp.mean(x, axis=-1, keepdims=True)
        var = jnp.mean((x - mu) ** 2, axis=-1, keepdims=True)
        normed = (x - mu) * jax.lax.rsqrt(var + 1e-05) * ln_w + ln_b
        silu = jax.nn.silu
        q = _l2norm(silu(normed @ Wq).reshape(Bx, Tx, H, DK)) * DK ** (-0.5)
        k = _l2norm(silu(normed @ Wk).reshape(Bx, Tx, H, DK))
        v = silu(normed @ Wv).reshape(Bx, Tx, H, DV)
        beta = jax.nn.sigmoid(normed @ Wb)
        qT = q.transpose(1, 0, 2, 3)
        kT = k.transpose(1, 0, 2, 3)
        vT = v.transpose(1, 0, 2, 3)
        bT = beta.transpose(1, 0, 2)

        def step(S, inp):
            qt, kt, vt, bt = inp
            pred = jnp.einsum('bhk,bhkv->bhv', kt, S)
            vd = bt[..., None] * (vt - pred)
            S = S + kt[..., None] * vd[..., None, :]
            o = jnp.einsum('bhk,bhkv->bhv', qt, S)
            return (S, o)
        S0 = jnp.zeros((Bx, H, DK, DV), x.dtype)
        _, oT = jax.lax.scan(step, S0, (qT, kT, vT, bT))
        o = oT.transpose(1, 0, 2, 3)
        o = o * jax.lax.rsqrt(jnp.mean(o * o, axis=-1, keepdims=True) + 1e-05) * o_norm_w
        out = o.reshape(Bx, Tx, H * DV) @ Wo
        return x + out

    def _L0_ffn_ref(x, Wq, bq, Wk, bk, Wv, bv, Wo, bo, Wg, bg, W1, b1, W2, b2, g1, be1, g2, be2):
        import jax, jax.numpy as jnp
        import numpy as np
        from math import sqrt
        B, S, D, H, E, K, FF = (2, 256, 256, 16, 8, 2, 1024)
        HD = D // H
        EPS = 1e-05

        def _rope_cache(seq_len, hd):
            inv_freq = 1.0 / 10000.0 ** (jnp.arange(0, hd, 2, dtype=jnp.float32) / hd)
            t = jnp.arange(seq_len, dtype=jnp.float32)
            freqs = t[:, None] * inv_freq[None, :]
            emb = jnp.concatenate([freqs, freqs], axis=-1)
            return (jnp.cos(emb), jnp.sin(emb))

        def _rotate_half(x):
            x1, x2 = jnp.split(x, 2, axis=-1)
            return jnp.concatenate([-x2, x1], axis=-1)

        def _layernorm(x, g, b):
            m = jnp.mean(x, axis=-1, keepdims=True)
            v = jnp.var(x, axis=-1, keepdims=True)
            return (x - m) * jax.lax.rsqrt(v + EPS) * g + b

        def _forward(x, Wq, bq, Wk, bk, Wv, bv, Wo, bo, Wg, bg, W1, b1, W2, b2, g1, be1, g2, be2):
            bsz, seq, d = x.shape
            q = (x @ Wq + bq).reshape(bsz, seq, H, HD).transpose(0, 2, 1, 3)
            k = (x @ Wk + bk).reshape(bsz, seq, H, HD).transpose(0, 2, 1, 3)
            v = (x @ Wv + bv).reshape(bsz, seq, H, HD).transpose(0, 2, 1, 3)
            cos, sin = _rope_cache(seq, HD)
            cos = cos[None, None]
            sin = sin[None, None]
            q = q * cos + _rotate_half(q) * sin
            k = k * cos + _rotate_half(k) * sin
            scores = jnp.einsum('bhqd,bhkd->bhqk', q, k) / sqrt(HD)
            attn = jax.nn.softmax(scores, axis=-1)
            ao = jnp.einsum('bhqk,bhkd->bhqd', attn, v)
            ao = ao.transpose(0, 2, 1, 3).reshape(bsz, seq, d)
            attn_out = ao @ Wo + bo
            x1 = _layernorm(x + attn_out, g1, be1)
            gate_logits = x1 @ Wg + bg
            gate_probs = jax.nn.softmax(gate_logits, axis=-1)
            topk_p, topk_i = jax.lax.top_k(gate_probs, K)
            topk_p = topk_p / jnp.sum(topk_p, axis=-1, keepdims=True)
            comb = jnp.sum(jax.nn.one_hot(topk_i, E, dtype=x.dtype) * topk_p[..., None], axis=-2)
            h = jax.nn.gelu(jnp.einsum('bsd,edf->bsef', x1, W1) + b1, approximate=False)
            y = jnp.einsum('bsef,efd->bsed', h, W2) + b2
            moe_out = jnp.einsum('bse,bsed->bsd', comb, y)
            return _layernorm(x1 + moe_out, g2, be2)
        return _forward(x, Wq, bq, Wk, bk, Wv, bv, Wo, bo, Wg, bg, W1, b1, W2, b2, g1, be1, g2, be2)
    h = _L0_tok_ref(x, L0_tok_W, L0_tok_b)
    h = h + _L0_attn_ref(_layernorm(h, axis=-1), L0_attn_ln_w, L0_attn_ln_b, L0_attn_Wq, L0_attn_Wk, L0_attn_Wv, L0_attn_Wb, L0_attn_o_norm_w, L0_attn_Wo)
    h = h + _L0_ffn_ref(_layernorm(h, axis=-1), L0_ffn_Wq, L0_ffn_bq, L0_ffn_Wk, L0_ffn_bk, L0_ffn_Wv, L0_ffn_bv, L0_ffn_Wo, L0_ffn_bo, L0_ffn_Wg, L0_ffn_bg, L0_ffn_W1, L0_ffn_b1, L0_ffn_W2, L0_ffn_b2, L0_ffn_g1, L0_ffn_be1, L0_ffn_g2, L0_ffn_be2)
    return h

_drawn_inputs = setup_inputs


def setup_inputs(seed=0):
    import zlib

    import numpy as np

    out = dict(_drawn_inputs(seed))
    spreads = {'L0_attn_ln_w': (1.0, 0.2),
     'L0_attn_ln_b': (0.0, 0.1),
     'L0_attn_o_norm_w': (1.0, 0.2),
     'L0_ffn_bq': (0.0, 0.8),
     'L0_ffn_bk': (0.0, 0.8),
     'L0_ffn_bv': (0.0, 0.692),
     'L0_ffn_bo': (0.0, 0.1),
     'L0_ffn_bg': (0.0, 0.444),
     'L0_ffn_b1': (0.0, 0.8),
     'L0_ffn_b2': (0.0, 0.32),
     'L0_ffn_g1': (1.0, 0.2),
     'L0_ffn_be1': (0.0, 0.1),
     'L0_ffn_g2': (1.0, 0.2),
     'L0_ffn_be2': (0.0, 0.1)}
    factors = {'L0_ffn_Wq': 8.0, 'L0_ffn_Wk': 8.0, 'L0_ffn_Wv': 3.354, 'L0_ffn_Wo': 2.747}
    for name, (base, spread) in spreads.items():
        noise = np.random.default_rng([zlib.crc32(name.encode()), seed]).standard_normal(out[name].shape)
        drawn = base * np.exp(spread * noise) if base else spread * noise
        out[name] = jnp.asarray(drawn.astype(out[name].dtype))
    for name, factor in factors.items():
        out[name] = (out[name] * factor).astype(out[name].dtype)
    return out
```

```python
from contextlib import ExitStack

import numpy as np

import concourse.bass as bass
from concourse import mybir

F32 = mybir.dt.float32
I32 = mybir.dt.int32
ALU = mybir.AluOpType
ACT = mybir.ActivationFunctionType
AX = mybir.AxisListType.X
ds = bass.ds

P = 128
D = 256
DC = D // P
IMGS, SEQ = 64, 16
TOK = IMGS * SEQ
NT = TOK // P
PAIRS = NT // 2
KP = 768
KC = KP // P
H, DK, DV = 4, 64, 128
MH, MD = 16, 16
E, FF = 8, 1024
FC = FF // P
SLOT_TILES = 2 * TOK // P + E - 1
EPS = 1e-5
CHOSEN, ROUTED = 26, 46
TAIL1 = 7

C_ID = 0
C_NP = C_ID + P
C_M = C_NP + 2 * P
C_COS = C_M + P
C_SIN = C_COS + 8
C_KEYB = C_SIN + 16
C_HM = C_KEYB + 32
C_VM = C_HM + 8
C_REP = C_VM + 4
C_UP = C_REP + 4 * P
C_ONE = C_UP + P
C_LT = C_ONE + P
C_TH = C_LT + 64
C_SL = C_TH + 8
C_END = C_SL + SLOT_TILES


def constants():
    c = np.zeros((P, C_END), np.float32)
    p = np.arange(P)
    same = p[:, None] // SEQ == p[None, :] // SEQ
    c[:, C_ID:C_ID + P] = np.eye(P)
    c[:, C_NP:C_NP + P] = same & (p[:, None] < p[None, :])
    c[:, C_NP + P:C_NP + 2 * P] = same & (p[:, None] <= p[None, :])
    c[:, C_M:C_M + P] = same & (p[None, :] < p[:, None])
    freq = 1.0 / 10000.0 ** (np.arange(0, MD, 2, dtype=np.float32) / MD)
    ang = (p % SEQ).astype(np.float32)[:, None] * freq[None, :].astype(np.float32)
    c[:, C_COS:C_COS + 8] = np.cos(ang)
    c[:, C_SIN:C_SIN + 16] = np.concatenate([-np.sin(ang), np.sin(ang)], axis=1)
    key = np.arange(32)
    c[:, C_KEYB:C_KEYB + 32] = np.where(p[:, None] % 32 // SEQ == key[None, :] // SEQ, 0.0, -1e30)
    c[:, C_HM:C_HM + 8] = p[:, None] // MD == np.arange(8)[None, :]
    c[:, C_VM:C_VM + 4] = p[:, None] // 32 == np.arange(4)[None, :]
    for j in range(4):
        c[:, C_REP + j * P:C_REP + (j + 1) * P] = p[:, None] == 32 * j + p[None, :] % 32
    c[:, C_UP:C_UP + P] = p[:, None] < p[None, :]
    c[:, C_ONE:C_ONE + P] = 1.0
    e = np.arange(E)
    c[:, C_LT:C_LT + 64] = (e[None, :] < e[:, None]).astype(np.float32).reshape(1, 64)
    c[:, C_TH:C_TH + 8] = P * np.arange(8)
    c[:, C_SL:C_SL + SLOT_TILES] = np.arange(SLOT_TILES)
    return c


SEMS = """
x_in0 x_in1 const_in tokw_in rows_in bias_in attnw_in ffnw_in w1_in w2lo_in w2hi_in zero_in
exponents_set zero_set
wT_mm xT_even_ready wT_ready x_split0 x_split1 xT_mm xT_ready emb_mm h_ready hstat_a hstat_b hstat_ready r1_ready rt_ready
r2_ready n1_ready hres_ready rows_mm cols_ready
n2_ready n2_mm n2T_ready beta_mm qk_mm v_mm beta_act qk_act v_act beta_ready ssq
rn_ready qnorm_ready knorm_ready kb_ready y0_ready kqT_mm kT_mm kqT_ready kT_ready np_mm m_mm np_ready m_ready
y1_mm m2_mm n2p_mm y1_ready m2_ready n2p_ready y2_mm m4_mm n4_mm y2_ready m4_ready n4_ready y3_mm n8_mm
y3_ready n8_ready y4_mm y4_ready o_mm oss_ready orv_ready orms_ready on_ready oT_mm oT_ready wo_mm h2_ready h2s_ready n3_stored
h2stat r3_ready
n3_ready n3b_ready n3_mm n3T_ready aqk_mm av_mm vs_ready vrep_mm qkb_ready ropea_ready ropeb_ready rope_ready
vbd_ready qkT_mm qT_ready kexp_ready score_mm centre exp_ready prob
pT_mm pT_ready pv_mm aoT_ready awo_mm xa_ready xastat r4_ready
x1n_ready x1g_ready x1_ready x1T_mm x1T_ready gate_mm logit_ready
route logit_exp count_mm combT_mm combT_ready b2_mm x1b_ready scattered hb_ready
slot_in0 slot_in1 xgT_mm xgT_ready up_mm up_ready hT_mm act_ready down_mm ys_ready y_out0 y_out1
tail r5_ready fin_ready out_done
""".split()


def tower(nc, A, out):
    with ExitStack() as ctx:
        def sb(name, shape, dt=F32):
            return ctx.enter_context(nc.sbuf_tensor(name, shape, dt))

        S = {name: ctx.enter_context(nc.semaphore(name)) for name in SEMS}

        w1 = sb("w1", [P, E * DC * FF])
        w2 = sb("w2", [P, E * FC * D])
        XL = KC * 512
        x_raw = [w2[:, k * XL:(k + 1) * XL] for k in range(2)]
        x_tok = [w2[:, (2 + k) * XL:(3 + k) * XL] for k in range(2)]
        xT = [w2[:, 4 * XL:5 * XL], w2[:, 0:XL]]
        con = sb("con", [P, C_END])
        hres = sb("hres", [P, NT, D])
        x1 = sb("x1", [P, NT, D])
        cols = sb("cols", [P, 76])
        misc = sb("misc", [P, 400])
        wqk_a = sb("wqk_a", [P, DC, 512])
        wv_a = sb("wv_a", [P, DC, 512])
        wb_a = sb("wb_a", [P, DC, H])
        wo_a = sb("wo_a", [P, H, D])
        wqk_f = sb("wqk_f", [P, DC, 512])
        wv_f = sb("wv_f", [P, DC, D])
        wo_f = sb("wo_f", [P, DC, D])
        wg_f = sb("wg_f", [P, DC, E])
        b2_f = sb("b2_f", [E, D])
        bc = sb("bc", [P, 8 * D + E])
        tokb, bqk, bo = bc[:, 0:D], bc[:, D:3 * D], bc[:, 3 * D:4 * D]
        g1, be1, g2, be2 = (bc[:, (4 + k) * D:(5 + k) * D] for k in range(4))
        bg = bc[:, 8 * D:8 * D + E]

        work = sb("work", [P, 5200])
        tokw = work[:, 0:2 * KP]
        tokwT = work[:, 2 * KP:4 * KP]
        rows = work[0:76, 4 * KP:4 * KP + P]
        ident = con[:, C_ID:C_ID + P]

        def m(a, n):
            return misc[:, a:a + n]
        mv1, ve1, r1, rt, r2 = m(0, 16), m(16, 8), m(24, 8), m(32, 8), m(40, 8)
        mv3, ve3, r3 = ([m(48 + 8 * u + k, n) for u in range(2)] for k, n in ((0, 2), (2, 1), (3, 1)))
        mv4, ve4, r4 = ([m(80 + 8 * u + k, n) for u in range(2)] for k, n in ((0, 2), (2, 1), (3, 1)))
        mv5, ve5, r5 = m(112, 16), m(128, 8), m(136, 8)
        negh = m(144, 8)
        bst = [m(152 + 6 * k, 6) for k in range(8)]
        th = [m(200 + 4 * u, 4) for u in range(2)]
        beta = [m(208 + 4 * u, 4) for u in range(2)]
        ssq = [m(216 + 8 * u, 8) for u in range(2)]
        rn = [m(232 + 8 * u, 8) for u in range(2)]
        oss = [m(248 + 4 * u, 4) for u in range(2)]
        orms = [m(256 + 4 * u, 4) for u in range(2)]
        mx = [m(264 + 16 * u, 16) for u in range(2)]
        sums = [m(296 + 16 * u, 16) for u in range(2)]
        recs = [m(328 + 16 * u, 16) for u in range(2)]
        spare = m(368, 1)
        orv = [m(360 + 4 * u, 4) for u in range(2)]

        LNW, LNB, ONW, BV, G1, BE1, B1 = 0, 2, 4, 5, 7, 9, 11
        ps = ctx.enter_context(nc.psum_tensor("ps", [P, 8, 512], F32))

        def bank(n, a=0, b=512):
            return ps[:, n, a:b]

        xs_dram = nc.dram_tensor("slots_x", [SLOT_TILES * P, D], F32, kind="Internal").ap()
        ys_dram = nc.dram_tensor("slots_y", [SLOT_TILES * P, D], F32, kind="Internal").ap()

        class Delta:
            pass
        dl = []
        for u in range(2):
            b = Delta()
            o = u * 6144
            b.n2 = work[:, u * 256:u * 256 + 256]
            b.h2 = work[:, 1024 + u * 256:1280 + u * 256]
            b.n2T = work[:, 512 + u * 256:768 + u * 256]
            b.qk = w2[:, o:o + 512]
            b.kb = w2[:, o + 512:o + 768]
            b.kT = w2[:, o + 768:o + 1024]
            b.y = [w2[:, o + 1024:o + 1536], w2[:, o + 1536:o + 2048]]
            b.kqT = w2[:, o + 2048:o + 2560]
            b.np = w2[:, o + 2560:o + 3584]
            b.m = w2[:, o + 3584:o + 4096]
            b.m2 = w2[:, o + 4096:o + 4608]
            b.n2p = w2[:, o + 4608:o + 5120]
            b.n4 = w2[:, o + 5120:o + 5632]
            b.sq = w2[:, o + 5632:o + 6144]
            dl.append(b)
        at = []
        for u in range(2):
            b = Delta()
            o = u * 2560
            b.n3 = work[:, o:o + 256]
            b.n3b = work[:, o + 256:o + 512]
            b.n3T = work[:, o + 512:o + 768]
            b.vs = work[:, o + 768:o + 1024]
            b.qkb = work[:, o + 1024:o + 1536]
            b.ta = work[:, o + 1536:o + 2048]
            b.qT = work[:, o + 2048:o + 2304]
            b.aoT = work[:, o + 2304:o + 2560]
            o = E * FC * D // 2 + u * 4096
            b.kexp = w2[:, o:o + 2048]
            b.vbd = w2[:, o + 2048:o + 3072]
            b.sm = w2[:, o + 3072:o + 3584]
            b.pT = w2[:, o + 3584:o + 4096]
            b.tb = b.pT
            b.xa = b.ta[:, 0:256]
            b.x1n = b.ta[:, 256:512]
            b.x1T = b.qkb[:, 0:256]
            at.append(b)
        lg = sb("lg", [P, NT * E])
        o = 0
        rt8 = []
        for k in range(3):
            rt8.append(work[:, o:o + 512])
            o += 512
        small = []
        for k in range(16):
            small.append(work[:, o:o + 72])
            o += 72
        combT = work[0:E, o:o + 2 * 512]
        o += 1024
        lmax, lsum, prob, rank, sel0, sel1, chosen, comb = (small[k][:, 0:64] for k in range(8))
        lmax, lsum = lmax[:, 0:NT], lsum[:, 0:NT]
        cum, pick, slot = small[8], small[9][:, 0:64], small[10][:, 0:64]
        total, tiles, begin, end, picked = (small[11 + k][:, 0:8] for k in range(5))
        xg = [sb(f"xg{u}", [P, D]) for u in range(2)]
        xgT = [sb(f"xgT{u}", [P, D]) for u in range(2)]
        hs = [work[:, u * FF:(u + 1) * FF] for u in range(2)]
        gT = [work[:, (2 + u) * FF:(3 + u) * FF] for u in range(2)]
        ys = [work[:, 4 * FF + u * D:4 * FF + (u + 1) * D] for u in range(2)]
        posi = sb("posi", [P, 2 * NT], I32)
        tilee = sb("tilee", [P, SLOT_TILES], I32)
        wsel = sb("wsel", [P, 2 * NT])
        yg = w1[:, 0:2 * NT * D].rearrange("p (k t d) -> p k t d", k=2, t=NT)
        fin = w1[:, 2 * NT * D:3 * NT * D].rearrange("p (t d) -> p t d", t=NT)

        gathered = [ctx.enter_context(nc.semaphore(f"gathered{t}")) for t in range(NT)]

        def x_split(copy, half, c):
            src = x_raw[half][:, c * 1024:(c + 1) * 1024].rearrange("p (r w j) -> p r w j", r=16, w=4)
            dst = x_tok[half].rearrange("p (w c r j) -> p c r w j", w=4, c=3, r=16)[:, c]
            return copy(dst, src)

        def xT_in(half, q):
            return bank(4 + (KC * half + q) % 3).rearrange("p (w b) -> p w b", w=4)

        def xT_out(half, q):
            return xT[half][:, q * 512:(q + 1) * 512].rearrange("p (b w) -> p w b", w=4)

        def tile_of(buf, t):
            return buf[:, ds(t, 1), :].rearrange("p a d -> p (a d)")

        def eights(ap):
            return ap.rearrange("p (h f) -> p h f", f=8)

        def heads4(ap):
            return ap.rearrange("p (h d) -> p h d", h=H)

        def upto(i, u):
            return 2 * i + (u + 1)

        def rep(ap, shape):
            return ap.broadcast_to(shape)

        def third(i, u, k):
            return 6 * i + (3 * u + k)

        block = ctx.enter_context(nc.Block())

        @block.sync
        def _(sp):
            for half in range(2):
                for c in range(3):
                    src = A["x"][32 * half:32 * half + 32, c].rearrange("b (h r) w -> b h (r w)", r=16)
                    sp.dma_start(x_raw[half][:, c * 1024:(c + 1) * 1024], src).then_inc(S[f"x_in{half}"], 16)
                if half == 0:
                    sp.dma_start(con[:, :], A["consts"]).then_inc(S["const_in"], 16)
                    sp.dma_start(tokw.rearrange("p (c k) -> p c k", c=DC),
                                 A["L0_tok_W"].rearrange("(c p) k -> p c k", p=P)).then_inc(S["tokw_in"], 16)
            for dst, name in ((wqk_a[:, :, 0:256], "L0_attn_Wq"), (wqk_a[:, :, 256:512], "L0_attn_Wk"),
                              (wv_a[:, :, :], "L0_attn_Wv"), (wb_a[:, :, :], "L0_attn_Wb"),
                              (wo_a[:, :, :], "L0_attn_Wo")):
                sp.dma_start(dst, A[name].rearrange("(c p) n -> p c n", p=P)).then_inc(S["attnw_in"], 16)
            for dst, name in ((wqk_f[:, :, 0:256], "L0_ffn_Wq"), (wqk_f[:, :, 256:512], "L0_ffn_Wk"),
                              (wv_f[:, :, :], "L0_ffn_Wv"), (wo_f[:, :, :], "L0_ffn_Wo"),
                              (wg_f[:, :, :], "L0_ffn_Wg")):
                sp.dma_start(dst, A[name].rearrange("(c p) n -> p c n", p=P)).then_inc(S["ffnw_in"], 16)
            sp.dma_start(b2_f[:, :], A["L0_ffn_b2"]).then_inc(S["ffnw_in"], 16)
            for e in range(E):
                sp.dma_start(w1[:, e * DC * FF:(e + 1) * DC * FF].rearrange("p (c f) -> p c f", c=DC),
                             A["L0_ffn_W1"][e].rearrange("(c p) f -> p c f", p=P)).then_inc(S["w1_in"], 16)
            sp.wait_ge(S["zero_set"], 1)
            sp.dma_start(xs_dram.rearrange("(t p) d -> p t d", p=P),
                         rep(xg[0][:, None, :], [P, SLOT_TILES, D])).then_inc(S["zero_in"], 16)

            def w2_load(e, sem):
                sp.dma_start(w2[:, e * FC * D:(e + 1) * FC * D].rearrange("p (c d) -> p c d", c=FC),
                             A["L0_ffn_W2"][e].rearrange("(c p) d -> p c d", p=P)).then_inc(S[sem], 16)
            sp.wait_ge(S["h2_ready"], NT)
            for e in range(E // 2):
                w2_load(e, "w2lo_in")
            sp.wait_ge(S["awo_mm"], NT)
            for e in range(E // 2, E):
                w2_load(e, "w2hi_in")

            def slot_load(t, u, steady):
                if steady:
                    sp.wait_ge(S["xgT_mm"], t - 1)
                sp.dma_start(xg[u][:, :], xs_dram[ds(t * P, P), :]).then_inc(S[f"slot_in{u}"], 16)

            def slot_store(t, u):
                sp.wait_ge(S["ys_ready"], t + 1)
                sp.dma_start(ys_dram[ds(t * P, P), :], ys[u]).then_inc(S[f"y_out{u}"], 16)

            sp.wait_ge(S["scattered"], 16 * 2 * NT)
            slot_load(0, 0, False)
            slot_load(1, 1, False)
            with sp.Fori(0, SLOT_TILES // 2 - 1) as i:
                for u in range(2):
                    slot_load(2 * i + (u + 2), u, True)
                    slot_store(2 * i + u, u)
            slot_load(SLOT_TILES - 1, 0, True)
            for t in range(SLOT_TILES - 3, SLOT_TILES):
                slot_store(t, t % 2)

            for t in range(NT):
                sp.wait_ge(S["fin_ready"], t + 1)
                sp.dma_start(out[t * P:(t + 1) * P, :], fin[:, t, :]).then_inc(S["out_done"], 16)
            sp.wait_ge(S["out_done"], 16 * NT)

        @block.gpsimd
        def _(pool):
            pool.memset(negh, -0.5).then_inc(S["exponents_set"], 1)
            pool.memset(xg[0][:, :], 0.0).then_inc(S["zero_set"], 1)
            pool.wait_ge(S["exponents_set"], 1)

            def inv_root(dst, src, n, sem):
                pool.tensor_tensor(dst, src, negh[:, 0:n], ALU.pow).then_inc(S[sem], 1)

            for half in range(2):
                pool.wait_ge(S[f"x_in{half}"], 48)
                x_split(pool.tensor_copy, half, 2).then_inc(S[f"x_split{half}"], 1)
            for half in range(2):
                a, b = 4 * half, 4 * half + 4
                pool.wait_ge(S["hstat_ready"], half + 1)
                inv_root(r1[:, a:b], ve1[:, a:b], 4, "r1_ready")
                var = mv1.rearrange("p (t k) -> p t k", k=2)[:, a:b, 1]
                pool.wait_ge(S["r1_ready"], half + 1)
                pool.tensor_tensor(rt[:, a:b], var, r1[:, a:b], ALU.mult).then_inc(S["rt_ready"], 1)
                pool.wait_ge(S["rt_ready"], 3 * half + 1)
                pool.tensor_tensor(rt[:, a:b], rt[:, a:b], r1[:, a:b], ALU.mult).then_inc(S["rt_ready"], 1)
                pool.wait_ge(S["rt_ready"], 3 * half + 2)
                pool.tensor_scalar(rt[:, a:b], rt[:, a:b], EPS, None, ALU.add).then_inc(S["rt_ready"], 1)
                pool.wait_ge(S["rt_ready"], 3 * half + 3)
                inv_root(r2[:, a:b], rt[:, a:b], 4, "r2_ready")
                for t in range(a, b):
                    pool.wait_ge(S["n1_ready"], t + 1)
                    pool.tensor_tensor(hres[:, t, :], hres[:, t, :], x1[:, t, :], ALU.add).then_inc(S["hres_ready"], 1)

            pool.wait_ge(S["r2_ready"], 2)

            def delta_norm(i, u, first):
                if not first:
                    pool.wait_ge(S["n2_mm"], upto(i, u) - 2)
                t = 2 * i + u
                pool.tensor_tensor(dl[u].n2, tile_of(x1, t), rep(r2[:, ds(t, 1)], [P, D]),
                                   ALU.mult).then_inc(S["n2_ready"], 1)

            def delta_pool(i, first):
                for u in range(2):
                    delta_norm(i, u, first)
                for u in range(2):
                    pool.wait_ge(S["ssq"], third(i, u, 3))
                    inv_root(rn[u], ssq[u], 8, "rn_ready")
                for u in range(2):
                    pool.wait_ge(S["orv_ready"], upto(i, u))
                    inv_root(orms[u], orv[u], 4, "orms_ready")
                for u in range(2):
                    pool.wait_ge(S["h2stat"], third(i, u, 3))
                    inv_root(r3[u], ve3[u], 1, "r3_ready")
            delta_pool(0, True)
            with pool.Fori(1, PAIRS) as i:
                delta_pool(i, False)

            pool.wait_ge(S["n3_stored"], NT)
            pool.wait_ge(S["bias_in"], 16 * 9)
            def attn_pool(i, first):
                for u in range(2):
                    t = 2 * i + u
                    if not first:
                        pool.wait_ge(S["xa_ready"], upto(i, u) - 2)
                    pool.tensor_copy(at[u].n3, tile_of(x1, t)).then_inc(S["n3_ready"], 1)
                    pool.tensor_tensor(at[u].n3b, tile_of(x1, t), bo, ALU.add).then_inc(S["n3b_ready"], 1)
                for u in range(2):
                    pool.wait_ge(S["qkb_ready"], upto(i, u))
                    pool.tensor_tensor(eights(at[u].ta), eights(at[u].qkb),
                                       rep(con[:, C_COS:C_COS + 8][:, None, :], [P, 64, 8]),
                                       ALU.mult).then_inc(S["ropea_ready"], 1)
                for u in range(2):
                    pool.wait_ge(S["xastat"], third(i, u, 3))
                    inv_root(r4[u], ve4[u], 1, "r4_ready")
                for u in range(2):
                    pool.wait_ge(S["x1T_mm"], upto(i, u))
                    pool.tensor_tensor(at[u].x1n, at[u].x1n, g1, ALU.mult).then_inc(S["x1g_ready"], 1)
            attn_pool(0, True)
            with pool.Fori(1, PAIRS) as i:
                attn_pool(i, False)

            pool.wait_ge(S["zero_in"], 16)
            pool.wait_ge(S["x1_ready"], NT)
            pool.wait_ge(S["route"], ROUTED)
            for t in range(NT):
                for k in range(2):
                    pool.indirect_dma_start(
                        out=xs_dram, out_offset=bass.IndirectOffsetOnAxis(posi[:, k * NT + t:k * NT + t + 1], 0),
                        in_=x1[:, t, :], in_offset=None).then_inc(S["scattered"], 16)
            for t in range(NT):
                pool.tensor_tensor(hres[:, t, :], hres[:, t, :], be2, ALU.add).then_inc(S["hb_ready"], 1)

            pool.wait_ge(S["y_out0"], 16 * (SLOT_TILES // 2 + 1))
            pool.wait_ge(S["y_out1"], 16 * (SLOT_TILES // 2))
            for t in range(NT):
                for k in range(2):
                    pool.indirect_dma_start(
                        out=yg[:, k, t, :], out_offset=None, in_=ys_dram,
                        in_offset=bass.IndirectOffsetOnAxis(posi[:, k * NT + t:k * NT + t + 1], 0)
                    ).then_inc(gathered[t], 16)
            for t in range(NT):
                pool.wait_ge(S["tail"], TAIL1 * t + 5)
                inv_root(r5[:, t:t + 1], ve5[:, t:t + 1], 1, "r5_ready")

        @block.scalar
        def _(act):
            r = 0
            for name, n in (("L0_attn_ln_w", 2), ("L0_attn_ln_b", 2), ("L0_attn_o_norm_w", 1), ("L0_ffn_bv", 2),
                            ("L0_ffn_g1", 2), ("L0_ffn_be1", 2)):
                act.dma_start(rows[r:r + n, :], A[name].rearrange("(c p) -> c p", p=P)).then_inc(S["rows_in"], 16)
                r += n
            act.dma_start(rows[r:r + E * FC, :],
                          A["L0_ffn_b1"].rearrange("e (c p) -> (e c) p", p=P)).then_inc(S["rows_in"], 16)
            for dst, name in ((tokb, "L0_tok_b"), (bqk[:, 0:D], "L0_ffn_bq"), (bqk[:, D:2 * D], "L0_ffn_bk"),
                              (bo, "L0_ffn_bo"), (g1, "L0_ffn_g1"), (be1, "L0_ffn_be1"), (g2, "L0_ffn_g2"),
                              (be2, "L0_ffn_be2"), (bg, "L0_ffn_bg")):
                act.dma_start(dst, A[name].partition_broadcast(P)).then_inc(S["bias_in"], 16)

            for half in range(2):
                act.wait_ge(S[f"x_in{half}"], 48)
                x_split(act.copy, half, 1).then_inc(S[f"x_split{half}"], 1)
                for q in range(1, KC, 2):
                    act.wait_ge(S["xT_mm"], KC * half + q + 1)
                    act.copy(xT_out(half, q), xT_in(half, q)).then_inc(S["xT_ready"], 1)
            act.wait_ge(S["rows_mm"], 1)
            act.copy(cols[:, 0:75], bank(0, 256, 331)).then_inc(S["cols_ready"], 1)
            act.wait_ge(S["cols_ready"], 1)

            def delta_act(i):
                for u in range(2):
                    b, k = dl[u], 4 * u
                    act.wait_ge(S["n2_mm"], upto(i, u))
                    for c in range(DC):
                        last = act.activation(b.n2T[:, c * P:(c + 1) * P], bank(k, c * P, (c + 1) * P), ACT.Identity,
                                              bias=cols[:, LNB + c:LNB + c + 1], scale=cols[:, LNW + c:LNW + c + 1])
                    last.then_inc(S["n2T_ready"], 1)
                for u in range(2):
                    b, k = dl[u], 4 * u
                    act.wait_ge(S["beta_mm"], upto(i, u))
                    act.activation(th[u], bank(k, 256, 260), ACT.Tanh, scale=0.5).then_inc(S["beta_act"], 1)
                    act.wait_ge(S["qk_mm"], upto(i, u))
                    act.activation(b.qk, bank(k + 1), ACT.Silu).then_inc(S["qk_act"], 1)
                    act.wait_ge(S["v_mm"], upto(i, u))
                    act.activation(b.y[1], bank(k + 2), ACT.Silu).then_inc(S["v_act"], 1)
                for u in range(2):
                    b, k = dl[u], 4 * u
                    act.wait_ge(S["kT_mm"], upto(i, u))
                    act.copy(b.kT, bank(k + 3, 0, 256)).then_inc(S["kT_ready"], 1)
                    act.wait_ge(S["kqT_mm"], upto(i, u))
                    act.copy(b.kqT, bank(k)).then_inc(S["kqT_ready"], 1)
                for u in range(2):
                    b, k = dl[u], 4 * u
                    act.wait_ge(S["m2_mm"], upto(i, u))
                    act.copy(b.m2, bank(k + 3)).then_inc(S["m2_ready"], 1)
                    act.wait_ge(S["n2p_mm"], upto(i, u))
                    act.copy(b.n2p, bank(k + 1)).then_inc(S["n2p_ready"], 1)
                for u in range(2):
                    b, k = dl[u], 4 * u
                    act.wait_ge(S["m4_mm"], upto(i, u))
                    act.copy(b.m, bank(k + 3)).then_inc(S["m4_ready"], 1)
                    act.wait_ge(S["n4_mm"], upto(i, u))
                    act.copy(b.n4, bank(k + 1)).then_inc(S["n4_ready"], 1)
                for u in range(2):
                    b, k = dl[u], 4 * u
                    act.wait_ge(S["n8_mm"], upto(i, u))
                    act.copy(b.m2, bank(k + 3)).then_inc(S["n8_ready"], 1)
                for u in range(2):
                    b, k = dl[u], 4 * u
                    act.wait_ge(S["o_mm"], upto(i, u))
                    for h in range(H):
                        last = act.activation(b.y[1][:, h * DV:(h + 1) * DV], bank(k + 1, h * DV, (h + 1) * DV),
                                              ACT.Square, accum_out=oss[u][:, h:h + 1])
                    last.then_inc(S["oss_ready"], 1)
                for u in range(2):
                    b, k = dl[u], 4 * u
                    act.wait_ge(S["oT_mm"], upto(i, u))
                    act.activation(b.n4, bank(k + 3), ACT.Copy, scale=cols[:, ONW:ONW + 1]).then_inc(S["oT_ready"], 1)
            with act.Fori(0, PAIRS) as i:
                delta_act(i)

            act.wait_ge(S["h2_ready"], NT)

            def attn_act(i):
                for u in range(2):
                    b, k = at[u], 4 * u
                    act.wait_ge(S["n3_mm"], upto(i, u))
                    act.copy(b.n3T, bank(k, 0, 256)).then_inc(S["n3T_ready"], 1)
                for u in range(2):
                    b, k = at[u], 4 * u
                    act.wait_ge(S["av_mm"], upto(i, u))
                    act.copy(b.vs, bank(k, 256, 512)).then_inc(S["vs_ready"], 1)
                for u in range(2):
                    b, k = at[u], 4 * u
                    act.wait_ge(S["qkT_mm"], upto(i, u))
                    act.copy(b.qT, bank(k + 1, 0, 256)).then_inc(S["qT_ready"], 1)
                for u in range(2):
                    b, k = at[u], 4 * u
                    act.wait_ge(S["centre"], third(i, u, 3))
                    act.activation(b.sm, b.sm, ACT.Exp, scale=MD ** -0.5).then_inc(S["exp_ready"], 1)
                for u in range(2):
                    b, k = at[u], 4 * u
                    act.wait_ge(S["pT_mm"], upto(i, u))
                    act.copy(b.pT, bank(k + 1)).then_inc(S["pT_ready"], 1)
                for u in range(2):
                    b, k = at[u], 4 * u
                    act.wait_ge(S["pv_mm"], upto(i, u))
                    for c in range(DC):
                        last = act.activation(b.aoT[:, c * P:(c + 1) * P], bank(k + 2, c * P, (c + 1) * P), ACT.Identity,
                                              bias=cols[:, BV + c:BV + c + 1])
                    last.then_inc(S["aoT_ready"], 1)
                for u in range(2):
                    b, k = at[u], 4 * u
                    act.wait_ge(S["x1T_mm"], upto(i, u))
                    for c in range(DC):
                        last = act.activation(b.x1T[:, c * P:(c + 1) * P], bank(k + 2, 256 + c * P, 256 + (c + 1) * P),
                                              ACT.Identity, bias=cols[:, BE1 + c:BE1 + c + 1],
                                              scale=cols[:, G1 + c:G1 + c + 1])
                    last.then_inc(S["x1T_ready"], 1)
            with act.Fori(0, PAIRS) as i:
                attn_act(i)

            act.wait_ge(S["route"], 2)
            act.activation(lg[:, :], lg[:, :], ACT.Exp).then_inc(S["logit_exp"], 1)
            act.wait_ge(S["combT_mm"], 1)
            act.copy(combT, ps[0:E, 1:3, :].rearrange("p a b -> p (a b)")).then_inc(S["combT_ready"], 1)

            act.wait_ge(S["route"], ROUTED)

            def moe_act(t, u):
                e = act.value_load(tilee[0:1, ds(t, 1)], min_val=0, max_val=E - 1)
                act.wait_ge(S["hT_mm"], t + 1)
                for f in range(FC):
                    last = act.activation(gT[u][:, f * P:(f + 1) * P], bank(4 + f // 4, f % 4 * P, f % 4 * P + P),
                                          ACT.Gelu, bias=cols[:, ds(e * FC + (B1 + f), 1)])
                last.then_inc(S["act_ready"], 1)
            with act.Fori(0, SLOT_TILES // 2) as i:
                for u in range(2):
                    moe_act(2 * i + u, u)
            moe_act(SLOT_TILES - 1, 0)

        @block.tensor
        def _(pe):
            pe.wait_ge(S["const_in"], 16)
            pe.wait_ge(S["tokw_in"], 16)
            for q in range(KC):
                for c in range(DC):
                    n = q * DC + c
                    mm = pe.transpose(bank(n // 4, n % 4 * P, n % 4 * P + P), tokw[:, c * KP + q * P:c * KP + (q + 1) * P],
                                      ident)
                if n % 4 == 3:
                    mm.then_inc(S["wT_mm"], 1)
            for half in range(2):
                pe.wait_ge(S[f"x_split{half}"], 3)
                for q in range(KC):
                    n = KC * half + q
                    if n >= 3:
                        pe.wait_ge(S["xT_ready" if (n - 3) % 2 else "xT_even_ready"], (n - 3) // 2 + 1)
                    for w in range(4):
                        mm = pe.transpose(bank(4 + n % 3, w * P, w * P + P),
                                          x_tok[half][:, w * KP + q * P:w * KP + (q + 1) * P], ident)
                    mm.then_inc(S["xT_mm"], 1)
                pe.wait_ge(S["xT_ready"], 3 * half + 3)
                pe.wait_ge(S["xT_even_ready"], 3 * half + 3)
                pe.wait_ge(S["wT_ready"], 3)
                for tt in range(4):
                    t = 4 * half + tt
                    if t >= 4:
                        pe.wait_ge(S["h_ready"], t - 3)
                    for q in range(KC):
                        mm = pe.matmul(bank(t % 4, 0, D), xT[half][:, q * 512 + tt * P:q * 512 + (tt + 1) * P],
                                       tokwT[:, q * D:(q + 1) * D], start=(q == 0), stop=(q == KC - 1))
                    mm.then_inc(S["emb_mm"], 1)
            pe.wait_ge(S["rows_in"], 16 * 7)
            pe.wait_ge(S["h_ready"], NT)
            pe.transpose(bank(0, 256, 331), rows[0:75, :], ident[0:75, 0:75]).then_inc(S["rows_mm"], 1)
            pe.wait_ge(S["cols_ready"], 1)
            pe.wait_ge(S["attnw_in"], 16 * 5)

            def delta_pe(i, first):
                for u in range(2):
                    b, k = dl[u], 4 * u
                    if not first:
                        pe.wait_ge(S["h2_ready"], upto(i, u) - 2)
                    pe.wait_ge(S["n2_ready"], upto(i, u))
                    for c in range(DC):
                        mm = pe.transpose(bank(k, c * P, (c + 1) * P), b.n2[:, c * P:(c + 1) * P], ident)
                    mm.then_inc(S["n2_mm"], 1)
                for u in range(2):
                    b, k = dl[u], 4 * u
                    pe.wait_ge(S["n2T_ready"], upto(i, u))
                    for dst, w, sem in ((bank(k, 256, 260), wb_a, "beta_mm"), (bank(k + 1), wqk_a, "qk_mm"),
                                        (bank(k + 2), wv_a, "v_mm")):
                        for c in range(DC):
                            mm = pe.matmul(dst, b.n2T[:, c * P:(c + 1) * P], w[:, c, :], start=(c == 0), stop=(c == DC - 1))
                        mm.then_inc(S[sem], 1)
                for u in range(2):
                    b, k = dl[u], 4 * u
                    pe.wait_ge(S["knorm_ready"], upto(i, u))
                    for p in range(2):
                        mm = pe.transpose(bank(k + 3, p * P, (p + 1) * P), b.qk[:, 256 + p * P:256 + (p + 1) * P], ident)
                    mm.then_inc(S["kT_mm"], 1)
                    pe.wait_ge(S["beta_act"], upto(i, u))
                    pe.wait_ge(S["kb_ready"], upto(i, u))
                    for p in range(2):
                        pe.transpose(bank(k, p * 256, p * 256 + P), b.kb[:, p * P:(p + 1) * P], ident)
                        mm = pe.transpose(bank(k, p * 256 + P, p * 256 + 256), b.qk[:, p * P:(p + 1) * P], ident)
                    mm.then_inc(S["kqT_mm"], 1)
                for u in range(2):
                    b, k = dl[u], 4 * u
                    pe.wait_ge(S["kT_ready"], upto(i, u))
                    pe.wait_ge(S["kqT_ready"], upto(i, u))
                    pe.wait_ge(S["v_act"], upto(i, u))
                    for hp in range(2):
                        for par in range(2):
                            r = slice(64 * par, 64 * par + 64)
                            mm = pe.matmul(bank(k + 1 + par, hp * 256, hp * 256 + 256), b.kT[r, hp * P:(hp + 1) * P],
                                           b.kqT[r, hp * 256:hp * 256 + 256], start=True, stop=True)
                    mm.then_inc(S["np_mm"], 1)
                    for hp in range(2):
                        for par in range(2):
                            r = slice(64 * par, 64 * par + 64)
                            mm = pe.matmul(bank(k + 3 * par, hp * P, (hp + 1) * P), b.kqT[r, hp * 256:hp * 256 + P],
                                           b.kT[r, hp * P:(hp + 1) * P], start=True, stop=True)
                    mm.then_inc(S["m_mm"], 1)

                def heads(dst, lhsT, rhs, sem):
                    for h in range(H):
                        mm = pe.matmul(dst[:, h * P:(h + 1) * P], lhsT(h), rhs(h), start=True, stop=True)
                    mm.then_inc(S[sem], 1)

                def by_head(buf):
                    return lambda h: buf[:, h * P:(h + 1) * P]

                def by_parity(buf, width, off=0):
                    return lambda h: buf[:, (h % 2) * 2 * width + (h // 2) * width + off:
                                         (h % 2) * 2 * width + (h // 2) * width + off + P]
                for u in range(2):
                    b, k = dl[u], 4 * u
                    n, m_ = by_parity(b.np, 256), by_parity(b.m, P)
                    pe.wait_ge(S["np_ready"], upto(i, u))
                    pe.wait_ge(S["m_ready"], upto(i, u))
                    heads(bank(k + 3), n, m_, "m2_mm")
                    heads(bank(k + 1), m_, n, "n2p_mm")
                    pe.wait_ge(S["y0_ready"], upto(i, u))
                    heads(bank(k), n, by_head(b.y[0]), "y1_mm")
                for u in range(2):
                    b, k = dl[u], 4 * u
                    m2, n2 = by_head(b.m2), by_head(b.n2p)
                    pe.wait_ge(S["m2_ready"], upto(i, u))
                    pe.wait_ge(S["n2p_ready"], upto(i, u))
                    heads(bank(k + 3), n2, m2, "m4_mm")
                    heads(bank(k + 1), m2, n2, "n4_mm")
                    pe.wait_ge(S["y1_ready"], upto(i, u))
                    heads(bank(k + 2), n2, by_head(b.y[1]), "y2_mm")
                for u in range(2):
                    b, k = dl[u], 4 * u
                    m4, n4 = by_head(b.m), by_head(b.n4)
                    pe.wait_ge(S["m4_ready"], upto(i, u))
                    pe.wait_ge(S["n4_ready"], upto(i, u))
                    heads(bank(k + 3), m4, n4, "n8_mm")
                    pe.wait_ge(S["y2_ready"], upto(i, u))
                    heads(bank(k), n4, by_head(b.y[0]), "y3_mm")
                for u in range(2):
                    b, k = dl[u], 4 * u
                    pe.wait_ge(S["n8_ready"], upto(i, u))
                    pe.wait_ge(S["y3_ready"], upto(i, u))
                    heads(bank(k + 2), by_head(b.m2), by_head(b.y[1]), "y4_mm")
                for u in range(2):
                    b, k = dl[u], 4 * u
                    pe.wait_ge(S["y4_ready"], upto(i, u))
                    heads(bank(k + 1), by_parity(b.np, 256, P), by_head(b.y[0]), "o_mm")
                for u in range(2):
                    b, k = dl[u], 4 * u
                    pe.wait_ge(S["on_ready"], upto(i, u))
                    for h in range(H):
                        mm = pe.transpose(bank(k + 3, h * P, (h + 1) * P), b.n2p[:, h * P:(h + 1) * P], ident)
                    mm.then_inc(S["oT_mm"], 1)
                for u in range(2):
                    b, k = dl[u], 4 * u
                    pe.wait_ge(S["oT_ready"], upto(i, u))
                    for h in range(H):
                        mm = pe.matmul(bank(k, 0, D), b.n4[:, h * P:(h + 1) * P], wo_a[:, h, :],
                                       start=(h == 0), stop=(h == H - 1))
                    mm.then_inc(S["wo_mm"], 1)
            delta_pe(0, True)
            with pe.Fori(1, PAIRS) as i:
                delta_pe(i, False)

            pe.wait_ge(S["h2_ready"], NT)
            pe.wait_ge(S["ffnw_in"], 16 * 6)

            def attn_pe(i, first):
                for u in range(2):
                    b, k = at[u], 4 * u
                    if not first:
                        pe.wait_ge(S["logit_ready"], upto(i, u) - 2)
                    pe.wait_ge(S["n3_ready"], upto(i, u))
                    for c in range(DC):
                        mm = pe.transpose(bank(k, c * P, (c + 1) * P), b.n3[:, c * P:(c + 1) * P], ident)
                    mm.then_inc(S["n3_mm"], 1)
                for u in range(2):
                    b, k = at[u], 4 * u
                    pe.wait_ge(S["n3T_ready"], upto(i, u))
                    for dst, w, sem in ((bank(k + 1), wqk_f, "aqk_mm"), (bank(k, 256, 512), wv_f, "av_mm")):
                        for c in range(DC):
                            mm = pe.matmul(dst, b.n3T[:, c * P:(c + 1) * P], w[:, c, :], start=(c == 0), stop=(c == DC - 1))
                        mm.then_inc(S[sem], 1)
                for u in range(2):
                    b, k = at[u], 4 * u
                    pe.wait_ge(S["vs_ready"], upto(i, u))
                    for j in range(4):
                        mm = pe.matmul(bank(k + 2 + j // 2, j % 2 * D, j % 2 * D + D),
                                       con[:, C_REP + j * P:C_REP + (j + 1) * P], b.vs, start=True, stop=True)
                    mm.then_inc(S["vrep_mm"], 1)
                for u in range(2):
                    b, k = at[u], 4 * u
                    pe.wait_ge(S["rope_ready"], upto(i, u))
                    for c in range(4):
                        mm = pe.transpose(bank(k + 1, c * P, (c + 1) * P), b.sm[:, c * P:(c + 1) * P], ident)
                    mm.then_inc(S["qkT_mm"], 1)
                for u in range(2):
                    b, k = at[u], 4 * u
                    pe.wait_ge(S["qT_ready"], upto(i, u))
                    pe.wait_ge(S["kexp_ready"], upto(i, u))
                    for g in range(2):
                        keys = b.kexp[:, g * 1024:(g + 1) * 1024].rearrange("p (h k) -> p h k", h=8)
                        for j in range(4):
                            mm = pe.matmul(ps[32 * j:32 * j + 32, k, g * 256:g * 256 + 256],
                                           b.qT[:, g * P + 32 * j:g * P + 32 * j + 32],
                                           keys[:, :, 32 * j:32 * j + 32], start=True, stop=True)
                    mm.then_inc(S["score_mm"], 1)
                for u in range(2):
                    b, k = at[u], 4 * u
                    pe.wait_ge(S["prob"], third(i, u, 3))
                    for c in range(4):
                        mm = pe.transpose(bank(k + 1, c * P, (c + 1) * P), b.sm[:, c * P:(c + 1) * P], ident)
                    mm.then_inc(S["pT_mm"], 1)
                for u in range(2):
                    b, k = at[u], 4 * u
                    pe.wait_ge(S["pT_ready"], upto(i, u))
                    pe.wait_ge(S["vbd_ready"], upto(i, u))
                    for hg in range(4):
                        for j in range(4):
                            col = hg // 2 * P + 32 * j
                            mm = pe.matmul(ps[64 * (hg % 2):64 * (hg % 2) + 64, k + 2, col:col + 32],
                                           b.vbd[:, j * 256 + hg * 64:j * 256 + hg * 64 + 64],
                                           b.pT[:, hg * P + 32 * j:hg * P + 32 * j + 32], start=True, stop=True)
                    mm.then_inc(S["pv_mm"], 1)
                for u in range(2):
                    b, k = at[u], 4 * u
                    pe.wait_ge(S["aoT_ready"], upto(i, u))
                    for c in range(DC):
                        mm = pe.matmul(bank(k + 3, 0, D), b.aoT[:, c * P:(c + 1) * P], wo_f[:, c, :],
                                       start=(c == 0), stop=(c == DC - 1))
                    mm.then_inc(S["awo_mm"], 1)
                for u in range(2):
                    b, k = at[u], 4 * u
                    pe.wait_ge(S["x1n_ready"], upto(i, u))
                    for c in range(DC):
                        mm = pe.transpose(bank(k + 2, 256 + c * P, 256 + (c + 1) * P), b.x1n[:, c * P:(c + 1) * P], ident)
                    mm.then_inc(S["x1T_mm"], 1)
                for u in range(2):
                    b, k = at[u], 4 * u
                    pe.wait_ge(S["x1T_ready"], upto(i, u))
                    for c in range(DC):
                        mm = pe.matmul(bank(k + 3, 256, 256 + E), b.x1T[:, c * P:(c + 1) * P], wg_f[:, c, :],
                                       start=(c == 0), stop=(c == DC - 1))
                    mm.then_inc(S["gate_mm"], 1)
            attn_pe(0, True)
            with pe.Fori(1, PAIRS) as i:
                attn_pe(i, False)

            pe.wait_ge(S["logit_ready"], NT)
            pe.wait_ge(S["route"], CHOSEN)
            pe.matmul(bank(0, 0, 72), con[:, C_ONE:C_ONE + P], cum, start=True, stop=False, skip_group_check=True)
            pe.matmul(bank(0, 0, 64), con[:, C_UP:C_UP + P], chosen, start=False, stop=True,
                      skip_group_check=True).then_inc(S["count_mm"], 1)
            for t in range(NT):
                mm = pe.transpose(ps[0:E, 1 + t // 4, t % 4 * P:t % 4 * P + P], comb[:, t * E:(t + 1) * E], ident)
            mm.then_inc(S["combT_mm"], 1)
            pe.wait_ge(S["combT_ready"], 1)
            for t in range(NT):
                mm = pe.matmul(bank(4 + t // 2, t % 2 * D, t % 2 * D + D), combT[:, t * P:(t + 1) * P], b2_f[:, :],
                               start=True, stop=True)
            mm.then_inc(S["b2_mm"], 1)

            pe.wait_ge(S["route"], ROUTED)
            pe.wait_ge(S["x1b_ready"], NT)
            pe.wait_ge(S["w1_in"], 16 * E)
            pe.wait_ge(S["w2lo_in"], 16 * (E // 2))
            pe.wait_ge(S["w2hi_in"], 16 * (E // 2))

            def turn_rows(t, u, wait_in, first):
                pe.wait_ge(S[f"slot_in{u}"], wait_in)
                if not first:
                    pe.wait_ge(S["xgT_ready"], t)
                for c in range(DC):
                    mm = pe.transpose(bank(7, c * P, (c + 1) * P), xg[u][:, c * P:(c + 1) * P], ident)
                mm.then_inc(S["xgT_mm"], 1)

            def up(t, u, e, first):
                pe.wait_ge(S["xgT_ready"], t + 1)
                if not first:
                    pe.wait_ge(S["up_ready"], t - 1)
                for n in range(2):
                    for c in range(DC):
                        mm = pe.matmul(bank(2 * u + n), xgT[u][:, c * P:(c + 1) * P],
                                       w1[:, ds(e * (DC * FF) + (c * FF + n * 512), 512)], start=(c == 0), stop=(c == DC - 1))
                mm.then_inc(S["up_mm"], 1)

            def turn_hidden(t, u, first):
                pe.wait_ge(S["up_ready"], t + 1)
                if not first:
                    pe.wait_ge(S["act_ready"], t)
                for f in range(FC):
                    mm = pe.transpose(bank(4 + f // 4, f % 4 * P, f % 4 * P + P), hs[u][:, f * P:(f + 1) * P], ident)
                mm.then_inc(S["hT_mm"], 1)

            def down(t, u, e, first):
                pe.wait_ge(S["act_ready"], t + 1)
                if not first:
                    pe.wait_ge(S["ys_ready"], t)
                for f in range(FC):
                    mm = pe.matmul(bank(6, 0, D), gT[u][:, f * P:(f + 1) * P],
                                   w2[:, ds(e * (FC * D) + f * D, D)], start=(f == 0), stop=(f == FC - 1))
                mm.then_inc(S["down_mm"], 1)

            def expert(t):
                return pe.value_load(tilee[0:1, ds(t, 1)], min_val=0, max_val=E - 1)

            turn_rows(0, 0, 16, True)
            up(0, 0, expert(0), True)
            turn_rows(1, 1, 16, False)
            turn_hidden(0, 0, True)
            up(1, 1, expert(1), True)
            turn_rows(2, 0, 32, False)
            down(0, 0, expert(0), True)
            turn_hidden(1, 1, False)
            with pe.Fori(1, SLOT_TILES // 2) as i:
                up(2 * i, 0, expert(2 * i), False)
                turn_rows(2 * i + 1, 1, 16 * i + 16, False)
                down(2 * i - 1, 1, expert(2 * i - 1), False)
                turn_hidden(2 * i, 0, False)
                up(2 * i + 1, 1, expert(2 * i + 1), False)
                turn_rows(2 * i + 2, 0, 16 * i + 32, False)
                down(2 * i, 0, expert(2 * i), False)
                turn_hidden(2 * i + 1, 1, False)
            t = SLOT_TILES - 1
            up(t, 0, expert(t), False)
            down(t - 1, 1, expert(t - 1), False)
            turn_hidden(t, 0, False)
            down(t, 0, expert(t), False)

        @block.vector
        def _(dve):
            dve.wait_ge(S["bias_in"], 16 * 9)
            for n in range(3):
                dve.wait_ge(S["wT_mm"], n + 1)
                dve.tensor_copy(tokwT[:, n * 512:(n + 1) * 512], bank(n)).then_inc(S["wT_ready"], 1)

            def stats(src, raw, mv, ve, waits):
                (a, na), (b, nb), (c, nc_) = waits
                dve.bn_stats(raw, src).then_inc(S[a], 1)
                dve.wait_ge(S[a], na)
                dve.bn_aggr(mv, raw).then_inc(S[b], 1)
                if ve is not None:
                    dve.wait_ge(S[b], nb)
                    dve.tensor_scalar(ve, mv[:, 1:2], EPS, None, ALU.add).then_inc(S[c], 1)

            def patches(half):
                dve.wait_ge(S[f"x_in{half}"], 48)
                x_split(dve.tensor_copy, half, 0).then_inc(S[f"x_split{half}"], 1)
                for q in range(0, KC, 2):
                    dve.wait_ge(S["xT_mm"], KC * half + q + 1)
                    if half and q == 0:
                        dve.wait_ge(S["x_split0"], 3)
                    dve.tensor_copy(xT_out(half, q), xT_in(half, q)).then_inc(S["xT_even_ready"], 1)

            def embed(half):
                for tt in range(4):
                    t = 4 * half + tt
                    dve.wait_ge(S["emb_mm"], t + 1)
                    dve.tensor_tensor(hres[:, t, :], bank(t % 4, 0, D), tokb, ALU.add).then_inc(S["h_ready"], 1)
                    dve.wait_ge(S["h_ready"], t + 1)
                    stats(hres[:, t, :], bst[t], mv1[:, 2 * t:2 * t + 2], None,
                          (("hstat_a", t + 1), ("hstat_b", t + 1), ("", 0)))
                a, b = 4 * half, 4 * half + 4
                dve.wait_ge(S["hstat_b"], b)
                dve.tensor_scalar(ve1[:, a:b], mv1.rearrange("p (t k) -> p t k", k=2)[:, a:b, 1], EPS, None,
                                  ALU.add).then_inc(S["hstat_ready"], 1)

            def first_norm(half):
                dve.wait_ge(S["r1_ready"], half + 1)
                for t in range(4 * half, 4 * half + 4):
                    dve.tensor_scalar(x1[:, t, :], hres[:, t, :], mv1[:, 2 * t:2 * t + 1], r1[:, t:t + 1],
                                      ALU.subtract, ALU.mult).then_inc(S["n1_ready"], 1)
            patches(0)
            dve.wait_ge(S["x_in1"], 48)
            x_split(dve.tensor_copy, 1, 0).then_inc(S["x_split1"], 1)
            embed(0)
            for q in range(0, KC, 2):
                dve.wait_ge(S["xT_mm"], KC + q + 1)
                dve.wait_ge(S["x_split0"], 3)
                dve.tensor_copy(xT_out(1, q), xT_in(1, q)).then_inc(S["xT_even_ready"], 1)
            first_norm(0)
            embed(1)
            first_norm(1)

            dve.wait_ge(S["hres_ready"], NT)

            def delta_dve(i):
                for u in range(2):
                    b = dl[u]
                    dve.wait_ge(S["beta_act"], upto(i, u))
                    dve.tensor_scalar(beta[u], th[u], 0.5, 0.5, ALU.mult, ALU.add).then_inc(S["beta_ready"], 1)
                    dve.wait_ge(S["qk_act"], upto(i, u))
                    dve.tensor_tensor(b.sq, b.qk, b.qk, ALU.mult).then_inc(S["ssq"], 1)
                    dve.wait_ge(S["ssq"], third(i, u, 1))
                    dve.tensor_reduce(rn[u], b.sq.rearrange("p (h d) -> p h d", h=8), AX, ALU.add).then_inc(S["ssq"], 1)
                    dve.wait_ge(S["ssq"], third(i, u, 2))
                    dve.tensor_scalar(ssq[u], rn[u], 1e-6, None, ALU.add).then_inc(S["ssq"], 1)
                for u in range(2):
                    b = dl[u]
                    dve.wait_ge(S["v_act"], upto(i, u))
                    dve.wait_ge(S["beta_ready"], upto(i, u))
                    dve.tensor_tensor(heads4(b.y[0]), heads4(b.y[1]), rep(beta[u][:, :, None], [P, H, DV]),
                                      ALU.mult).then_inc(S["y0_ready"], 1)
                for u in range(2):
                    b = dl[u]
                    q, k = (b.qk[:, c * 256:(c + 1) * 256].rearrange("p (h d) -> p h d", h=H) for c in range(2))
                    dve.wait_ge(S["rn_ready"], upto(i, u))
                    dve.tensor_tensor(k, k, rep(rn[u][:, H:2 * H][:, :, None], [P, H, DK]),
                                      ALU.mult).then_inc(S["qnorm_ready"], 1)
                    dve.scalar_tensor_tensor(q, q, DK ** -0.5, rep(rn[u][:, 0:H][:, :, None], [P, H, DK]),
                                             ALU.mult, ALU.mult).then_inc(S["knorm_ready"], 1)
                    dve.wait_ge(S["qnorm_ready"], upto(i, u))
                    dve.tensor_tensor(b.kb.rearrange("p (h d) -> p h d", h=H), k, rep(beta[u][:, :, None], [P, H, DK]),
                                      ALU.mult).then_inc(S["kb_ready"], 1)
                for u in range(2):
                    b, k = dl[u], 4 * u
                    dve.wait_ge(S["np_mm"], upto(i, u))
                    dve.tensor_tensor(b.np.rearrange("p (g c) -> p g c", g=4),
                                      ps[:, k + 1:k + 3, :].rearrange("p a (g c) -> p (a g) c", g=2),
                                      rep(con[:, C_NP:C_NP + 256][:, None, :], [P, 4, 256]),
                                      ALU.mult).then_inc(S["np_ready"], 1)
                    dve.wait_ge(S["m_mm"], upto(i, u))
                    dve.tensor_tensor(b.m.rearrange("p (a g c) -> p a g c", a=2, g=2),
                                      ps[:, k:k + 4:3, 0:256].rearrange("p a (g c) -> p a g c", g=2),
                                      rep(con[:, C_M:C_M + P][:, None, None, :], [P, 2, 2, P]),
                                      ALU.mult).then_inc(S["m_ready"], 1)
                for n, src, dst, off, op in (("y1", 0, 1, 0, ALU.subtract), ("y2", 1, 0, 2, ALU.add),
                                             ("y3", 0, 1, 0, ALU.add), ("y4", 1, 0, 2, ALU.add)):
                    for u in range(2):
                        b, k = dl[u], 4 * u
                        dve.wait_ge(S[n + "_mm"], upto(i, u))
                        dve.tensor_tensor(b.y[dst], b.y[src], bank(k + off), op).then_inc(S[n + "_ready"], 1)
                for u in range(2):
                    dve.wait_ge(S["oss_ready"], upto(i, u))
                    dve.tensor_scalar(orv[u], oss[u], 1.0 / DV, EPS, ALU.mult, ALU.add).then_inc(S["orv_ready"], 1)
                for u in range(2):
                    b, k = dl[u], 4 * u
                    dve.wait_ge(S["orms_ready"], upto(i, u))
                    dve.tensor_tensor(heads4(b.n2p), heads4(bank(k + 1)), rep(orms[u][:, :, None], [P, H, DV]),
                                      ALU.mult).then_inc(S["on_ready"], 1)
                for u in range(2):
                    t, k = 2 * i + u, 4 * u
                    dve.wait_ge(S["wo_mm"], upto(i, u))
                    dve.tensor_tensor(dl[u].h2, tile_of(hres, t), bank(k, 0, D), ALU.add).then_inc(S["h2s_ready"], 1)
                    dve.wait_ge(S["h2s_ready"], upto(i, u))
                    dve.bn_stats(bst[u], dl[u].h2).then_inc(S["h2stat"], 1)
                    dve.wait_ge(S["h2stat"], third(i, u, 1))
                    dve.tensor_tensor(tile_of(hres, t), tile_of(hres, t), bank(k, 0, D), ALU.add).then_inc(S["h2_ready"], 1)
                    dve.bn_aggr(mv3[u], bst[u]).then_inc(S["h2stat"], 1)
                    dve.wait_ge(S["h2stat"], third(i, u, 2))
                    dve.tensor_scalar(ve3[u], mv3[u][:, 1:2], EPS, None, ALU.add).then_inc(S["h2stat"], 1)
                for u in range(2):
                    dve.wait_ge(S["r3_ready"], upto(i, u))
                    dve.tensor_scalar(tile_of(x1, 2 * i + u), dl[u].h2, mv3[u][:, 0:1], r3[u],
                                      ALU.subtract, ALU.mult).then_inc(S["n3_stored"], 1)
            with dve.Fori(0, PAIRS) as i:
                delta_dve(i)

            dve.wait_ge(S["n3_stored"], NT)

            def attn_dve(i):
                for u in range(2):
                    b, k = at[u], 4 * u
                    dve.wait_ge(S["aqk_mm"], upto(i, u))
                    dve.tensor_tensor(b.qkb, bank(k + 1), bqk, ALU.add).then_inc(S["qkb_ready"], 1)
                for u in range(2):
                    b, k = at[u], 4 * u
                    dve.wait_ge(S["qkb_ready"], upto(i, u))
                    x, y = (v.rearrange("p (h s f) -> p h s f", s=2, f=8) for v in (b.qkb, b.tb))
                    for s in range(2):
                        last = dve.tensor_tensor(y[:, :, s, :], x[:, :, 1 - s, :],
                                                 rep(con[:, C_SIN + 8 * s:C_SIN + 8 * s + 8][:, None, :], [P, 32, 8]), ALU.mult)
                    last.then_inc(S["ropeb_ready"], 1)
                for u in range(2):
                    b, k = at[u], 4 * u
                    dve.wait_ge(S["ropea_ready"], upto(i, u))
                    dve.wait_ge(S["ropeb_ready"], upto(i, u))
                    dve.tensor_tensor(b.sm, b.ta, b.tb, ALU.add).then_inc(S["rope_ready"], 1)
                for u in range(2):
                    b, k = at[u], 4 * u
                    dve.wait_ge(S["vrep_mm"], upto(i, u))
                    dve.tensor_tensor(b.vbd.rearrange("p (g h d) -> p g h d", h=4, d=MD),
                                      ps[:, k + 2:k + 4, :].rearrange("p a (g h d) -> p (a g) h d", h=4, d=MD),
                                      rep(con[:, C_VM:C_VM + 4][:, None, :, None], [P, 16, 4, MD]),
                                      ALU.mult).then_inc(S["vbd_ready"], 1)
                for u in range(2):
                    b, k = at[u], 4 * u
                    dve.wait_ge(S["qT_ready"], upto(i, u))
                    dve.tensor_tensor(b.kexp.rearrange("p (g h k) -> p g h k", g=2, h=8),
                                      rep(bank(k + 1, 256, 512).rearrange("p (g k) -> p g k", g=2)[:, :, None, :], [P, 2, 8, P]),
                                      rep(con[:, C_HM:C_HM + 8][:, None, :, None], [P, 2, 8, P]),
                                      ALU.mult).then_inc(S["kexp_ready"], 1)
                for u in range(2):
                    b, k = at[u], 4 * u
                    sm = b.sm.rearrange("p (h k) -> p h k", h=MH)
                    dve.wait_ge(S["score_mm"], upto(i, u))
                    dve.tensor_tensor(sm, bank(k).rearrange("p (h k) -> p h k", h=MH),
                                      rep(con[:, C_KEYB:C_KEYB + 32][:, None, :], [P, MH, 32]),
                                      ALU.add).then_inc(S["centre"], 1)
                    dve.wait_ge(S["centre"], third(i, u, 1))
                    dve.tensor_reduce(mx[u], sm, AX, ALU.max).then_inc(S["centre"], 1)
                    dve.wait_ge(S["centre"], third(i, u, 2))
                    dve.tensor_tensor(sm, sm, rep(mx[u][:, :, None], [P, MH, 32]), ALU.subtract).then_inc(S["centre"], 1)
                for u in range(2):
                    b, k = at[u], 4 * u
                    sm = b.sm.rearrange("p (h k) -> p h k", h=MH)
                    dve.wait_ge(S["exp_ready"], upto(i, u))
                    dve.tensor_reduce(sums[u], sm, AX, ALU.add).then_inc(S["prob"], 1)
                    dve.wait_ge(S["prob"], third(i, u, 1))
                    dve.reciprocal(recs[u], sums[u]).then_inc(S["prob"], 1)
                    dve.wait_ge(S["prob"], third(i, u, 2))
                    dve.tensor_tensor(sm, sm, rep(recs[u][:, :, None], [P, MH, 32]), ALU.mult).then_inc(S["prob"], 1)
                for u in range(2):
                    b, t, k = at[u], 2 * i + u, 4 * u
                    dve.wait_ge(S["awo_mm"], upto(i, u))
                    dve.wait_ge(S["n3b_ready"], upto(i, u))
                    dve.tensor_tensor(b.xa, bank(k + 3, 0, D), b.n3b, ALU.add).then_inc(S["xa_ready"], 1)
                    dve.wait_ge(S["xa_ready"], upto(i, u))
                    dve.bn_stats(bst[u], b.xa).then_inc(S["xastat"], 1)
                    dve.wait_ge(S["xastat"], third(i, u, 1))
                    dve.memset(spare, 0.0)
                    dve.bn_aggr(mv4[u], bst[u]).then_inc(S["xastat"], 1)
                    dve.wait_ge(S["xastat"], third(i, u, 2))
                    dve.tensor_scalar(ve4[u], mv4[u][:, 1:2], EPS, None, ALU.add).then_inc(S["xastat"], 1)
                for u in range(2):
                    b, t = at[u], 2 * i + u
                    dve.wait_ge(S["r4_ready"], upto(i, u))
                    dve.tensor_scalar(b.x1n, b.xa, mv4[u][:, 0:1], r4[u],
                                      ALU.subtract, ALU.mult).then_inc(S["x1n_ready"], 1)
                for u in range(2):
                    dve.wait_ge(S["x1g_ready"], upto(i, u))
                    dve.tensor_tensor(tile_of(x1, 2 * i + u), at[u].x1n, be1, ALU.add).then_inc(S["x1_ready"], 1)
                for u in range(2):
                    t, k = 2 * i + u, 4 * u
                    dve.wait_ge(S["gate_mm"], upto(i, u))
                    dve.tensor_tensor(lg[:, ds(t * E, E)], bank(k + 3, 256, 256 + E), bg, ALU.add).then_inc(S["logit_ready"], 1)
            with dve.Fori(0, PAIRS) as i:
                attn_dve(i)

            dve.wait_ge(S["logit_ready"], NT)
            steps = [0]

            def link(ins):
                steps[0] += 1
                ins.then_inc(S["route"], 1)
                dve.wait_ge(S["route"], steps[0])

            def te(ap):
                return ap.rearrange("p (t e) -> p t e", e=E)
            link(dve.tensor_reduce(lmax, te(lg), AX, ALU.max))
            link(dve.tensor_tensor(te(lg), te(lg), rep(lmax[:, :, None], [P, NT, E]), ALU.subtract))
            dve.wait_ge(S["logit_exp"], 1)
            link(dve.tensor_reduce(lsum, te(lg), AX, ALU.add))
            link(dve.reciprocal(lsum, lsum))
            link(dve.tensor_tensor(te(prob), te(lg), rep(lsum[:, :, None], [P, NT, E]), ALU.mult))
            four = [P, NT, E, E]
            mine, other = rep(te(prob)[:, :, :, None], four), rep(te(prob)[:, :, None, :], four)
            ahead, tied = (v.rearrange("p (t e j) -> p t e j", e=E, j=E) for v in (rt8[0], rt8[1]))
            link(dve.tensor_tensor(ahead, other, mine, ALU.is_gt))
            link(dve.tensor_tensor(tied, other, mine, ALU.is_equal))
            link(dve.tensor_tensor(rt8[1].rearrange("p (t c) -> p t c", t=NT), rt8[1].rearrange("p (t c) -> p t c", t=NT),
                                   rep(con[:, C_LT:C_LT + 64][:, None, :], [P, NT, 64]), ALU.mult))
            link(dve.tensor_tensor(rt8[0], rt8[0], rt8[1], ALU.add))
            link(dve.tensor_reduce(rank, rt8[0].rearrange("p (c j) -> p c j", j=E), AX, ALU.add))
            link(dve.tensor_scalar(sel0, rank, 0.5, None, ALU.is_lt))
            link(dve.tensor_scalar(chosen, rank, 1.5, None, ALU.is_lt))
            link(dve.tensor_tensor(sel1, chosen, sel0, ALU.subtract))
            link(dve.tensor_tensor(comb, prob, chosen, ALU.mult))
            link(dve.tensor_reduce(lsum, te(comb), AX, ALU.add))
            link(dve.reciprocal(lsum, lsum))
            link(dve.tensor_tensor(te(comb), te(comb), rep(lsum[:, :, None], [P, NT, E]), ALU.mult))
            link(dve.memset(cum[:, 0:E], 0.0))
            for t in range(NT):
                link(dve.tensor_tensor(cum[:, (t + 1) * E:(t + 2) * E], cum[:, t * E:(t + 1) * E],
                                       chosen[:, t * E:(t + 1) * E], ALU.add))
            assert steps[0] == CHOSEN
            for s, sel in enumerate((sel0, sel1)):
                link(dve.tensor_tensor(pick, comb, sel, ALU.mult))
                link(dve.tensor_reduce(wsel[:, s * NT:(s + 1) * NT], te(pick), AX, ALU.add))
            dve.wait_ge(S["count_mm"], 1)
            link(dve.tensor_copy(total, bank(0, 64, 72)))
            link(dve.tensor_tensor(te(pick), rep(total[:, :, None], [P, E, 8]),
                                   rep(con[:, C_TH:C_TH + 8][:, None, :], [P, E, 8]), ALU.is_gt))
            link(dve.tensor_reduce(tiles, te(pick), AX, ALU.add))
            link(dve.tensor_tensor(te(pick), rep(tiles[:, None, :], [P, E, E]), te(con[:, C_LT:C_LT + 64]), ALU.mult))
            link(dve.tensor_reduce(begin, te(pick), AX, ALU.add))
            link(dve.tensor_tensor(end, begin, tiles, ALU.add))
            link(dve.scalar_tensor_tensor(te(slot), rep(begin[:, None, :], [P, NT, E]), float(P),
                                          te(bank(0, 0, 64)), ALU.mult, ALU.add))
            for s, sel in enumerate((sel0, sel1)):
                link(dve.tensor_tensor(pick, slot, sel, ALU.mult))
                link(dve.tensor_reduce(picked, te(pick), AX, ALU.add))
                link(dve.tensor_copy(posi[:, s * NT:(s + 1) * NT], picked))
            ends = rt8[2][:, 0:SLOT_TILES * E].rearrange("p (j e) -> p j e", e=E)
            link(dve.tensor_tensor(ends, rep(end[:, None, :], [P, SLOT_TILES, E]),
                                   rep(con[:, C_SL:C_SL + SLOT_TILES][:, :, None], [P, SLOT_TILES, E]), ALU.is_le))
            link(dve.tensor_reduce(rt8[1][:, 0:SLOT_TILES], ends, AX, ALU.add))
            link(dve.tensor_scalar(tilee[:, :], rt8[1][:, 0:SLOT_TILES], float(E - 1), None, ALU.min))
            assert steps[0] == ROUTED

            dve.wait_ge(S["b2_mm"], 1)
            dve.wait_ge(S["scattered"], 16 * 2 * NT)
            for t in range(NT):
                dve.tensor_tensor(x1[:, t, :], x1[:, t, :], bank(4 + t // 2, t % 2 * D, t % 2 * D + D),
                                  ALU.add).then_inc(S["x1b_ready"], 1)

            def rows_out(t, u):
                dve.wait_ge(S["xgT_mm"], t + 1)
                dve.tensor_copy(xgT[u][:, :], bank(7, 0, D)).then_inc(S["xgT_ready"], 1)

            def hidden_out(t, u):
                dve.wait_ge(S["up_mm"], t + 1)
                dve.tensor_copy(hs[u], ps[:, 2 * u:2 * u + 2, :].rearrange("p a b -> p (a b)")).then_inc(S["up_ready"], 1)

            def output_out(t, u, y_sent):
                dve.wait_ge(S["down_mm"], t + 1)
                if y_sent is not None:
                    dve.wait_ge(S[f"y_out{u}"], y_sent)
                dve.tensor_copy(ys[u], bank(6, 0, D)).then_inc(S["ys_ready"], 1)
            rows_out(0, 0)
            hidden_out(0, 0)
            rows_out(1, 1)
            hidden_out(1, 1)
            rows_out(2, 0)
            output_out(0, 0, None)
            hidden_out(2, 0)
            rows_out(3, 1)
            output_out(1, 1, None)
            hidden_out(3, 1)
            rows_out(4, 0)
            output_out(2, 0, 16)
            with dve.Fori(2, SLOT_TILES // 2) as i:
                hidden_out(2 * i, 0)
                rows_out(2 * i + 1, 1)
                output_out(2 * i - 1, 1, 16 * i - 16)
                hidden_out(2 * i + 1, 1)
                rows_out(2 * i + 2, 0)
                output_out(2 * i, 0, 16 * i)
            t = SLOT_TILES - 1
            hidden_out(t, 0)
            output_out(t - 1, 1, 16 * (t // 2 - 1))
            output_out(t, 0, 16 * (t // 2))

            n = [0]

            def step(ins):
                n[0] += 1
                ins.then_inc(S["tail"], 1)
                dve.wait_ge(S["tail"], n[0])
            for t in range(NT):
                dve.wait_ge(gathered[t], 32)
                for s in range(2):
                    step(dve.scalar_tensor_tensor(x1[:, t, :], yg[:, s, t, :], wsel[:, s * NT + t:s * NT + t + 1],
                                                  x1[:, t, :], ALU.mult, ALU.add))
                step(dve.bn_stats(bst[t], x1[:, t, :]))
                step(dve.bn_aggr(mv5[:, 2 * t:2 * t + 2], bst[t]))
                step(dve.tensor_scalar(ve5[:, t:t + 1], mv5[:, 2 * t + 1:2 * t + 2], EPS, None, ALU.add))
                assert n[0] == TAIL1 * t + 5
                dve.wait_ge(S["r5_ready"], t + 1)
                step(dve.tensor_scalar(x1[:, t, :], x1[:, t, :], mv5[:, 2 * t:2 * t + 1], r5[:, t:t + 1],
                                       ALU.subtract, ALU.mult))
                step(dve.tensor_tensor(x1[:, t, :], x1[:, t, :], g2, ALU.mult))
                dve.wait_ge(S["hb_ready"], t + 1)
                dve.tensor_tensor(fin[:, t, :], x1[:, t, :], hres[:, t, :], ALU.add).then_inc(S["fin_ready"], 1)


INPUTS = ["x", "L0_tok_W", "L0_tok_b", "L0_attn_ln_w", "L0_attn_ln_b", "L0_attn_Wq", "L0_attn_Wk", "L0_attn_Wv",
          "L0_attn_Wb", "L0_attn_o_norm_w", "L0_attn_Wo", "L0_ffn_Wq", "L0_ffn_bq", "L0_ffn_Wk", "L0_ffn_bk",
          "L0_ffn_Wv", "L0_ffn_bv", "L0_ffn_Wo", "L0_ffn_bo", "L0_ffn_Wg", "L0_ffn_bg", "L0_ffn_W1", "L0_ffn_b1",
          "L0_ffn_W2", "L0_ffn_b2", "L0_ffn_g1", "L0_ffn_be1", "L0_ffn_g2", "L0_ffn_be2"]


def kernel(**inputs):
    import concourse.bacc as bacc
    from concourse.bass_utils import run_bass_kernel_spmd

    nc = bacc.Bacc("TRN2", target_bir_lowering=False, num_devices=1)
    arrays = {"in_" + name: np.ascontiguousarray(inputs[name]) for name in INPUTS}
    arrays["in_consts"] = constants()
    aps = {name[3:]: nc.dram_tensor(name, a.shape, F32, kind="ExternalInput").ap() for name, a in arrays.items()}
    out = nc.dram_tensor("out", (TOK, D), F32, kind="ExternalOutput").ap()
    tower(nc, aps, out)
    result = run_bass_kernel_spmd(nc, [arrays], core_ids=[0])
    return result.results[0]["out"].reshape(IMGS, SEQ, D)
```

```python
from contextlib import ExitStack

import numpy as np

import concourse.bass as bass
from concourse import mybir

F32 = mybir.dt.float32
I32 = mybir.dt.int32
ALU = mybir.AluOpType
ACT = mybir.ActivationFunctionType
AX = mybir.AxisListType.X
ds = bass.ds

P = 128
D = 256
DC = D // P
IMGS, SEQ = 64, 16
TOK = IMGS * SEQ
NT = TOK // P
PAIRS = NT // 2
KP = 768
KC = KP // P
H, DK, DV = 4, 64, 128
MH, MD = 16, 16
E, FF = 8, 1024
FC = FF // P
SLOT_TILES = 2 * TOK // P + E - 1
EPS = 1e-5
WEIGHED, CHOSEN, MAPPED0, MAPPED1, ROUTED = 17, 24, 44, 45, 46

C_ID = 0
C_NP = C_ID + P
C_M = C_NP + 2 * P
C_COS = C_M + P
C_SIN = C_COS + 8
C_KEYB = C_SIN + 16
C_HM = C_KEYB + 32
C_VM = C_HM + 8
C_REP = C_VM + 4
C_UP = C_REP + 4 * P
C_ONE = C_UP + P
C_LT = C_ONE + P
C_TH = C_LT + 64
C_SL = C_TH + 8
C_SE = C_SL + SLOT_TILES
C_TOK = C_SE + SLOT_TILES
C_IO = C_TOK + NT
C_END = C_IO + P


def constants():
    c = np.zeros((P, C_END), np.float32)
    p = np.arange(P)
    same = p[:, None] // SEQ == p[None, :] // SEQ
    c[:, C_ID:C_ID + P] = np.eye(P)
    c[:, C_NP:C_NP + P] = same & (p[:, None] < p[None, :])
    c[:, C_NP + P:C_NP + 2 * P] = same & (p[:, None] <= p[None, :])
    c[:, C_M:C_M + P] = same & (p[None, :] < p[:, None])
    freq = 1.0 / 10000.0 ** (np.arange(0, MD, 2, dtype=np.float32) / MD)
    ang = (p % SEQ).astype(np.float32)[:, None] * freq[None, :].astype(np.float32)
    c[:, C_COS:C_COS + 8] = np.cos(ang)
    c[:, C_SIN:C_SIN + 16] = np.concatenate([-np.sin(ang), np.sin(ang)], axis=1)
    key = np.arange(32)
    c[:, C_KEYB:C_KEYB + 32] = np.where(p[:, None] % 32 // SEQ == key[None, :] // SEQ, 0.0, -1e30)
    c[:, C_HM:C_HM + 8] = p[:, None] // MD == np.arange(8)[None, :]
    c[:, C_VM:C_VM + 4] = p[:, None] // 32 == np.arange(4)[None, :]
    for j in range(4):
        c[:, C_REP + j * P:C_REP + (j + 1) * P] = p[:, None] == 32 * j + p[None, :] % 32
    c[:, C_UP:C_UP + P] = p[:, None] < p[None, :]
    c[:, C_ONE:C_ONE + P] = 1.0
    e = np.arange(E)
    c[:, C_LT:C_LT + 64] = (e[None, :] < e[:, None]).astype(np.float32).reshape(1, 64)
    c[:, C_TH:C_TH + 8] = P * np.arange(8)
    c[:, C_SL:C_SL + SLOT_TILES] = np.arange(SLOT_TILES)
    c[:, C_SE:C_SE + SLOT_TILES] = P * np.arange(1, SLOT_TILES + 1)
    c[:, C_TOK:C_TOK + NT] = P * np.arange(NT)[None, :] + p[:, None]
    c[:, C_IO:C_IO + P] = np.arange(P)
    return c


SEMS = """
x_in0 x_in1 const_in tokw_in rows_in bias_in attnw_in ffnw_in w1_in w2lo_in w2hi_in
exponents_set
wT_mm xT_even_ready wT_ready x_split0 x_split1 xT_mm xT_ready emb_mm h_ready hstat_a hstat_b hstat_ready r1_ready rt_ready
r2_ready n1_ready hres_ready rows_mm cols_ready
n2_ready n2_mm n2T_ready beta_mm qk_mm v_mm beta_act qk_act v_act beta_ready ssq
rn_ready qnorm_ready knorm_ready kb_ready y0_ready kqT_mm kT_mm kqT_ready kT_ready np_mm m_mm np_ready m_ready
y1_mm m2_mm n2p_mm y1_ready m2_ready n2p_ready y2_mm m4_mm n4_mm y2_ready m4_ready n4_ready y3_mm n8_mm
y3_ready n8_ready y4_mm y4_ready o_mm oss_ready orv_ready orms_ready on_ready oT_mm oT_ready wo_mm h2_ready h2s_ready
h2stat r3_ready exp_table silu_table
n3_ready n3b_ready n3_mm n3T_ready aqk_mm av_mm vs_ready vrep_mm qkb_ready ropea_ready ropeb_ready rope_ready
vbd_ready qkT_mm qT_ready kexp_ready score_mm centre exp_ready prob
pT_mm pT_ready pv_mm aoT_ready awo_mm xa_ready xastat r4_ready
x1n_ready x1g_ready x1_ready x1T_mm x1T_ready gate_mm logit_ready
route logit_exp count_mm combT_mm combT_ready b2_mm x1b_ready x1_out map_mm hb_ready
slot_in0 slot_in1 xgT_mm xgT_ready up_mm up_ready hT_mm act_ready down_mm ys_ready y_out0 y_out1
tail ve5_ready r5_ready fin_ready out_done
""".split()


def tower(nc, A, out):
    with ExitStack() as ctx:
        def sb(name, shape, dt=F32):
            return ctx.enter_context(nc.sbuf_tensor(name, shape, dt))

        S = {name: ctx.enter_context(nc.semaphore(name)) for name in SEMS}

        w1 = sb("w1", [P, E * DC * FF])
        w2 = sb("w2", [P, E * FC * D])
        XL = KC * 512
        x_raw = [w2[:, k * XL:(k + 1) * XL] for k in range(2)]
        x_tok = [w2[:, (2 + k) * XL:(3 + k) * XL] for k in range(2)]
        xT = [w2[:, 4 * XL:5 * XL], w2[:, 0:XL]]
        con = sb("con", [P, C_END])
        hres = sb("hres", [P, NT, D])
        x1 = sb("x1", [P, NT, D])
        cols = sb("cols", [P, 76])
        misc = sb("misc", [P, 400])
        wqk_a = sb("wqk_a", [P, DC, 512])
        wv_a = sb("wv_a", [P, DC, 512])
        wb_a = sb("wb_a", [P, DC, H])
        wo_a = sb("wo_a", [P, H, D])
        wqk_f = sb("wqk_f", [P, DC, 512])
        wv_f = sb("wv_f", [P, DC, D])
        wo_f = sb("wo_f", [P, DC, D])
        wg_f = sb("wg_f", [P, DC, E])
        b2_f = sb("b2_f", [E, D])
        bc = sb("bc", [P, 8 * D + E])
        tokb, bqk, bo = bc[:, 0:D], bc[:, D:3 * D], bc[:, 3 * D:4 * D]
        g1, be1, g2, be2 = (bc[:, (4 + k) * D:(5 + k) * D] for k in range(4))
        bg = bc[:, 8 * D:8 * D + E]

        work = sb("work", [P, 5200])
        tokw = work[:, 0:2 * KP]
        tokwT = work[:, 2 * KP:4 * KP]
        rows = work[0:76, 4 * KP:4 * KP + P]
        ident = con[:, C_ID:C_ID + P]

        def m(a, n):
            return misc[:, a:a + n]
        mv1, ve1, r1, rt, r2 = m(0, 16), m(16, 8), m(24, 8), m(32, 8), m(40, 8)
        mv3, ve3, r3 = m(48, 2), m(50, 1), m(51, 1)
        mv4, ve4, r4 = m(80, 2), m(82, 1), m(83, 1)
        mv5, ve5, r5 = m(112, 16), m(128, 8), m(136, 8)
        negh = m(144, 8)
        bst = [m(152 + 6 * k, 6) for k in range(8)]
        th, beta, oss, orv, orms = (m(200 + 4 * k, 4) for k in range(5))
        ssq0, ssq, rn = (m(220 + 8 * k, 8) for k in range(3))
        mx, sums, recs = (m(244 + 16 * k, 16) for k in range(3))
        spare, spare_in, spare_exp, spare_silu = (m(292 + k, 1) for k in range(4))

        LNW, LNB, ONW, BV, G1, BE1, B1 = 0, 2, 4, 5, 7, 9, 11
        ps = ctx.enter_context(nc.psum_tensor("ps", [P, 8, 512], F32))

        def bank(n, a=0, b=512):
            return ps[:, n, a:b]

        x1_dram = nc.dram_tensor("mixture_x", [TOK, D], F32, kind="Internal").ap()
        ys_dram = nc.dram_tensor("slots_y", [SLOT_TILES * P, D], F32, kind="Internal").ap()

        hi = w2[:, E * FC * D // 2:]
        kqT = hi[:, 0:512]
        y = [hi[:, 512:1024], hi[:, 1024:1536]]
        qk = hi[:, 1536:2048]
        npm = hi[:, 2048:3072]
        sq = npm[:, 0:512]
        mm_ = hi[:, 3072:3584]
        m2 = hi[:, 3584:4096]
        n2p = hi[:, 4096:4608]
        n4 = hi[:, 4608:5120]
        kexp = hi[:, 5120:7168]
        vbd = hi[:, 7168:8192]
        n2, n2T, h2 = (work[:, k * D:(k + 1) * D] for k in range(3))
        n3, n3b, n3T, vs, qT, aoT, xa, x1n = (work[:, (3 + k) * D:(4 + k) * D] for k in range(8))
        qkb, ta, sm, pT = (work[:, 11 * D + k * 512:11 * D + (k + 1) * 512] for k in range(4))
        tb, x1T = pT, work[:, 11 * D + 2048:12 * D + 2048]
        lg = sb("lg", [P, NT * E])
        o = 0
        rt8 = []
        for k in range(3):
            rt8.append(work[:, o:o + 512])
            o += 512
        small = []
        for k in range(16):
            small.append(work[:, o:o + 72])
            o += 72
        combT = work[0:E, o:o + 2 * 512]
        o += 1024
        tile_ends = work[:, o:o + 2 * NT * SLOT_TILES]
        onehot = [work[:, o + 384:o + 384 + NT * P], work[:, 0:NT * P]]
        tok_col = work[:, 2 * 512:2 * 512 + 2 * NT * SLOT_TILES]
        lmax, lsum, prob, rank, sel0, sel1, chosen, comb = (small[k][:, 0:64] for k in range(8))
        lmax, lsum = lmax[:, 0:NT], lsum[:, 0:NT]
        cum, pick, place = small[8], small[9][:, 0:64], small[10][:, 0:64]
        total, tiles, begin, end = (small[11][:, 8 * k:8 * k + 8] for k in range(4))
        slots, slot_tile, in_tile = (small[12][:, 16 * k:16 * k + 16] for k in range(3))
        lead0, lead1, owner = small[13][:, 0:64], small[14][:, 0:64], small[15][:, 0:SLOT_TILES]
        xg = [sb(f"xg{u}", [P, D]) for u in range(2)]
        xgT = [sb(f"xgT{u}", [P, D]) for u in range(2)]
        kb, kT = xgT[0][:, :], xgT[1][:, :]
        hs = [work[:, u * FF:(u + 1) * FF] for u in range(2)]
        gT = [work[:, (2 + u) * FF:(3 + u) * FF] for u in range(2)]
        ys = [work[:, 4 * FF + u * D:4 * FF + (u + 1) * D] for u in range(2)]
        posi = sb("posi", [P, 2 * NT], I32)
        tilee = sb("tilee", [P, SLOT_TILES], I32)
        slot_tok = sb("slot_tok", [P, SLOT_TILES], I32)
        wsel = sb("wsel", [P, 2 * NT])
        yg = w1[:, 0:2 * NT * D].rearrange("p (k t d) -> p k t d", k=2, t=NT)
        fin = w1[:, 2 * NT * D:3 * NT * D].rearrange("p (t d) -> p t d", t=NT)

        gathered = [ctx.enter_context(nc.semaphore(f"gathered{t}")) for t in range(NT)]

        def x_split(copy, half, c):
            src = x_raw[half][:, c * 1024:(c + 1) * 1024].rearrange("p (r w j) -> p r w j", r=16, w=4)
            dst = x_tok[half].rearrange("p (w c r j) -> p c r w j", w=4, c=3, r=16)[:, c]
            return copy(dst, src)

        def xT_in(half, q):
            return bank(4 + (KC * half + q) % 3).rearrange("p (w b) -> p w b", w=4)

        def xT_out(half, q):
            return xT[half][:, q * 512:(q + 1) * 512].rearrange("p (b w) -> p w b", w=4)

        def tile_of(buf, t):
            return buf[:, ds(t, 1), :].rearrange("p a d -> p (a d)")

        def eights(ap):
            return ap.rearrange("p (h f) -> p h f", f=8)

        def heads4(ap):
            return ap.rearrange("p (h d) -> p h d", h=H)

        def rep(ap, shape):
            return ap.broadcast_to(shape)

        def is_first(t):
            return isinstance(t, int) and t == 0

        def is_last(t):
            return isinstance(t, int) and t == NT - 1

        def run_slots(eng, slot):
            slot(0, True, False, False)
            slot(1, True, True, False)
            with eng.Fori(2, NT - 1) as t:
                slot(t, True, True, True)
            slot(NT - 1, True, True, True)
            slot(NT, False, True, True)
            slot(NT + 1, False, False, True)

        block = ctx.enter_context(nc.Block())

        @block.sync
        def _(sp):
            for half in range(2):
                for c in range(3):
                    src = A["x"][32 * half:32 * half + 32, c].rearrange("b (h r) w -> b h (r w)", r=16)
                    sp.dma_start(x_raw[half][:, c * 1024:(c + 1) * 1024], src).then_inc(S[f"x_in{half}"], 16)
                if half == 0:
                    sp.dma_start(con[:, :], A["consts"]).then_inc(S["const_in"], 16)
                    sp.dma_start(tokw.rearrange("p (c k) -> p c k", c=DC),
                                 A["L0_tok_W"].rearrange("(c p) k -> p c k", p=P)).then_inc(S["tokw_in"], 16)
            for dst, name in ((wqk_a[:, :, 0:256], "L0_attn_Wq"), (wqk_a[:, :, 256:512], "L0_attn_Wk"),
                              (wv_a[:, :, :], "L0_attn_Wv"), (wb_a[:, :, :], "L0_attn_Wb"),
                              (wo_a[:, :, :], "L0_attn_Wo")):
                sp.dma_start(dst, A[name].rearrange("(c p) n -> p c n", p=P)).then_inc(S["attnw_in"], 16)
            for dst, name in ((wqk_f[:, :, 0:256], "L0_ffn_Wq"), (wqk_f[:, :, 256:512], "L0_ffn_Wk"),
                              (wv_f[:, :, :], "L0_ffn_Wv"), (wo_f[:, :, :], "L0_ffn_Wo"),
                              (wg_f[:, :, :], "L0_ffn_Wg")):
                sp.dma_start(dst, A[name].rearrange("(c p) n -> p c n", p=P)).then_inc(S["ffnw_in"], 16)
            sp.dma_start(b2_f[:, :], A["L0_ffn_b2"]).then_inc(S["ffnw_in"], 16)
            for e in range(E):
                sp.dma_start(w1[:, e * DC * FF:(e + 1) * DC * FF].rearrange("p (c f) -> p c f", c=DC),
                             A["L0_ffn_W1"][e].rearrange("(c p) f -> p c f", p=P)).then_inc(S["w1_in"], 16)

            def w2_load(e, sem):
                sp.dma_start(w2[:, e * FC * D:(e + 1) * FC * D].rearrange("p (c d) -> p c d", c=FC),
                             A["L0_ffn_W2"][e].rearrange("(c p) d -> p c d", p=P)).then_inc(S[sem], 16)
            sp.wait_ge(S["emb_mm"], NT)
            for e in range(E // 2):
                w2_load(e, "w2lo_in")
            with sp.Fori(0, NT - 1) as t:
                sp.wait_ge(S["x1_ready"], t + 1)
                sp.dma_start(x1_dram[ds(t * P, P), :], tile_of(x1, t)).then_inc(S["x1_out"], 16)
            sp.wait_ge(S["awo_mm"], NT)
            for e in range(E // 2, E):
                w2_load(e, "w2hi_in")

            def slot_store(t, u):
                sp.wait_ge(S["ys_ready"], t + 1)
                sp.dma_start(ys_dram[ds(t * P, P), :], ys[u]).then_inc(S[f"y_out{u}"], 16)

            with sp.Fori(0, SLOT_TILES // 2) as i:
                for u in range(2):
                    slot_store(2 * i + u, u)
            slot_store(SLOT_TILES - 1, 0)

            for t in range(NT):
                sp.wait_ge(S["fin_ready"], t + 1)
                sp.dma_start(out[t * P:(t + 1) * P, :], fin[:, t, :]).then_inc(S["out_done"], 16)
            sp.wait_ge(S["out_done"], 16 * NT)

        @block.gpsimd
        def _(pool):
            pool.memset(negh, -0.5).then_inc(S["exponents_set"], 1)
            pool.memset(spare_in, 0.0).then_inc(S["exponents_set"], 1)
            pool.wait_ge(S["exponents_set"], 2)

            def inv_root(dst, src, n, sem):
                pool.tensor_tensor(dst, src, negh[:, 0:n], ALU.pow).then_inc(S[sem], 1)

            for half in range(2):
                pool.wait_ge(S[f"x_in{half}"], 48)
                x_split(pool.tensor_copy, half, 2).then_inc(S[f"x_split{half}"], 1)
            for half in range(2):
                a, b = 4 * half, 4 * half + 4
                pool.wait_ge(S["hstat_ready"], half + 1)
                inv_root(r1[:, a:b], ve1[:, a:b], 4, "r1_ready")
                var = mv1.rearrange("p (t k) -> p t k", k=2)[:, a:b, 1]
                pool.wait_ge(S["r1_ready"], half + 1)
                pool.tensor_tensor(rt[:, a:b], var, r1[:, a:b], ALU.mult).then_inc(S["rt_ready"], 1)
                pool.wait_ge(S["rt_ready"], 3 * half + 1)
                pool.tensor_tensor(rt[:, a:b], rt[:, a:b], r1[:, a:b], ALU.mult).then_inc(S["rt_ready"], 1)
                pool.wait_ge(S["rt_ready"], 3 * half + 2)
                pool.tensor_scalar(rt[:, a:b], rt[:, a:b], EPS, None, ALU.add).then_inc(S["rt_ready"], 1)
                pool.wait_ge(S["rt_ready"], 3 * half + 3)
                inv_root(r2[:, a:b], rt[:, a:b], 4, "r2_ready")
                for t in range(a, b):
                    pool.wait_ge(S["n1_ready"], t + 1)
                    pool.tensor_tensor(hres[:, t, :], hres[:, t, :], x1[:, t, :], ALU.add).then_inc(S["hres_ready"], 1)

            pool.wait_ge(S["r2_ready"], 2)

            def delta_norm(t, first):
                if not first:
                    pool.wait_ge(S["n2_mm"], t)
                pool.tensor_tensor(n2, tile_of(x1, t), rep(r2[:, ds(t, 1)], [P, D]), ALU.mult).then_inc(S["n2_ready"], 1)
            delta_norm(0, True)

            def next_norm(t):
                pool.wait_ge(S["n2_mm"], t)
                pool.tensor_tensor(n2, tile_of(x1, t), rep(r2[:, ds(t, 1)], [P, D]), ALU.mult).then_inc(S["n2_ready"], 1)

            def qk_root(t):
                pool.wait_ge(S["ssq"], 3 * t + 3)
                inv_root(rn, ssq, 8, "rn_ready")

            def slot(t, delta, attn, tail):
                if attn:
                    if tail:
                        pool.wait_ge(S["xa_ready"], t - 1)
                    pool.wait_ge(S["n3_ready"], t)
                    pool.tensor_tensor(n3b, n3, bo, ALU.add).then_inc(S["n3b_ready"], 1)
                if delta and not is_last(t):
                    next_norm(t + 1)
                if tail:
                    pool.wait_ge(S["xastat"], 3 * t - 3)
                    inv_root(r4, ve4, 1, "r4_ready")
                    pool.wait_ge(S["x1T_mm"], t - 1)
                    pool.tensor_tensor(x1n, x1n, g1, ALU.mult).then_inc(S["x1g_ready"], 1)
                if attn:
                    pool.wait_ge(S["qkb_ready"], t)
                    pool.tensor_tensor(eights(ta), eights(qkb), rep(con[:, C_COS:C_COS + 8][:, None, :], [P, 64, 8]),
                                       ALU.mult).then_inc(S["ropea_ready"], 1)
                if delta:
                    pool.wait_ge(S["orv_ready"], t + 1)
                    inv_root(orms, orv, 4, "orms_ready")
                    if not is_last(t):
                        qk_root(t + 1)
                    pool.wait_ge(S["h2stat"], 3 * t + 3)
                    inv_root(r3, ve3, 1, "r3_ready")
            qk_root(0)
            pool.wait_ge(S["bias_in"], 16 * 9)
            run_slots(pool, slot)

            pool.wait_ge(S["h2_ready"], NT)
            for t in range(NT):
                pool.tensor_tensor(hres[:, t, :], hres[:, t, :], be2, ALU.add).then_inc(S["hb_ready"], 1)

            pool.wait_ge(S["x1_out"], 16 * NT)
            pool.wait_ge(S["route"], ROUTED)
            for t in range(SLOT_TILES):
                if t >= 2:
                    pool.wait_ge(S["xgT_mm"], t - 1)
                pool.indirect_dma_start(
                    out=xg[t % 2][:, :], out_offset=None, in_=x1_dram,
                    in_offset=bass.IndirectOffsetOnAxis(slot_tok[:, t:t + 1], 0)).then_inc(S[f"slot_in{t % 2}"], 16)

            pool.wait_ge(S["y_out0"], 16 * (SLOT_TILES // 2 + 1))
            pool.wait_ge(S["y_out1"], 16 * (SLOT_TILES // 2))

            def last_root(t):
                pool.wait_ge(S["ve5_ready"], t + 1)
                inv_root(r5[:, t:t + 1], ve5[:, t:t + 1], 1, "r5_ready")
            for t in range(NT):
                for k in range(2):
                    pool.indirect_dma_start(
                        out=yg[:, k, t, :], out_offset=None, in_=ys_dram,
                        in_offset=bass.IndirectOffsetOnAxis(posi[:, k * NT + t:k * NT + t + 1], 0)
                    ).then_inc(gathered[t], 16)
                if t >= 2:
                    last_root(t - 2)
            last_root(NT - 2)
            last_root(NT - 1)

        @block.scalar
        def _(act):
            r = 0
            for name, n in (("L0_attn_ln_w", 2), ("L0_attn_ln_b", 2), ("L0_attn_o_norm_w", 1), ("L0_ffn_bv", 2),
                            ("L0_ffn_g1", 2), ("L0_ffn_be1", 2)):
                act.dma_start(rows[r:r + n, :], A[name].rearrange("(c p) -> c p", p=P)).then_inc(S["rows_in"], 16)
                r += n
            act.dma_start(rows[r:r + E * FC, :],
                          A["L0_ffn_b1"].rearrange("e (c p) -> (e c) p", p=P)).then_inc(S["rows_in"], 16)
            for dst, name in ((tokb, "L0_tok_b"), (bqk[:, 0:D], "L0_ffn_bq"), (bqk[:, D:2 * D], "L0_ffn_bk"),
                              (bo, "L0_ffn_bo"), (g1, "L0_ffn_g1"), (be1, "L0_ffn_be1"), (g2, "L0_ffn_g2"),
                              (be2, "L0_ffn_be2"), (bg, "L0_ffn_bg")):
                act.dma_start(dst, A[name].partition_broadcast(P)).then_inc(S["bias_in"], 16)

            for half in range(2):
                act.wait_ge(S[f"x_in{half}"], 48)
                x_split(act.copy, half, 1).then_inc(S[f"x_split{half}"], 1)
                for q in range(1, KC, 2):
                    act.wait_ge(S["xT_mm"], KC * half + q + 1)
                    act.copy(xT_out(half, q), xT_in(half, q)).then_inc(S["xT_ready"], 1)
            act.wait_ge(S["rows_mm"], 1)
            act.copy(cols[:, 0:75], bank(0, 256, 331)).then_inc(S["cols_ready"], 1)
            act.wait_ge(S["cols_ready"], 1)

            def turned_norm(t):
                act.wait_ge(S["n2_mm"], t + 1)
                for c in range(DC):
                    last = act.activation(n2T[:, c * P:(c + 1) * P], bank(5, c * P, (c + 1) * P), ACT.Identity,
                                          bias=cols[:, LNB + c:LNB + c + 1], scale=cols[:, LNW + c:LNW + c + 1])
                last.then_inc(S["n2T_ready"], 1)

            def silus(t):
                act.wait_ge(S["beta_mm"], t + 1)
                act.activation(th, bank(2, 256, 260), ACT.Tanh, scale=0.5).then_inc(S["beta_act"], 1)
                act.wait_ge(S["qk_mm"], t + 1)
                act.activation(qk, bank(5), ACT.Silu).then_inc(S["qk_act"], 1)
                act.wait_ge(S["v_mm"], t + 1)
                if not is_first(t):
                    act.wait_ge(S["oss_ready"], t)
                act.activation(y[1], bank(4), ACT.Silu).then_inc(S["v_act"], 1)

            def slot(t, delta, attn, tail):
                if delta:
                    act.wait_ge(S["kT_mm"], t + 1)
                    act.copy(kT, bank(3, 0, 256)).then_inc(S["kT_ready"], 1)
                    act.wait_ge(S["kqT_mm"], t + 1)
                    act.copy(kqT, bank(1)).then_inc(S["kqT_ready"], 1)
                if attn:
                    act.wait_ge(S["n3_mm"], t)
                    act.copy(n3T, bank(4, 0, 256)).then_inc(S["n3T_ready"], 1)
                if attn:
                    act.wait_ge(S["av_mm"], t)
                    act.copy(vs, bank(4, 256, 512)).then_inc(S["vs_ready"], 1)
                if tail:
                    act.wait_ge(S["x1T_mm"], t - 1)
                    for c in range(DC):
                        last = act.activation(x1T[:, c * P:(c + 1) * P], bank(6, 256 + c * P, 256 + (c + 1) * P),
                                              ACT.Identity, bias=cols[:, BE1 + c:BE1 + c + 1],
                                              scale=cols[:, G1 + c:G1 + c + 1])
                    last.then_inc(S["x1T_ready"], 1)
                if delta:
                    act.wait_ge(S["m2_mm"], t + 1)
                    act.copy(m2, bank(3)).then_inc(S["m2_ready"], 1)
                    act.wait_ge(S["n2p_mm"], t + 1)
                    act.copy(n2p, bank(1)).then_inc(S["n2p_ready"], 1)
                if attn:
                    act.wait_ge(S["qkT_mm"], t)
                    act.copy(qT, bank(5, 0, 256)).then_inc(S["qT_ready"], 1)
                if delta:
                    act.wait_ge(S["m4_mm"], t + 1)
                    act.copy(mm_, bank(3)).then_inc(S["m4_ready"], 1)
                    act.wait_ge(S["n4_mm"], t + 1)
                    act.copy(n4, bank(1)).then_inc(S["n4_ready"], 1)
                if attn:
                    if not (isinstance(t, int) and t == 1):
                        act.wait_ge(S["exp_table"], t - 1)
                    act.activation(spare_exp, spare_in, ACT.Exp).then_inc(S["exp_table"], 1)
                if delta:
                    act.wait_ge(S["n8_mm"], t + 1)
                    act.copy(m2, bank(3)).then_inc(S["n8_ready"], 1)
                    if not is_last(t):
                        turned_norm(t + 1)
                if attn:
                    act.wait_ge(S["centre"], 3 * t)
                    act.activation(sm, sm, ACT.Exp, scale=MD ** -0.5).then_inc(S["exp_ready"], 1)
                if delta:
                    if not is_last(t):
                        if not is_first(t):
                            act.wait_ge(S["silu_table"], t)
                        act.activation(spare_silu, spare_in, ACT.Silu).then_inc(S["silu_table"], 1)
                    act.wait_ge(S["o_mm"], t + 1)
                    for h in range(H):
                        last = act.activation(y[1][:, h * DV:(h + 1) * DV], bank(1, h * DV, (h + 1) * DV),
                                              ACT.Square, accum_out=oss[:, h:h + 1])
                    last.then_inc(S["oss_ready"], 1)
                    if not is_last(t):
                        silus(t + 1)
                if attn:
                    act.wait_ge(S["pT_mm"], t)
                    act.copy(pT, bank(7)).then_inc(S["pT_ready"], 1)
                if delta:
                    act.wait_ge(S["oT_mm"], t + 1)
                    act.activation(n4, bank(3), ACT.Copy, scale=cols[:, ONW:ONW + 1]).then_inc(S["oT_ready"], 1)
                if attn:
                    act.wait_ge(S["pv_mm"], t)
                    for c in range(DC):
                        last = act.activation(aoT[:, c * P:(c + 1) * P], bank(6, c * P, (c + 1) * P), ACT.Identity,
                                              bias=cols[:, BV + c:BV + c + 1])
                    last.then_inc(S["aoT_ready"], 1)
            act.wait_ge(S["exponents_set"], 2)
            turned_norm(0)
            silus(0)
            run_slots(act, slot)

            act.wait_ge(S["x1_ready"], NT)
            act.dma_start(x1_dram[(NT - 1) * P:NT * P, :], x1[:, NT - 1, :]).then_inc(S["x1_out"], 16)
            act.wait_ge(S["route"], 2)
            act.activation(lg[:, :], lg[:, :], ACT.Exp).then_inc(S["logit_exp"], 1)
            act.wait_ge(S["combT_mm"], 1)
            act.copy(combT, ps[0:E, 1:3, :].rearrange("p a b -> p (a b)")).then_inc(S["combT_ready"], 1)

            act.wait_ge(S["route"], ROUTED)

            def moe_act(t, u):
                e = act.value_load(tilee[0:1, ds(t, 1)], min_val=0, max_val=E - 1)
                act.wait_ge(S["hT_mm"], t + 1)
                for f in range(FC):
                    last = act.activation(gT[u][:, f * P:(f + 1) * P], bank(4 + f // 4, f % 4 * P, f % 4 * P + P),
                                          ACT.Gelu, bias=cols[:, ds(e * FC + (B1 + f), 1)])
                last.then_inc(S["act_ready"], 1)
            with act.Fori(0, SLOT_TILES // 2) as i:
                for u in range(2):
                    moe_act(2 * i + u, u)
            moe_act(SLOT_TILES - 1, 0)

        @block.tensor
        def _(pe):
            pe.wait_ge(S["const_in"], 16)
            pe.wait_ge(S["tokw_in"], 16)
            for q in range(KC):
                for c in range(DC):
                    n = q * DC + c
                    mm = pe.transpose(bank(n // 4, n % 4 * P, n % 4 * P + P), tokw[:, c * KP + q * P:c * KP + (q + 1) * P],
                                      ident)
                if n % 4 == 3:
                    mm.then_inc(S["wT_mm"], 1)
            for half in range(2):
                pe.wait_ge(S[f"x_split{half}"], 3)
                for q in range(KC):
                    n = KC * half + q
                    if n >= 3:
                        pe.wait_ge(S["xT_ready" if (n - 3) % 2 else "xT_even_ready"], (n - 3) // 2 + 1)
                    for w in range(4):
                        mm = pe.transpose(bank(4 + n % 3, w * P, w * P + P),
                                          x_tok[half][:, w * KP + q * P:w * KP + (q + 1) * P], ident)
                    mm.then_inc(S["xT_mm"], 1)
                pe.wait_ge(S["xT_ready"], 3 * half + 3)
                pe.wait_ge(S["xT_even_ready"], 3 * half + 3)
                pe.wait_ge(S["wT_ready"], 3)
                for tt in range(4):
                    t = 4 * half + tt
                    if t >= 4:
                        pe.wait_ge(S["h_ready"], t - 3)
                    for q in range(KC):
                        mm = pe.matmul(bank(t % 4, 0, D), xT[half][:, q * 512 + tt * P:q * 512 + (tt + 1) * P],
                                       tokwT[:, q * D:(q + 1) * D], start=(q == 0), stop=(q == KC - 1))
                    mm.then_inc(S["emb_mm"], 1)
            pe.wait_ge(S["rows_in"], 16 * 7)
            pe.wait_ge(S["h_ready"], NT)
            pe.transpose(bank(0, 256, 331), rows[0:75, :], ident[0:75, 0:75]).then_inc(S["rows_mm"], 1)
            pe.wait_ge(S["cols_ready"], 1)
            pe.wait_ge(S["attnw_in"], 16 * 5)

            pe.wait_ge(S["ffnw_in"], 16 * 6)

            def turn_norm(t):
                pe.wait_ge(S["n2_ready"], t + 1)
                for c in range(DC):
                    mm = pe.transpose(bank(5, c * P, (c + 1) * P), n2[:, c * P:(c + 1) * P], ident)
                mm.then_inc(S["n2_mm"], 1)

            def project(dst, lhsT, w, sem):
                for c in range(DC):
                    mm = pe.matmul(dst, lhsT[:, c * P:(c + 1) * P], w[:, c, :], start=(c == 0), stop=(c == DC - 1))
                mm.then_inc(S[sem], 1)

            def project_delta(t):
                pe.wait_ge(S["n2T_ready"], t + 1)
                project(bank(2, 256, 260), n2T, wb_a, "beta_mm")
                project(bank(5), n2T, wqk_a, "qk_mm")
                project(bank(4), n2T, wv_a, "v_mm")

            def heads(dst, lhsT, rhs, sem):
                for h in range(H):
                    mm = pe.matmul(dst[:, h * P:(h + 1) * P], lhsT(h), rhs(h), start=True, stop=True)
                mm.then_inc(S[sem], 1)

            def by_head(buf):
                return lambda h: buf[:, h * P:(h + 1) * P]

            def by_parity(buf, width, off=0):
                return lambda h: buf[:, (h % 2) * 2 * width + (h // 2) * width + off:
                                     (h % 2) * 2 * width + (h // 2) * width + off + P]

            def slot(t, delta, attn, tail):
                if delta:
                    pe.wait_ge(S["knorm_ready"], t + 1)
                    for p in range(2):
                        mm = pe.transpose(bank(3, p * P, (p + 1) * P), qk[:, 256 + p * P:256 + (p + 1) * P], ident)
                    mm.then_inc(S["kT_mm"], 1)
                    pe.wait_ge(S["kb_ready"], t + 1)
                    for p in range(2):
                        pe.transpose(bank(1, p * 256, p * 256 + P), kb[:, p * P:(p + 1) * P], ident)
                        mm = pe.transpose(bank(1, p * 256 + P, p * 256 + 256), qk[:, p * P:(p + 1) * P], ident)
                    mm.then_inc(S["kqT_mm"], 1)
                if tail:
                    pe.wait_ge(S["aoT_ready"], t - 1)
                    project(bank(7, 0, D), aoT, wo_f, "awo_mm")
                if delta:
                    pe.wait_ge(S["kT_ready"], t + 1)
                    pe.wait_ge(S["kqT_ready"], t + 1)
                    pe.wait_ge(S["beta_act"], t + 1)
                    for hp in range(2):
                        for par in range(2):
                            r = slice(64 * par, 64 * par + 64)
                            mm = pe.matmul(bank(1 + par, hp * 256, hp * 256 + 256), kT[r, hp * P:(hp + 1) * P],
                                           kqT[r, hp * 256:hp * 256 + 256], start=True, stop=True)
                    mm.then_inc(S["np_mm"], 1)
                if attn:
                    pe.wait_ge(S["n3_ready"], t)
                    pe.wait_ge(S["v_act"], t)
                    for c in range(DC):
                        mm = pe.transpose(bank(4, c * P, (c + 1) * P), n3[:, c * P:(c + 1) * P], ident)
                    mm.then_inc(S["n3_mm"], 1)
                if delta:
                    if not is_first(t):
                        pe.wait_ge(S["h2_ready"], t)
                    for hp in range(2):
                        for par in range(2):
                            r = slice(64 * par, 64 * par + 64)
                            mm = pe.matmul(bank(3 * par, hp * P, (hp + 1) * P), kqT[r, hp * 256:hp * 256 + P],
                                           kT[r, hp * P:(hp + 1) * P], start=True, stop=True)
                    mm.then_inc(S["m_mm"], 1)
                if attn:
                    pe.wait_ge(S["n3T_ready"], t)
                    project(bank(5), n3T, wqk_f, "aqk_mm")
                    project(bank(4, 256, 512), n3T, wv_f, "av_mm")
                if tail:
                    pe.wait_ge(S["x1n_ready"], t - 1)
                    for c in range(DC):
                        mm = pe.transpose(bank(6, 256 + c * P, 256 + (c + 1) * P), x1n[:, c * P:(c + 1) * P], ident)
                    mm.then_inc(S["x1T_mm"], 1)
                if delta:
                    n, m_ = by_parity(npm, 256), by_parity(mm_, P)
                    pe.wait_ge(S["np_ready"], t + 1)
                    pe.wait_ge(S["y0_ready"], t + 1)
                    pe.wait_ge(S["m_ready"], t + 1)
                    heads(bank(0), n, by_head(y[0]), "y1_mm")
                    heads(bank(3), n, m_, "m2_mm")
                    heads(bank(1), m_, n, "n2p_mm")
                if tail:
                    pe.wait_ge(S["x1T_ready"], t - 1)
                    project(bank(7, 256, 256 + E), x1T, wg_f, "gate_mm")
                if attn:
                    pe.wait_ge(S["rope_ready"], t)
                    for c in range(4):
                        mm = pe.transpose(bank(5, c * P, (c + 1) * P), sm[:, c * P:(c + 1) * P], ident)
                    mm.then_inc(S["qkT_mm"], 1)
                if delta:
                    pe.wait_ge(S["m2_ready"], t + 1)
                    pe.wait_ge(S["n2p_ready"], t + 1)
                    heads(bank(3), by_head(n2p), by_head(m2), "m4_mm")
                    heads(bank(1), by_head(m2), by_head(n2p), "n4_mm")
                    pe.wait_ge(S["y1_ready"], t + 1)
                    heads(bank(2), by_head(n2p), by_head(y[1]), "y2_mm")
                    pe.wait_ge(S["m4_ready"], t + 1)
                    pe.wait_ge(S["n4_ready"], t + 1)
                    heads(bank(3), by_head(mm_), by_head(n4), "n8_mm")
                    pe.wait_ge(S["y2_ready"], t + 1)
                    heads(bank(0), by_head(n4), by_head(y[0]), "y3_mm")
                if attn:
                    pe.wait_ge(S["qT_ready"], t)
                    pe.wait_ge(S["kexp_ready"], t)
                    for g in range(2):
                        keys = kexp[:, g * 1024:(g + 1) * 1024].rearrange("p (h k) -> p h k", h=8)
                        for j in range(4):
                            mm = pe.matmul(ps[32 * j:32 * j + 32, 4, g * 256:g * 256 + 256],
                                           qT[:, g * P + 32 * j:g * P + 32 * j + 32],
                                           keys[:, :, 32 * j:32 * j + 32], start=True, stop=True)
                    mm.then_inc(S["score_mm"], 1)
                if delta:
                    if not is_last(t):
                        if attn:
                            pe.wait_ge(S["kexp_ready"], t)
                        turn_norm(t + 1)
                    pe.wait_ge(S["n8_ready"], t + 1)
                    pe.wait_ge(S["y3_ready"], t + 1)
                    heads(bank(2), by_head(m2), by_head(y[1]), "y4_mm")
                if attn:
                    pe.wait_ge(S["vs_ready"], t)
                    if tail:
                        pe.wait_ge(S["logit_ready"], t - 1)
                    for j in range(4):
                        mm = pe.matmul(bank(6 + j // 2, j % 2 * D, j % 2 * D + D),
                                       con[:, C_REP + j * P:C_REP + (j + 1) * P], vs, start=True, stop=True)
                    mm.then_inc(S["vrep_mm"], 1)
                if delta:
                    pe.wait_ge(S["y4_ready"], t + 1)
                    heads(bank(1), by_parity(npm, 256, P), by_head(y[0]), "o_mm")
                    if not is_last(t):
                        if attn:
                            pe.wait_ge(S["centre"], 3 * t - 2)
                        project_delta(t + 1)
                if attn:
                    pe.wait_ge(S["prob"], 3 * t)
                    pe.wait_ge(S["vbd_ready"], t)
                    for c in range(4):
                        mm = pe.transpose(bank(7, c * P, (c + 1) * P), sm[:, c * P:(c + 1) * P], ident)
                    mm.then_inc(S["pT_mm"], 1)
                if delta:
                    pe.wait_ge(S["on_ready"], t + 1)
                    for h in range(H):
                        mm = pe.transpose(bank(3, h * P, (h + 1) * P), n2p[:, h * P:(h + 1) * P], ident)
                    mm.then_inc(S["oT_mm"], 1)
                if attn:
                    pe.wait_ge(S["pT_ready"], t)
                    pe.wait_ge(S["vbd_ready"], t)
                    for hg in range(4):
                        for j in range(4):
                            col = hg // 2 * P + 32 * j
                            mm = pe.matmul(ps[64 * (hg % 2):64 * (hg % 2) + 64, 6, col:col + 32],
                                           vbd[:, j * 256 + hg * 64:j * 256 + hg * 64 + 64],
                                           pT[:, hg * P + 32 * j:hg * P + 32 * j + 32], start=True, stop=True)
                    mm.then_inc(S["pv_mm"], 1)
                if delta:
                    pe.wait_ge(S["oT_ready"], t + 1)
                    for h in range(H):
                        mm = pe.matmul(bank(0, 0, D), n4[:, h * P:(h + 1) * P], wo_a[:, h, :],
                                       start=(h == 0), stop=(h == H - 1))
                    mm.then_inc(S["wo_mm"], 1)
            turn_norm(0)
            project_delta(0)
            run_slots(pe, slot)

            pe.wait_ge(S["logit_ready"], NT)
            pe.wait_ge(S["route"], WEIGHED)
            for t in range(NT):
                mm = pe.transpose(ps[0:E, 1 + t // 4, t % 4 * P:t % 4 * P + P], comb[:, t * E:(t + 1) * E], ident)
            mm.then_inc(S["combT_mm"], 1)
            pe.wait_ge(S["route"], CHOSEN)
            pe.matmul(bank(0, 0, 72), con[:, C_ONE:C_ONE + P], cum, start=True, stop=False, skip_group_check=True)
            pe.matmul(bank(0, 0, 64), con[:, C_UP:C_UP + P], chosen, start=False, stop=True,
                      skip_group_check=True).then_inc(S["count_mm"], 1)
            pe.wait_ge(S["combT_ready"], 1)
            for t in range(NT):
                mm = pe.matmul(bank(4 + t // 2, t % 2 * D, t % 2 * D + D), combT[:, t * P:(t + 1) * P], b2_f[:, :],
                               start=True, stop=True)
            mm.then_inc(S["b2_mm"], 1)
            for k, mapped in ((0, MAPPED0), (1, MAPPED1)):
                pe.wait_ge(S["route"], mapped)
                for t in range(NT):
                    n = k * NT + t
                    mm = pe.matmul(bank(3, 0, SLOT_TILES), onehot[k][:, t * P:(t + 1) * P],
                                   tok_col[:, n * SLOT_TILES:(n + 1) * SLOT_TILES],
                                   start=(n == 0), stop=(n == 2 * NT - 1))
            mm.then_inc(S["map_mm"], 1)

            pe.wait_ge(S["route"], ROUTED)
            pe.wait_ge(S["x1b_ready"], NT)
            pe.wait_ge(S["w1_in"], 16 * E)
            pe.wait_ge(S["w2lo_in"], 16 * (E // 2))
            pe.wait_ge(S["w2hi_in"], 16 * (E // 2))

            def turn_rows(t, u, wait_in, first):
                pe.wait_ge(S[f"slot_in{u}"], wait_in)
                if not first:
                    pe.wait_ge(S["xgT_ready"], t)
                for c in range(DC):
                    mm = pe.transpose(bank(7, c * P, (c + 1) * P), xg[u][:, c * P:(c + 1) * P], ident)
                mm.then_inc(S["xgT_mm"], 1)

            def up(t, u, e, first):
                pe.wait_ge(S["xgT_ready"], t + 1)
                if not first:
                    pe.wait_ge(S["up_ready"], t - 1)
                for n in range(2):
                    for c in range(DC):
                        mm = pe.matmul(bank(2 * u + n), xgT[u][:, c * P:(c + 1) * P],
                                       w1[:, ds(e * (DC * FF) + (c * FF + n * 512), 512)], start=(c == 0), stop=(c == DC - 1))
                mm.then_inc(S["up_mm"], 1)

            def turn_hidden(t, u, first):
                pe.wait_ge(S["up_ready"], t + 1)
                if not first:
                    pe.wait_ge(S["act_ready"], t)
                for f in range(FC):
                    mm = pe.transpose(bank(4 + f // 4, f % 4 * P, f % 4 * P + P), hs[u][:, f * P:(f + 1) * P], ident)
                mm.then_inc(S["hT_mm"], 1)

            def down(t, u, e, first):
                pe.wait_ge(S["act_ready"], t + 1)
                if not first:
                    pe.wait_ge(S["ys_ready"], t)
                for f in range(FC):
                    mm = pe.matmul(bank(6, 0, D), gT[u][:, f * P:(f + 1) * P],
                                   w2[:, ds(e * (FC * D) + f * D, D)], start=(f == 0), stop=(f == FC - 1))
                mm.then_inc(S["down_mm"], 1)

            def expert(t):
                return pe.value_load(tilee[0:1, ds(t, 1)], min_val=0, max_val=E - 1)

            turn_rows(0, 0, 16, True)
            up(0, 0, expert(0), True)
            turn_rows(1, 1, 16, False)
            turn_hidden(0, 0, True)
            up(1, 1, expert(1), True)
            turn_rows(2, 0, 32, False)
            down(0, 0, expert(0), True)
            turn_hidden(1, 1, False)
            with pe.Fori(1, SLOT_TILES // 2) as i:
                up(2 * i, 0, expert(2 * i), False)
                turn_rows(2 * i + 1, 1, 16 * i + 16, False)
                down(2 * i - 1, 1, expert(2 * i - 1), False)
                turn_hidden(2 * i, 0, False)
                up(2 * i + 1, 1, expert(2 * i + 1), False)
                turn_rows(2 * i + 2, 0, 16 * i + 32, False)
                down(2 * i, 0, expert(2 * i), False)
                turn_hidden(2 * i + 1, 1, False)
            t = SLOT_TILES - 1
            up(t, 0, expert(t), False)
            down(t - 1, 1, expert(t - 1), False)
            turn_hidden(t, 0, False)
            down(t, 0, expert(t), False)

        @block.vector
        def _(dve):
            dve.wait_ge(S["bias_in"], 16 * 9)
            for n in range(3):
                dve.wait_ge(S["wT_mm"], n + 1)
                dve.tensor_copy(tokwT[:, n * 512:(n + 1) * 512], bank(n)).then_inc(S["wT_ready"], 1)

            def stats(src, raw, mv, ve, waits):
                (a, na), (b, nb), (c, nc_) = waits
                dve.bn_stats(raw, src).then_inc(S[a], 1)
                dve.wait_ge(S[a], na)
                dve.bn_aggr(mv, raw).then_inc(S[b], 1)
                if ve is not None:
                    dve.wait_ge(S[b], nb)
                    dve.tensor_scalar(ve, mv[:, 1:2], EPS, None, ALU.add).then_inc(S[c], 1)

            def patches(half):
                dve.wait_ge(S[f"x_in{half}"], 48)
                x_split(dve.tensor_copy, half, 0).then_inc(S[f"x_split{half}"], 1)
                for q in range(0, KC, 2):
                    dve.wait_ge(S["xT_mm"], KC * half + q + 1)
                    if half and q == 0:
                        dve.wait_ge(S["x_split0"], 3)
                    dve.tensor_copy(xT_out(half, q), xT_in(half, q)).then_inc(S["xT_even_ready"], 1)

            def embed(half):
                for tt in range(4):
                    t = 4 * half + tt
                    dve.wait_ge(S["emb_mm"], t + 1)
                    dve.tensor_tensor(hres[:, t, :], bank(t % 4, 0, D), tokb, ALU.add).then_inc(S["h_ready"], 1)
                    dve.wait_ge(S["h_ready"], t + 1)
                    stats(hres[:, t, :], bst[t], mv1[:, 2 * t:2 * t + 2], None,
                          (("hstat_a", t + 1), ("hstat_b", t + 1), ("", 0)))
                a, b = 4 * half, 4 * half + 4
                dve.wait_ge(S["hstat_b"], b)
                dve.tensor_scalar(ve1[:, a:b], mv1.rearrange("p (t k) -> p t k", k=2)[:, a:b, 1], EPS, None,
                                  ALU.add).then_inc(S["hstat_ready"], 1)

            def first_norm(half):
                dve.wait_ge(S["r1_ready"], half + 1)
                for t in range(4 * half, 4 * half + 4):
                    dve.tensor_scalar(x1[:, t, :], hres[:, t, :], mv1[:, 2 * t:2 * t + 1], r1[:, t:t + 1],
                                      ALU.subtract, ALU.mult).then_inc(S["n1_ready"], 1)
            patches(0)
            dve.wait_ge(S["x_in1"], 48)
            x_split(dve.tensor_copy, 1, 0).then_inc(S["x_split1"], 1)
            embed(0)
            for q in range(0, KC, 2):
                dve.wait_ge(S["xT_mm"], KC + q + 1)
                dve.wait_ge(S["x_split0"], 3)
                dve.tensor_copy(xT_out(1, q), xT_in(1, q)).then_inc(S["xT_even_ready"], 1)
            first_norm(0)
            embed(1)
            first_norm(1)

            dve.wait_ge(S["hres_ready"], NT)

            def centred_rows(t):
                sm_ = sm.rearrange("p (h k) -> p h k", h=MH)
                dve.wait_ge(S["score_mm"], t)
                dve.tensor_tensor(sm_, bank(4).rearrange("p (h k) -> p h k", h=MH),
                                  rep(con[:, C_KEYB:C_KEYB + 32][:, None, :], [P, MH, 32]), ALU.add).then_inc(S["centre"], 1)
                dve.wait_ge(S["centre"], 3 * t - 2)
                dve.tensor_reduce(mx, sm_, AX, ALU.max).then_inc(S["centre"], 1)
                dve.wait_ge(S["centre"], 3 * t - 1)
                dve.tensor_tensor(sm_, sm_, rep(mx[:, :, None], [P, MH, 32]), ALU.subtract).then_inc(S["centre"], 1)

            def probabilities(t):
                sm_ = sm.rearrange("p (h k) -> p h k", h=MH)
                dve.wait_ge(S["exp_ready"], t)
                dve.tensor_reduce(sums, sm_, AX, ALU.add).then_inc(S["prob"], 1)
                dve.wait_ge(S["prob"], 3 * t - 2)
                dve.reciprocal(recs, sums).then_inc(S["prob"], 1)
                dve.wait_ge(S["prob"], 3 * t - 1)
                dve.tensor_tensor(sm_, sm_, rep(recs[:, :, None], [P, MH, 32]), ALU.mult).then_inc(S["prob"], 1)

            def apply_power(t, n, src, dst, b, op):
                dve.wait_ge(S[n + "_mm"], t + 1)
                dve.tensor_tensor(y[dst], y[src], bank(b), op).then_inc(S[n + "_ready"], 1)

            def qk_squares(t):
                dve.wait_ge(S["beta_act"], t + 1)
                dve.tensor_scalar(beta, th, 0.5, 0.5, ALU.mult, ALU.add).then_inc(S["beta_ready"], 1)
                dve.wait_ge(S["qk_act"], t + 1)
                dve.tensor_tensor(sq, qk, qk, ALU.mult).then_inc(S["ssq"], 1)
                dve.wait_ge(S["ssq"], 3 * t + 1)
                dve.tensor_reduce(ssq0, sq.rearrange("p (h d) -> p h d", h=8), AX, ALU.add).then_inc(S["ssq"], 1)
                dve.wait_ge(S["ssq"], 3 * t + 2)
                dve.tensor_scalar(ssq, ssq0, 1e-6, None, ALU.add).then_inc(S["ssq"], 1)

            def qkv_scaled(t):
                dve.wait_ge(S["v_act"], t + 1)
                dve.wait_ge(S["beta_ready"], t + 1)
                dve.tensor_tensor(heads4(y[0]), heads4(y[1]), rep(beta[:, :, None], [P, H, DV]),
                                  ALU.mult).then_inc(S["y0_ready"], 1)
                q, k = (qk[:, c * 256:(c + 1) * 256].rearrange("p (h d) -> p h d", h=H) for c in range(2))
                dve.wait_ge(S["rn_ready"], t + 1)
                dve.tensor_tensor(k, k, rep(rn[:, H:2 * H][:, :, None], [P, H, DK]), ALU.mult).then_inc(S["qnorm_ready"], 1)
                dve.scalar_tensor_tensor(q, q, DK ** -0.5, rep(rn[:, 0:H][:, :, None], [P, H, DK]),
                                         ALU.mult, ALU.mult).then_inc(S["knorm_ready"], 1)
                dve.wait_ge(S["qnorm_ready"], t + 1)
                dve.tensor_tensor(kb.rearrange("p (h d) -> p h d", h=H), k, rep(beta[:, :, None], [P, H, DK]),
                                  ALU.mult).then_inc(S["kb_ready"], 1)

            def slot(t, delta, attn, tail):
                if tail:
                    dve.wait_ge(S["awo_mm"], t - 1)
                    dve.wait_ge(S["n3b_ready"], t - 1)
                    dve.tensor_tensor(xa, bank(7, 0, D), n3b, ALU.add).then_inc(S["xa_ready"], 1)
                    dve.wait_ge(S["xa_ready"], t - 1)
                    dve.bn_stats(bst[1], xa).then_inc(S["xastat"], 1)
                    dve.wait_ge(S["xastat"], 3 * t - 5)
                    dve.memset(spare, 0.0)
                    dve.bn_aggr(mv4, bst[1]).then_inc(S["xastat"], 1)
                    dve.wait_ge(S["xastat"], 3 * t - 4)
                    dve.tensor_scalar(ve4, mv4[:, 1:2], EPS, None, ALU.add).then_inc(S["xastat"], 1)
                if delta:
                    dve.wait_ge(S["np_mm"], t + 1)
                    dve.tensor_tensor(npm.rearrange("p (g c) -> p g c", g=4),
                                      ps[:, 1:3, :].rearrange("p a (g c) -> p (a g) c", g=2),
                                      rep(con[:, C_NP:C_NP + 256][:, None, :], [P, 4, 256]), ALU.mult).then_inc(S["np_ready"], 1)
                    dve.wait_ge(S["m_mm"], t + 1)
                    dve.tensor_tensor(mm_.rearrange("p (a g c) -> p a g c", a=2, g=2),
                                      ps[:, 0:4:3, 0:256].rearrange("p a (g c) -> p a g c", g=2),
                                      rep(con[:, C_M:C_M + P][:, None, None, :], [P, 2, 2, P]), ALU.mult).then_inc(S["m_ready"], 1)
                if tail:
                    dve.wait_ge(S["r4_ready"], t - 1)
                    dve.tensor_scalar(x1n, xa, mv4[:, 0:1], r4, ALU.subtract, ALU.mult).then_inc(S["x1n_ready"], 1)
                if attn:
                    dve.wait_ge(S["aqk_mm"], t)
                    dve.tensor_tensor(qkb, bank(5), bqk, ALU.add).then_inc(S["qkb_ready"], 1)
                    dve.wait_ge(S["qkb_ready"], t)
                    x, z = (v.rearrange("p (h s f) -> p h s f", s=2, f=8) for v in (qkb, tb))
                    for s in range(2):
                        last = dve.tensor_tensor(z[:, :, s, :], x[:, :, 1 - s, :],
                                                 rep(con[:, C_SIN + 8 * s:C_SIN + 8 * s + 8][:, None, :], [P, 32, 8]), ALU.mult)
                    last.then_inc(S["ropeb_ready"], 1)
                if delta:
                    apply_power(t, "y1", 0, 1, 0, ALU.subtract)
                if attn:
                    dve.wait_ge(S["ropea_ready"], t)
                    dve.wait_ge(S["ropeb_ready"], t)
                    dve.tensor_tensor(sm, ta, tb, ALU.add).then_inc(S["rope_ready"], 1)
                if tail:
                    dve.wait_ge(S["x1g_ready"], t - 1)
                    dve.tensor_tensor(tile_of(x1, t - 2), x1n, be1, ALU.add).then_inc(S["x1_ready"], 1)
                    dve.wait_ge(S["gate_mm"], t - 1)
                    dve.tensor_tensor(lg[:, ds((t - 2) * E, E)], bank(7, 256, 256 + E), bg, ALU.add).then_inc(S["logit_ready"], 1)
                if attn:
                    dve.wait_ge(S["qT_ready"], t)
                    dve.tensor_tensor(kexp.rearrange("p (g h k) -> p g h k", g=2, h=8),
                                      rep(bank(5, 256, 512).rearrange("p (g k) -> p g k", g=2)[:, :, None, :], [P, 2, 8, P]),
                                      rep(con[:, C_HM:C_HM + 8][:, None, :, None], [P, 2, 8, P]),
                                      ALU.mult).then_inc(S["kexp_ready"], 1)
                if delta:
                    apply_power(t, "y2", 1, 0, 2, ALU.add)
                    apply_power(t, "y3", 0, 1, 0, ALU.add)
                if attn:
                    centred_rows(t)
                if delta:
                    apply_power(t, "y4", 1, 0, 2, ALU.add)
                if attn:
                    dve.wait_ge(S["vrep_mm"], t)
                    dve.tensor_tensor(vbd.rearrange("p (g h d) -> p g h d", h=4, d=MD),
                                      ps[:, 6:8, :].rearrange("p a (g h d) -> p (a g) h d", h=4, d=MD),
                                      rep(con[:, C_VM:C_VM + 4][:, None, :, None], [P, 16, 4, MD]),
                                      ALU.mult).then_inc(S["vbd_ready"], 1)
                    probabilities(t)
                if delta:
                    dve.wait_ge(S["oss_ready"], t + 1)
                    dve.tensor_scalar(orv, oss, 1.0 / DV, EPS, ALU.mult, ALU.add).then_inc(S["orv_ready"], 1)
                    dve.wait_ge(S["orms_ready"], t + 1)
                    dve.tensor_tensor(heads4(n2p), heads4(bank(1)), rep(orms[:, :, None], [P, H, DV]),
                                      ALU.mult).then_inc(S["on_ready"], 1)
                    if not is_last(t):
                        qk_squares(t + 1)
                        qkv_scaled(t + 1)
                    dve.wait_ge(S["wo_mm"], t + 1)
                    dve.tensor_tensor(h2, tile_of(hres, t), bank(0, 0, D), ALU.add).then_inc(S["h2s_ready"], 1)
                    dve.wait_ge(S["h2s_ready"], t + 1)
                    dve.bn_stats(bst[0], h2).then_inc(S["h2stat"], 1)
                    dve.wait_ge(S["h2stat"], 3 * t + 1)
                    dve.tensor_tensor(tile_of(hres, t), tile_of(hres, t), bank(0, 0, D), ALU.add).then_inc(S["h2_ready"], 1)
                    dve.bn_aggr(mv3, bst[0]).then_inc(S["h2stat"], 1)
                    dve.wait_ge(S["h2stat"], 3 * t + 2)
                    dve.tensor_scalar(ve3, mv3[:, 1:2], EPS, None, ALU.add).then_inc(S["h2stat"], 1)
                    dve.wait_ge(S["r3_ready"], t + 1)
                    dve.tensor_scalar(n3, h2, mv3[:, 0:1], r3, ALU.subtract, ALU.mult).then_inc(S["n3_ready"], 1)
            qk_squares(0)
            qkv_scaled(0)
            run_slots(dve, slot)

            dve.wait_ge(S["logit_ready"], NT)
            steps = [0]

            def link(ins):
                steps[0] += 1
                ins.then_inc(S["route"], 1)
                dve.wait_ge(S["route"], steps[0])

            def te(ap):
                return ap.rearrange("p (t e) -> p t e", e=E)
            link(dve.tensor_reduce(lmax, te(lg), AX, ALU.max))
            link(dve.tensor_tensor(te(lg), te(lg), rep(lmax[:, :, None], [P, NT, E]), ALU.subtract))
            dve.wait_ge(S["logit_exp"], 1)
            link(dve.tensor_reduce(lsum, te(lg), AX, ALU.add))
            link(dve.reciprocal(lsum, lsum))
            link(dve.tensor_tensor(te(prob), te(lg), rep(lsum[:, :, None], [P, NT, E]), ALU.mult))
            four = [P, NT, E, E]
            mine, other = rep(te(prob)[:, :, :, None], four), rep(te(prob)[:, :, None, :], four)
            ahead, tied = (v.rearrange("p (t e j) -> p t e j", e=E, j=E) for v in (rt8[0], rt8[1]))
            link(dve.tensor_tensor(ahead, other, mine, ALU.is_gt))
            link(dve.tensor_tensor(tied, other, mine, ALU.is_equal))
            link(dve.tensor_tensor(rt8[1].rearrange("p (t c) -> p t c", t=NT), rt8[1].rearrange("p (t c) -> p t c", t=NT),
                                   rep(con[:, C_LT:C_LT + 64][:, None, :], [P, NT, 64]), ALU.mult))
            link(dve.tensor_tensor(rt8[0], rt8[0], rt8[1], ALU.add))
            link(dve.tensor_reduce(rank, rt8[0].rearrange("p (c j) -> p c j", j=E), AX, ALU.add))
            link(dve.tensor_scalar(sel0, rank, 0.5, None, ALU.is_lt))
            link(dve.tensor_scalar(chosen, rank, 1.5, None, ALU.is_lt))
            link(dve.tensor_tensor(sel1, chosen, sel0, ALU.subtract))
            link(dve.tensor_tensor(comb, prob, chosen, ALU.mult))
            link(dve.tensor_reduce(lsum, te(comb), AX, ALU.add))
            link(dve.reciprocal(lsum, lsum))
            link(dve.tensor_tensor(te(comb), te(comb), rep(lsum[:, :, None], [P, NT, E]), ALU.mult))
            assert steps[0] == WEIGHED
            src = chosen
            for n, dst in ((E, lead0), (2 * E, lead1), (4 * E, cum[:, E:E + 64])):
                if n == E:
                    dve.memset(cum[:, 0:E], 0.0).then_inc(S["route"], 1)
                    steps[0] += 1
                dve.tensor_copy(dst[:, 0:n], src[:, 0:n]).then_inc(S["route"], 1)
                steps[0] += 1
                link(dve.tensor_tensor(dst[:, n:64], src[:, n:64], src[:, 0:64 - n], ALU.add))
                src = dst
            assert steps[0] == CHOSEN
            dve.wait_ge(S["count_mm"], 1)
            link(dve.tensor_copy(total, bank(0, 64, 72)))
            link(dve.tensor_tensor(te(pick), rep(total[:, :, None], [P, E, 8]),
                                   rep(con[:, C_TH:C_TH + 8][:, None, :], [P, E, 8]), ALU.is_gt))
            link(dve.tensor_reduce(tiles, te(pick), AX, ALU.add))
            link(dve.tensor_tensor(te(pick), rep(tiles[:, None, :], [P, E, E]), te(con[:, C_LT:C_LT + 64]), ALU.mult))
            link(dve.tensor_reduce(begin, te(pick), AX, ALU.add))
            link(dve.scalar_tensor_tensor(te(place), rep(begin[:, None, :], [P, NT, E]), float(P),
                                          te(bank(0, 0, 64)), ALU.mult, ALU.add))
            for s, sel in enumerate((sel0, sel1)):
                link(dve.tensor_tensor(pick, place, sel, ALU.mult))
                link(dve.tensor_reduce(slots[:, s * NT:(s + 1) * NT], te(pick), AX, ALU.add))
            by_tile = [P, 2 * NT, SLOT_TILES]
            grid, cols_ = (v.rearrange("p (c j) -> p c j", j=SLOT_TILES) for v in (tile_ends, tok_col))
            link(dve.tensor_tensor(grid, rep(slots[:, :, None], by_tile),
                                   rep(con[:, C_SE:C_SE + SLOT_TILES][:, None, :], by_tile), ALU.is_ge))
            link(dve.tensor_reduce(slot_tile, grid, AX, ALU.add))
            link(dve.scalar_tensor_tensor(in_tile, slot_tile, -float(P), slots, ALU.mult, ALU.add))
            link(dve.tensor_tensor(cols_, rep(slot_tile[:, :, None], by_tile),
                                   rep(con[:, C_SL:C_SL + SLOT_TILES][:, None, :], by_tile), ALU.is_equal))
            for k in range(2):
                half = cols_[:, k * NT:(k + 1) * NT, :]
                link(dve.tensor_tensor(half, half, rep(con[:, C_TOK:C_TOK + NT][:, :, None], [P, NT, SLOT_TILES]),
                                       ALU.mult))
            link(dve.tensor_tensor(end, begin, tiles, ALU.add))
            ends = tile_ends[:, 0:SLOT_TILES * E].rearrange("p (j e) -> p j e", e=E)
            link(dve.tensor_tensor(ends, rep(end[:, None, :], [P, SLOT_TILES, E]),
                                   rep(con[:, C_SL:C_SL + SLOT_TILES][:, :, None], [P, SLOT_TILES, E]), ALU.is_le))
            link(dve.tensor_reduce(owner, ends, AX, ALU.add))
            for k, mapped in ((0, MAPPED0), (1, MAPPED1)):
                dve.tensor_tensor(onehot[k].rearrange("p (t s) -> p t s", s=P),
                                  rep(in_tile[:, k * NT:(k + 1) * NT][:, :, None], [P, NT, P]),
                                  rep(con[:, C_IO:C_IO + P][:, None, :], [P, NT, P]), ALU.is_equal).then_inc(S["route"], 1)
                steps[0] += 1
                assert steps[0] == mapped, steps
            dve.tensor_scalar(tilee[:, :], owner, float(E - 1), None, ALU.min)
            dve.wait_ge(S["map_mm"], 1)
            link(dve.tensor_copy(slot_tok[:, :], bank(3, 0, SLOT_TILES)))
            assert steps[0] == ROUTED
            dve.tensor_copy(posi[:, :], slots).then_inc(S["route"], 1)
            steps[0] += 1
            for s, sel in enumerate((sel0, sel1)):
                link(dve.tensor_tensor(pick, comb, sel, ALU.mult))
                link(dve.tensor_reduce(wsel[:, s * NT:(s + 1) * NT], te(pick), AX, ALU.add))

            dve.wait_ge(S["b2_mm"], 1)
            dve.wait_ge(S["x1_out"], 16 * NT)
            for t in range(NT):
                dve.tensor_tensor(x1[:, t, :], x1[:, t, :], bank(4 + t // 2, t % 2 * D, t % 2 * D + D),
                                  ALU.add).then_inc(S["x1b_ready"], 1)

            def rows_out(t, u):
                dve.wait_ge(S["xgT_mm"], t + 1)
                dve.tensor_copy(xgT[u][:, :], bank(7, 0, D)).then_inc(S["xgT_ready"], 1)

            def hidden_out(t, u):
                dve.wait_ge(S["up_mm"], t + 1)
                dve.tensor_copy(hs[u], ps[:, 2 * u:2 * u + 2, :].rearrange("p a b -> p (a b)")).then_inc(S["up_ready"], 1)

            def output_out(t, u, y_sent):
                dve.wait_ge(S["down_mm"], t + 1)
                if y_sent is not None:
                    dve.wait_ge(S[f"y_out{u}"], y_sent)
                dve.tensor_copy(ys[u], bank(6, 0, D)).then_inc(S["ys_ready"], 1)
            rows_out(0, 0)
            hidden_out(0, 0)
            rows_out(1, 1)
            hidden_out(1, 1)
            rows_out(2, 0)
            output_out(0, 0, None)
            hidden_out(2, 0)
            rows_out(3, 1)
            output_out(1, 1, None)
            hidden_out(3, 1)
            rows_out(4, 0)
            output_out(2, 0, 16)
            with dve.Fori(2, SLOT_TILES // 2) as i:
                hidden_out(2 * i, 0)
                rows_out(2 * i + 1, 1)
                output_out(2 * i - 1, 1, 16 * i - 16)
                hidden_out(2 * i + 1, 1)
                rows_out(2 * i + 2, 0)
                output_out(2 * i, 0, 16 * i)
            t = SLOT_TILES - 1
            hidden_out(t, 0)
            output_out(t - 1, 1, 16 * (t // 2 - 1))
            output_out(t, 0, 16 * (t // 2))

            n = [0]

            def step(ins):
                n[0] += 1
                ins.then_inc(S["tail"], 1)
                return n[0]

            def combine(t, k):
                return step(dve.scalar_tensor_tensor(x1[:, t, :], yg[:, k, t, :], wsel[:, k * NT + t:k * NT + t + 1],
                                                     x1[:, t, :], ALU.mult, ALU.add))
            for t in range(NT + 2):
                o = t - 2
                if t < NT:
                    dve.wait_ge(gathered[t], 32)
                    new = combine(t, 0)
                if o >= 0:
                    dve.wait_ge(S["r5_ready"], o + 1)
                    old = step(dve.tensor_scalar(x1[:, o, :], x1[:, o, :], mv5[:, 2 * o:2 * o + 1], r5[:, o:o + 1],
                                                 ALU.subtract, ALU.mult))
                if t < NT:
                    dve.wait_ge(S["tail"], new)
                    new = combine(t, 1)
                if o >= 0:
                    dve.wait_ge(S["tail"], old)
                    old = step(dve.tensor_tensor(x1[:, o, :], x1[:, o, :], g2, ALU.mult))
                if t < NT:
                    dve.wait_ge(S["tail"], new)
                    new = step(dve.bn_stats(bst[t], x1[:, t, :]))
                if o >= 0:
                    dve.wait_ge(S["tail"], old)
                    dve.wait_ge(S["hb_ready"], o + 1)
                    dve.tensor_tensor(fin[:, o, :], x1[:, o, :], hres[:, o, :], ALU.add).then_inc(S["fin_ready"], 1)
                if t < NT:
                    dve.wait_ge(S["tail"], new)
                    new = step(dve.bn_aggr(mv5[:, 2 * t:2 * t + 2], bst[t]))
                    dve.wait_ge(S["tail"], new)
                    dve.tensor_scalar(ve5[:, t:t + 1], mv5[:, 2 * t + 1:2 * t + 2], EPS, None,
                                      ALU.add).then_inc(S["ve5_ready"], 1)


INPUTS = ["x", "L0_tok_W", "L0_tok_b", "L0_attn_ln_w", "L0_attn_ln_b", "L0_attn_Wq", "L0_attn_Wk", "L0_attn_Wv",
          "L0_attn_Wb", "L0_attn_o_norm_w", "L0_attn_Wo", "L0_ffn_Wq", "L0_ffn_bq", "L0_ffn_Wk", "L0_ffn_bk",
          "L0_ffn_Wv", "L0_ffn_bv", "L0_ffn_Wo", "L0_ffn_bo", "L0_ffn_Wg", "L0_ffn_bg", "L0_ffn_W1", "L0_ffn_b1",
          "L0_ffn_W2", "L0_ffn_b2", "L0_ffn_g1", "L0_ffn_be1", "L0_ffn_g2", "L0_ffn_be2"]


def kernel(**inputs):
    import concourse.bacc as bacc
    from concourse.bass_utils import run_bass_kernel_spmd

    nc = bacc.Bacc("TRN2", target_bir_lowering=False, num_devices=1)
    arrays = {"in_" + name: np.ascontiguousarray(inputs[name]) for name in INPUTS}
    arrays["in_consts"] = constants()
    aps = {name[3:]: nc.dram_tensor(name, a.shape, F32, kind="ExternalInput").ap() for name, a in arrays.items()}
    out = nc.dram_tensor("out", (TOK, D), F32, kind="ExternalOutput").ap()
    tower(nc, aps, out)
    result = run_bass_kernel_spmd(nc, [arrays], core_ids=[0])
    return result.results[0]["out"].reshape(IMGS, SEQ, D)
```

```python
from contextlib import ExitStack

import numpy as np

import concourse.bass as bass
from concourse import mybir

F32 = mybir.dt.float32
F16 = mybir.dt.float16
I32 = mybir.dt.int32
ALU = mybir.AluOpType
ACT = mybir.ActivationFunctionType
AX = mybir.AxisListType.X
ds = bass.ds

P = 128
D = 256
DC = D // P
IMGS, SEQ = 64, 16
TOK = IMGS * SEQ
NT = TOK // P
KP = 768
KC = KP // P
H, DK, DV = 4, 64, 128
MH, MD = 16, 16
E, FF = 8, 1024
FC = FF // P
SLOT_TILES = 2 * TOK // P + E - 1
W = 64
EPS = 1e-5
RANKED = 12
CHOSEN, WEIGHED, MAPPED0, MAPPED1, ROUTED, WEIGHTS = 31, 36, 52, 53, 60, 68

C_ID = 0
C_NP = C_ID + P
C_MF = C_NP + 2 * W
C_COS = C_MF + P
C_SIN = C_COS + 8
C_KEYB = C_SIN + 16
C_HM = C_KEYB + 32
C_G = C_HM + 8
C_UP = C_G + P // W
C_ONE = C_UP + P
C_LT = C_ONE + P
C_TH = C_LT + 64
C_SL = C_TH + 8
C_SE = C_SL + SLOT_TILES
C_CHO = C_SE + SLOT_TILES
C_IO = C_CHO + 2 * NT
C_FREE = C_IO + P
C_END = C_FREE + SLOT_TILES


def constants():
    c = np.zeros((P, C_END), np.float32)
    p = np.arange(P)
    same = p[:, None] // SEQ == p[None, :] // SEQ
    c[:, C_ID:C_ID + P] = np.eye(P)
    q, r = p[:, None] % W, np.arange(W)[None, :]
    near = q // SEQ == r // SEQ
    c[:, C_NP:C_NP + W] = near & (q < r)
    c[:, C_NP + W:C_NP + 2 * W] = near & (q <= r)
    c[:, C_G:C_G + P // W] = p[:, None] // W == np.arange(P // W)[None, :]
    c[:, C_MF:C_MF + P] = same & (p[None, :] < p[:, None])
    freq = 1.0 / 10000.0 ** (np.arange(0, MD, 2, dtype=np.float32) / MD)
    ang = (p % SEQ).astype(np.float32)[:, None] * freq[None, :].astype(np.float32)
    c[:, C_COS:C_COS + 8] = np.cos(ang)
    c[:, C_SIN:C_SIN + 16] = np.concatenate([-np.sin(ang), np.sin(ang)], axis=1)
    key = np.arange(32)
    c[:, C_KEYB:C_KEYB + 32] = np.where(p[:, None] % 32 // SEQ == key[None, :] // SEQ, 0.0, -1e30)
    c[:, C_HM:C_HM + 8] = p[:, None] // MD == np.arange(8)[None, :]
    c[:, C_UP:C_UP + P] = p[:, None] < p[None, :]
    c[:, C_ONE:C_ONE + P] = 1.0
    e = np.arange(E)
    c[:, C_LT:C_LT + 64] = (e[None, :] < e[:, None]).astype(np.float32).reshape(1, 64)
    c[:, C_TH:C_TH + 8] = P * np.arange(8)
    c[:, C_SL:C_SL + SLOT_TILES] = np.arange(SLOT_TILES)
    c[:, C_SE:C_SE + SLOT_TILES] = P * np.arange(1, SLOT_TILES + 1)
    c[:, C_CHO:C_CHO + 2 * NT] = 1 + P * np.arange(2 * NT)[None, :] + p[:, None]
    c[:, C_FREE:C_FREE + SLOT_TILES] = 1 + 2 * TOK + P * np.arange(SLOT_TILES)[None, :] + p[:, None]
    c[:, C_IO:C_IO + P] = np.arange(P)
    return c


SEMS = """
x_in0 x_in1 const_in routing_const_in tokw_in rows_in bias_in attnw_in ffnw_in w1_in w2lo_in w2hi_in
exponents_set
wT_mm xT_even_ready wT_ready x_split0 x_split1 xT_mm xT_ready emb_mm h_ready hstat_raw hstat_mv hstat_ready r1_ready rt_ready
r2_ready n1_ready hres_ready rows_mm cols_ready
n2_ready n2_mm n2T_ready beta_mm qk_mm v_mm beta_act qk_act v_act beta_ready ssq
rn_ready qnorm_ready knorm_ready kb_ready y0_ready kqT_mm kT_mm kqT_ready kT_ready np_mm m_mm npc_ready m_ready
nx1_mm n2f_ready m2_mm m2_ready nx2_mm n4f_ready m4_mm m4_ready nx3_mm n8f_ready m8_mm m8_ready x4_mm x4_ready xf_ready o_mm oss_ready orv_ready orms_ready on_ready oT_mm oT_ready wo_mm h2_ready h2s_ready
h2stat r3_ready exp_table silu_table
n3_ready n3b_ready n3_mm n3T_ready aqk_mm av_mm vs_ready vbd_zero qkb_ready ropea_ready ropeb_ready rope_ready
vbd_in qkT_mm qT_ready kexp_ready score_mm centre exp_ready prob
pT_mm pT_ready pv_mm aoT_ready awo_mm xa_ready xastat r4_ready
x1n_ready x1g_ready x1_ready x1T_mm x1T_ready gate_mm logit_ready
route logit_exp count_mm combT_mm combT_ready b2_mm x1b_ready x1_out map_mm hb_ready
slot_in0 slot_in1 xgT_mm xgT_ready w1_staged hT_mm act_ready down_mm ys_ready y_out0 y_out1 diag_ready combined_mm
tail ve5_ready r5_ready fin_ready out_done
""".split()


def tower(nc, A, out):
    with ExitStack() as ctx:
        def sb(name, shape, dt=F32):
            return ctx.enter_context(nc.sbuf_tensor(name, shape, dt))

        S = {name: ctx.enter_context(nc.semaphore(name)) for name in SEMS}

        w1 = sb("w1", [P, E * DC * FF])
        w2 = sb("w2", [P, E * FC * D])
        XL = KC * 512
        x_raw = [w2[:, k * XL:(k + 1) * XL] for k in range(2)]
        x_tok = [w2[:, (2 + k) * XL:(3 + k) * XL] for k in range(2)]
        xT = [w2[:, 4 * XL:5 * XL], w2[:, 0:XL]]
        con = sb("con", [P, C_END])
        hres = sb("hres", [P, NT, D])
        x1 = sb("x1", [P, NT, D])
        cols = sb("cols", [P, 76])
        misc = sb("misc", [P, 400])
        wqk_a = sb("wqk_a", [P, DC, 512])
        wv_a = sb("wv_a", [P, DC, 512])
        wb_a = sb("wb_a", [P, DC, H])
        wo_a = sb("wo_a", [P, H, D])
        wqk_f = sb("wqk_f", [P, DC, 512])
        wv_f = sb("wv_f", [P, DC, D])
        wo_f = sb("wo_f", [P, DC, D])
        wg_f = sb("wg_f", [P, DC, E])
        b2_f = sb("b2_f", [E, D])
        bc = sb("bc", [P, 8 * D + E])
        tokb, bqk, bo = bc[:, 0:D], bc[:, D:3 * D], bc[:, 3 * D:4 * D]
        g1, be1, g2, be2 = (bc[:, (4 + k) * D:(5 + k) * D] for k in range(4))
        bg = bc[:, 8 * D:8 * D + E]

        work = sb("work", [P, 5200])
        nx1 = sb("nx1", [P, 512])
        sq = sb("sq", [P, 2 * D])[:, :]
        xg = [sq[:, u * D:(u + 1) * D] for u in range(2)]
        xgT_all = sb("xgT", [P, 2 * D])[:, :]
        xgT = [xgT_all[:, u * D:(u + 1) * D] for u in range(2)]
        tokw = work[:, 0:2 * KP]
        tokwT = work[:, 2 * KP:4 * KP]
        rows = work[0:76, 4 * KP:4 * KP + P]
        ident = con[:, C_ID:C_ID + P]

        def m(a, n):
            return misc[:, a:a + n]
        mv1, ve1, r1, rt, r2 = m(0, 16), m(16, 8), m(24, 8), m(32, 8), m(40, 8)
        mv3, ve3, r3 = m(48, 2), m(50, 1), m(51, 1)
        mv4, ve4, r4 = m(80, 2), m(82, 1), m(83, 1)
        mv5, ve5, r5 = m(112, 16), m(128, 8), m(136, 8)
        negh = m(144, 8)
        bst = [m(152 + 6 * k, 6) for k in range(8)]
        th, beta, oss, orv, orms = (m(200 + 4 * k, 4) for k in range(5))
        ssq0, ssq, rn = (m(220 + 8 * k, 8) for k in range(3))
        mx, sums, recs = (m(244 + 16 * k, 16) for k in range(3))
        spare, spare_in, spare_exp, spare_silu = (m(292 + k, 1) for k in range(4))

        LNW, LNB, ONW, BV, G1, BE1, B1 = 0, 2, 4, 5, 7, 9, 11
        ps = ctx.enter_context(nc.psum_tensor("ps", [P, 8, 512], F32))

        def bank(n, a=0, b=512):
            return ps[:, n, a:b]

        x1_dram = nc.dram_tensor("mixture_x", [TOK, D], F32, kind="Internal").ap()
        y_dram = nc.dram_tensor("choices_y", [2 * TOK + SLOT_TILES * P, D], F32, kind="Internal").ap()

        hi = w2[:, E * FC * D // 2:]
        kqT = hi[:, 0:512]
        y = [hi[:, 512:1024], hi[:, 1024:1536]]
        qk = hi[:, 1536:2048]
        xf = oT = hi[:, 2048:2560]
        nx = [hi[:, 2560:3072], nx1[:, :]]
        mf = m4f = hi[:, 3072:3584]
        m2f = m8f = junk = hi[:, 3584:4096]
        n2f = n8f = on = hi[:, 4096:4608]
        n4f = hi[:, 4608:5120]
        kexp = hi[:, 5120:7168]
        vbd = hi[:, 7168:8192]
        n2, n2T, h2 = (work[:, k * D:(k + 1) * D] for k in range(3))
        n3, n3b, n3T, vs, qT, aoT, xa, x1n = (work[:, (3 + k) * D:(4 + k) * D] for k in range(8))
        qkb, ta, sm, pT = (work[:, 11 * D + k * 512:11 * D + (k + 1) * 512] for k in range(4))
        tb, x1T = pT, work[:, 11 * D + 2048:12 * D + 2048]
        lg = sb("lg", [P, NT * E])
        prob, rank, sel0, sel1, chosen, comb = (nx1[:, 64 * k:64 * k + 64] for k in range(6))
        lmax, lsum = nx1[:, 384:384 + NT], nx1[:, 384 + NT:384 + 2 * NT]
        ahead, tied = sq, xgT_all
        o = 0
        small = []
        for _ in range(8):
            small.append(work[:, o:o + 72])
            o += 72
        combT = work[0:E, o:o + 2 * 512]
        o += 1024
        tile_ends = work[:, o:o + 2 * NT * SLOT_TILES]
        o += 2 * NT * SLOT_TILES
        choice_col = work[:, o:o + NT * SLOT_TILES].bitcast(F16)
        o += NT * SLOT_TILES
        onehot = [work[:, o + k * NT * P // 2:o + (k + 1) * NT * P // 2].bitcast(F16) for k in range(2)]
        cum, pick, place = small[0], small[1][:, 0:64], small[2][:, 0:64]
        total, tiles, begin, end = (small[3][:, 8 * k:8 * k + 8] for k in range(4))
        slots, slot_tile, in_tile = (small[4][:, 16 * k:16 * k + 16] for k in range(3))
        lead0, lead1, owner = small[5][:, 0:64], small[6][:, 0:64], small[7][:, 0:SLOT_TILES]
        choice, second = small[5][:, 0:SLOT_TILES], small[6][:, 0:SLOT_TILES]
        kb, kT = xgT
        weight_diag = [[wqk_f[:, :, :].rearrange("p c n -> p (c n)")],
                       [v[:, :, :].rearrange("p c n -> p (c n)") for v in (wv_f, wo_f)]]
        w1_stage = [[v.rearrange("p c n -> p (c n)") for v in (wqk_a[:, :, :], wv_a[:, :, :])],
                    [work[:, c * FF:(c + 1) * FF] for c in range(DC)]]
        gT = [work[:, (2 + u) * FF:(3 + u) * FF] for u in range(2)]
        ys = [work[:, 4 * FF + u * D:4 * FF + (u + 1) * D] for u in range(2)]
        tilee = sb("tilee", [P, SLOT_TILES], I32)
        slot_tok = sb("slot_tok", [P, SLOT_TILES], I32)
        slot_row = sb("slot_row", [P, SLOT_TILES], I32)
        wsel = m(304, 2 * NT)
        yg = w1[:, 0:2 * NT * D].rearrange("p (k t d) -> p k t d", k=2, t=NT)
        fin = w1[:, 2 * NT * D:3 * NT * D].rearrange("p (t d) -> p t d", t=NT)

        def diag_of(k, t):
            part, column = divmod(t, NT // len(weight_diag[k]))
            return weight_diag[k][part][:, column * P:(column + 1) * P]

        choices_in = [ctx.enter_context(nc.semaphore(f"choices_in{t}")) for t in range(NT)]

        def x_split(copy, half, c):
            src = x_raw[half][:, c * 1024:(c + 1) * 1024].rearrange("p (r w j) -> p r w j", r=16, w=4)
            dst = x_tok[half].rearrange("p (w c r j) -> p c r w j", w=4, c=3, r=16)[:, c]
            return copy(dst, src)

        def xT_in(half, q):
            return bank(4 + (KC * half + q) % 3).rearrange("p (w b) -> p w b", w=4)

        def xT_out(half, q):
            return xT[half][:, q * 512:(q + 1) * 512].rearrange("p (b w) -> p w b", w=4)

        def tile_of(buf, t):
            return buf[:, ds(t, 1), :].rearrange("p a d -> p (a d)")

        def eights(ap):
            return ap.rearrange("p (h f) -> p h f", f=8)

        def heads4(ap):
            return ap.rearrange("p (h d) -> p h d", h=H)

        def rep(ap, shape):
            return ap.broadcast_to(shape)

        def packed(ap):
            return ap.rearrange("p (h c) -> p h c", h=H)

        def is_first(t):
            return isinstance(t, int) and t == 0

        def is_last(t):
            return isinstance(t, int) and t == NT - 1

        def run_slots(eng, slot):
            slot(0, True, False, False)
            slot(1, True, True, False)
            with eng.Fori(2, NT - 1) as t:
                slot(t, True, True, True)
            slot(NT - 1, True, True, True)
            slot(NT, False, True, True)
            slot(NT + 1, False, False, True)

        block = ctx.enter_context(nc.Block())

        @block.sync
        def _(sp):
            def patches_in(half):
                for c in range(3):
                    src = A["x"][32 * half:32 * half + 32, c].rearrange("b (h r) w -> b h (r w)", r=16)
                    sp.dma_start(x_raw[half][:, c * 1024:(c + 1) * 1024], src).then_inc(S[f"x_in{half}"], 16)
            sp.dma_start(con[:, 0:C_UP], A["consts"][:, 0:C_UP]).then_inc(S["const_in"], 16)
            patches_in(0)
            sp.dma_start(tokw.rearrange("p (c k) -> p c k", c=DC),
                         A["L0_tok_W"].rearrange("(c p) k -> p c k", p=P)).then_inc(S["tokw_in"], 16)
            patches_in(1)
            r = 0
            for name, n in (("L0_attn_ln_w", 2), ("L0_attn_ln_b", 2), ("L0_attn_o_norm_w", 1), ("L0_ffn_bv", 2),
                            ("L0_ffn_g1", 2), ("L0_ffn_be1", 2)):
                sp.dma_start(rows[r:r + n, :], A[name].rearrange("(c p) -> c p", p=P)).then_inc(S["rows_in"], 16)
                r += n
            sp.dma_start(rows[r:r + E * FC, :],
                         A["L0_ffn_b1"].rearrange("e (c p) -> (e c) p", p=P)).then_inc(S["rows_in"], 16)
            for dst, name in ((tokb, "L0_tok_b"), (bqk[:, 0:D], "L0_ffn_bq"), (bqk[:, D:2 * D], "L0_ffn_bk"),
                              (bo, "L0_ffn_bo"), (g1, "L0_ffn_g1"), (be1, "L0_ffn_be1"), (g2, "L0_ffn_g2"),
                              (be2, "L0_ffn_be2"), (bg, "L0_ffn_bg")):
                sp.dma_start(dst, A[name].partition_broadcast(P)).then_inc(S["bias_in"], 16)
            for dst, name in ((wqk_a[:, :, 0:256], "L0_attn_Wq"), (wqk_a[:, :, 256:512], "L0_attn_Wk"),
                              (wv_a[:, :, :], "L0_attn_Wv"), (wb_a[:, :, :], "L0_attn_Wb"),
                              (wo_a[:, :, :], "L0_attn_Wo")):
                sp.dma_start(dst, A[name].rearrange("(c p) n -> p c n", p=P)).then_inc(S["attnw_in"], 16)
            for dst, name in ((wqk_f[:, :, 0:256], "L0_ffn_Wq"), (wqk_f[:, :, 256:512], "L0_ffn_Wk"),
                              (wv_f[:, :, :], "L0_ffn_Wv"), (wo_f[:, :, :], "L0_ffn_Wo"),
                              (wg_f[:, :, :], "L0_ffn_Wg")):
                sp.dma_start(dst, A[name].rearrange("(c p) n -> p c n", p=P)).then_inc(S["ffnw_in"], 16)
            sp.dma_start(b2_f[:, :], A["L0_ffn_b2"]).then_inc(S["ffnw_in"], 16)
            for e in range(E):
                sp.dma_start(w1[:, e * DC * FF:(e + 1) * DC * FF].rearrange("p (c f) -> p c f", c=DC),
                             A["L0_ffn_W1"][e].rearrange("(c p) f -> p c f", p=P)).then_inc(S["w1_in"], 16)

            sp.dma_start(con[:, C_UP:], A["consts"][:, C_UP:]).then_inc(S["routing_const_in"], 16)

            def w2_load(e, sem):
                sp.dma_start(w2[:, e * FC * D:(e + 1) * FC * D].rearrange("p (c d) -> p c d", c=FC),
                             A["L0_ffn_W2"][e].rearrange("(c p) d -> p c d", p=P)).then_inc(S[sem], 16)
            sp.wait_ge(S["emb_mm"], NT)
            for e in range(E // 2):
                w2_load(e, "w2lo_in")
            sp.wait_ge(S["vbd_zero"], 1)

            def slot(t, delta, attn, tail):
                if attn:
                    sp.wait_ge(S["vs_ready"], t)
                    for r in range(4):
                        for j in range(4):
                            sp.dma_start(
                                vbd[32 * r:32 * r + 32, j * D:(j + 1) * D].rearrange("p (g h d) -> p g h d", g=4, h=4)[:, :, r, :],
                                vs[32 * j:32 * j + 32, :].rearrange("p (g h d) -> p g h d", g=4, h=4)[:, :, r, :]
                            ).then_inc(S["vbd_in"], 16)
                if tail and not (isinstance(t, int) and t == NT + 1):
                    sp.wait_ge(S["x1_ready"], t - 1)
                    sp.dma_start(x1_dram[ds((t - 2) * P, P), :], tile_of(x1, t - 2)).then_inc(S["x1_out"], 16)
            run_slots(sp, slot)
            sp.wait_ge(S["awo_mm"], NT)
            for e in range(E // 2, E):
                w2_load(e, "w2hi_in")

            sp.wait_ge(S["y_out0"], 16 * (SLOT_TILES // 2 + 1))
            sp.wait_ge(S["y_out1"], 16 * (SLOT_TILES // 2))
            for t in range(NT):
                sp.dma_start(yg[:, :, t, :], y_dram[0:2 * TOK, :].rearrange("(k t p) d -> p k t d", k=2, t=NT)[:, :, t, :]
                             ).then_inc(choices_in[t], 16)
            for t in range(NT):
                sp.wait_ge(S["fin_ready"], t + 1)
                sp.dma_start(out[t * P:(t + 1) * P, :], fin[:, t, :]).then_inc(S["out_done"], 16)
            sp.wait_ge(S["out_done"], 16 * NT)

        @block.gpsimd
        def _(pool):
            pool.memset(negh, -0.5).then_inc(S["exponents_set"], 1)
            pool.memset(spare_in, 0.0).then_inc(S["exponents_set"], 1)
            pool.memset(vbd, 0.0).then_inc(S["vbd_zero"], 1)
            pool.wait_ge(S["exponents_set"], 2)

            def inv_root(dst, src, n, sem):
                pool.tensor_tensor(dst, src, negh[:, 0:n], ALU.pow).then_inc(S[sem], 1)

            def hres_rows(half):
                for t in range(4 * half, 4 * half + 4):
                    pool.wait_ge(S["n1_ready"], t + 1)
                    pool.tensor_tensor(hres[:, t, :], hres[:, t, :], x1[:, t, :], ALU.add).then_inc(S["hres_ready"], 1)

            for half in range(2):
                a, b = 4 * half, 4 * half + 4
                pool.wait_ge(S["hstat_ready"], half + 1)
                inv_root(r1[:, a:b], ve1[:, a:b], 4, "r1_ready")
                var = mv1.rearrange("p (t k) -> p t k", k=2)[:, a:b, 1]
                pool.wait_ge(S["r1_ready"], half + 1)
                pool.tensor_tensor(rt[:, a:b], var, r1[:, a:b], ALU.mult).then_inc(S["rt_ready"], 1)
                pool.wait_ge(S["rt_ready"], 3 * half + 1)
                pool.tensor_tensor(rt[:, a:b], rt[:, a:b], r1[:, a:b], ALU.mult).then_inc(S["rt_ready"], 1)
                pool.wait_ge(S["rt_ready"], 3 * half + 2)
                pool.tensor_scalar(rt[:, a:b], rt[:, a:b], EPS, None, ALU.add).then_inc(S["rt_ready"], 1)
                pool.wait_ge(S["rt_ready"], 3 * half + 3)
                inv_root(r2[:, a:b], rt[:, a:b], 4, "r2_ready")
                pool.wait_ge(S["r2_ready"], half + 1)
                if half == 0:
                    pool.wait_ge(S["n1_ready"], 1)
                    pool.wait_ge(S["wT_mm"], 3)
                    pool.tensor_tensor(n2, x1[:, 0, :], rep(r2[:, 0:1], [P, D]), ALU.mult).then_inc(S["n2_ready"], 1)
                    hres_rows(0)

            def next_norm(t):
                pool.wait_ge(S["n2_mm"], t)
                pool.tensor_tensor(n2, tile_of(x1, t), rep(r2[:, ds(t, 1)], [P, D]), ALU.mult).then_inc(S["n2_ready"], 1)

            def qk_root(t):
                pool.wait_ge(S["ssq"], 3 * t + 3)
                inv_root(rn, ssq, 8, "rn_ready")

            def slot(t, delta, attn, tail):
                nxt = delta and not is_last(t)
                if nxt:
                    next_norm(t + 1)
                if attn:
                    pool.wait_ge(S["h2stat"], 3 * t)
                    inv_root(r3, ve3, 1, "r3_ready")
                    if tail:
                        pool.wait_ge(S["xa_ready"], t - 1)
                    pool.wait_ge(S["n3_ready"], t)
                    pool.tensor_tensor(n3b, n3, bo, ALU.add).then_inc(S["n3b_ready"], 1)
                if tail:
                    pool.wait_ge(S["xastat"], 3 * t - 3)
                    inv_root(r4, ve4, 1, "r4_ready")
                if attn:
                    pool.wait_ge(S["qkb_ready"], t)
                    pool.tensor_tensor(eights(ta), eights(qkb), rep(con[:, C_COS:C_COS + 8][:, None, :], [P, 64, 8]),
                                       ALU.mult).then_inc(S["ropea_ready"], 1)
                if tail:
                    pool.wait_ge(S["x1T_mm"], t - 1)
                    pool.tensor_tensor(x1n, x1n, g1, ALU.mult).then_inc(S["x1g_ready"], 1)
                if nxt:
                    qk_root(t + 1)
                if delta:
                    pool.wait_ge(S["orv_ready"], t + 1)
                    inv_root(orms, orv, 4, "orms_ready")
            qk_root(0)
            hres_rows(1)
            pool.wait_ge(S["bias_in"], 16 * 9)
            run_slots(pool, slot)

            pool.wait_ge(S["h2_ready"], NT)
            for t in range(NT):
                pool.tensor_tensor(hres[:, t, :], hres[:, t, :], be2, ALU.add).then_inc(S["hb_ready"], 1)

            def dispatch(t):
                if t >= 2:
                    pool.wait_ge(S["xgT_mm"], t - 1)
                pool.indirect_dma_start(
                    out=xg[t % 2], out_offset=None, in_=x1_dram,
                    in_offset=bass.IndirectOffsetOnAxis(slot_tok[:, t:t + 1], 0)).then_inc(S[f"slot_in{t % 2}"], 16)

            def give_back(t):
                pool.wait_ge(S["ys_ready"], t + 1)
                pool.indirect_dma_start(
                    out=y_dram, out_offset=bass.IndirectOffsetOnAxis(slot_row[:, t:t + 1], 0), in_=ys[t % 2],
                    in_offset=None).then_inc(S[f"y_out{t % 2}"], 16)
            pool.wait_ge(S["x1_out"], 16 * NT)
            pool.wait_ge(S["route"], ROUTED)
            for t in range(SLOT_TILES):
                dispatch(t)
                if t == 4:
                    pool.wait_ge(S["route"], WEIGHTS)
                    for k in range(2):
                        n = NT // len(weight_diag[k])
                        for part, dst in enumerate(weight_diag[k]):
                            a = k * NT + part * n
                            pool.tensor_tensor(dst.rearrange("p (t j) -> p t j", t=n), rep(ident[:, None, :], [P, n, P]),
                                               rep(wsel[:, a:a + n][:, :, None], [P, n, P]), ALU.mult).then_inc(S["diag_ready"], 1)
                if t >= 4:
                    give_back(t - 4)
            for t in range(SLOT_TILES - 4, SLOT_TILES):
                give_back(t)

            for t in range(NT):
                pool.wait_ge(S["ve5_ready"], t + 1)
                inv_root(r5[:, t:t + 1], ve5[:, t:t + 1], 1, "r5_ready")

        @block.scalar
        def _(act):
            for half in range(2):
                act.wait_ge(S[f"x_in{half}"], 48)
                x_split(act.copy, half, 1).then_inc(S[f"x_split{half}"], 1)
                for q in range(1, KC, 2):
                    act.wait_ge(S["xT_mm"], KC * half + q + 1)
                    act.copy(xT_out(half, q), xT_in(half, q)).then_inc(S["xT_ready"], 1)
            act.wait_ge(S["rows_mm"], 1)
            act.copy(cols[:, 0:75], bank(7, 0, 75)).then_inc(S["cols_ready"], 1)
            act.wait_ge(S["cols_ready"], 1)

            def turned_norm(t):
                act.wait_ge(S["n2_mm"], t + 1)
                for c in range(DC):
                    last = act.activation(n2T[:, c * P:(c + 1) * P], bank(0, c * P, (c + 1) * P), ACT.Identity,
                                          bias=cols[:, LNB + c:LNB + c + 1], scale=cols[:, LNW + c:LNW + c + 1])
                last.then_inc(S["n2T_ready"], 1)

            def silus(t):
                act.wait_ge(S["beta_mm"], t + 1)
                act.activation(th, bank(0, 256, 260), ACT.Tanh, scale=0.5).then_inc(S["beta_act"], 1)
                act.wait_ge(S["qk_mm"], t + 1)
                act.activation(qk, bank(1), ACT.Silu).then_inc(S["qk_act"], 1)

            def silu_v(t):
                act.wait_ge(S["v_mm"], t + 1)
                act.activation(y[1], bank(6), ACT.Silu).then_inc(S["v_act"], 1)

            def turned_qk(t):
                act.wait_ge(S["kT_mm"], t + 1)
                act.copy(kT, bank(3, 0, 256)).then_inc(S["kT_ready"], 1)
                act.wait_ge(S["kqT_mm"], t + 1)
                act.copy(kqT, bank(1)).then_inc(S["kqT_ready"], 1)

            def power_out(t, dst, name):
                act.wait_ge(S[name + "_mm"], t + 1)
                act.copy(dst, bank(3)).then_inc(S[name + "_ready"], 1)

            def slot(t, delta, attn, tail):
                nxt = delta and not is_last(t)
                if not attn and not delta:
                    act.wait_ge(S["route"], 2)
                    act.activation(lg[:, 0:(NT - 1) * E], lg[:, 0:(NT - 1) * E], ACT.Exp).then_inc(S["logit_exp"], 1)
                if attn:
                    act.wait_ge(S["oT_mm"], t)
                    act.activation(oT, bank(1), ACT.Copy, scale=cols[:, ONW:ONW + 1]).then_inc(S["oT_ready"], 1)
                if delta:
                    power_out(t, m2f, "m2")
                if tail:
                    act.wait_ge(S["pT_mm"], t - 1)
                    act.copy(pT, bank(7)).then_inc(S["pT_ready"], 1)
                    act.wait_ge(S["pv_mm"], t - 1)
                    for c in range(DC):
                        last = act.activation(aoT[:, c * P:(c + 1) * P], bank(6, c * P, (c + 1) * P), ACT.Identity,
                                              bias=cols[:, BV + c:BV + c + 1])
                    last.then_inc(S["aoT_ready"], 1)
                if nxt:
                    turned_norm(t + 1)
                if attn:
                    act.wait_ge(S["n3_mm"], t)
                    act.copy(n3T, bank(4, 0, 256)).then_inc(S["n3T_ready"], 1)
                if delta:
                    power_out(t, m4f, "m4")
                if nxt:
                    if not is_first(t):
                        act.wait_ge(S["silu_table"], t)
                    act.activation(spare_silu, spare_in, ACT.Silu).then_inc(S["silu_table"], 1)
                if attn:
                    act.wait_ge(S["av_mm"], t)
                    act.copy(vs, bank(4, 256, 512)).then_inc(S["vs_ready"], 1)
                if nxt:
                    silus(t + 1)
                if delta:
                    power_out(t, m8f, "m8")
                if tail:
                    act.wait_ge(S["x1T_mm"], t - 1)
                    for c in range(DC):
                        last = act.activation(x1T[:, c * P:(c + 1) * P], bank(7, 256 + c * P, 256 + (c + 1) * P),
                                              ACT.Identity, bias=cols[:, BE1 + c:BE1 + c + 1],
                                              scale=cols[:, G1 + c:G1 + c + 1])
                    last.then_inc(S["x1T_ready"], 1)
                if attn:
                    act.wait_ge(S["qkT_mm"], t)
                    act.copy(qT, bank(5, 0, 256)).then_inc(S["qT_ready"], 1)
                if delta:
                    act.wait_ge(S["o_mm"], t + 1)
                    for h in range(H):
                        last = act.activation(junk[:, h * DV:(h + 1) * DV], bank(0, h * DV, (h + 1) * DV),
                                              ACT.Square, accum_out=oss[:, h:h + 1])
                    last.then_inc(S["oss_ready"], 1)
                if nxt:
                    silu_v(t + 1)
                    turned_qk(t + 1)
                if attn:
                    if not (isinstance(t, int) and t == 1):
                        act.wait_ge(S["exp_table"], t - 1)
                    act.activation(spare_exp, spare_in, ACT.Exp).then_inc(S["exp_table"], 1)
                    act.wait_ge(S["centre"], 3 * t)
                    act.activation(sm, sm, ACT.Exp, scale=MD ** -0.5).then_inc(S["exp_ready"], 1)
            act.wait_ge(S["exponents_set"], 2)
            turned_norm(0)
            silus(0)
            silu_v(0)
            turned_qk(0)
            run_slots(act, slot)

            act.wait_ge(S["x1_ready"], NT)
            act.dma_start(x1_dram[(NT - 1) * P:NT * P, :], x1[:, NT - 1, :]).then_inc(S["x1_out"], 16)
            act.wait_ge(S["route"], RANKED + 2)
            act.activation(lg[:, (NT - 1) * E:], lg[:, (NT - 1) * E:], ACT.Exp).then_inc(S["logit_exp"], 1)
            act.wait_ge(S["combT_mm"], 1)
            act.copy(combT, ps[0:E, 1:3, :].rearrange("p a b -> p (a b)")).then_inc(S["combT_ready"], 1)

            act.wait_ge(S["route"], ROUTED)

            def moe_act(t, u):
                e = act.value_load(tilee[0:1, ds(t, 1)], min_val=0, max_val=E - 1)
                act.wait_ge(S["hT_mm"], t + 1)
                for f in range(FC):
                    last = act.activation(gT[u][:, f * P:(f + 1) * P], bank(2 * u + f // 4, f % 4 * P, f % 4 * P + P),
                                          ACT.Gelu, bias=cols[:, ds(e * FC + (B1 + f), 1)])
                last.then_inc(S["act_ready"], 1)
            with act.Fori(0, SLOT_TILES // 2) as i:
                for u in range(2):
                    moe_act(2 * i + u, u)
            moe_act(SLOT_TILES - 1, 0)

        @block.tensor
        def _(pe):
            pe.wait_ge(S["const_in"], 16)
            for half in range(2):
                pe.wait_ge(S[f"x_split{half}"], 3)
                for q in range(KC):
                    n = KC * half + q
                    if n >= 3:
                        pe.wait_ge(S["xT_ready" if (n - 3) % 2 else "xT_even_ready"], (n - 3) // 2 + 1)
                    for w in range(4):
                        mm = pe.transpose(bank(4 + n % 3, w * P, w * P + P),
                                          x_tok[half][:, w * KP + q * P:w * KP + (q + 1) * P], ident)
                    mm.then_inc(S["xT_mm"], 1)
                if half == 0:
                    pe.wait_ge(S["tokw_in"], 16)
                    for q in range(KC):
                        for c in range(DC):
                            n = q * DC + c
                            mm = pe.transpose(bank(n // 4, n % 4 * P, n % 4 * P + P), tokw[:, c * KP + q * P:c * KP + (q + 1) * P],
                                              ident)
                        if n % 4 == 3:
                            mm.then_inc(S["wT_mm"], 1)
                pe.wait_ge(S["xT_ready"], 3 * half + 3)
                pe.wait_ge(S["xT_even_ready"], 3 * half + 3)
                pe.wait_ge(S["wT_ready"], 3)
                for tt in range(4):
                    t = 4 * half + tt
                    if t >= 4:
                        pe.wait_ge(S["h_ready"], t - 3)
                    for q in range(KC):
                        mm = pe.matmul(bank(t % 4, 0, D), xT[half][:, q * 512 + tt * P:q * 512 + (tt + 1) * P],
                                       tokwT[:, q * D:(q + 1) * D], start=(q == 0), stop=(q == KC - 1))
                    mm.then_inc(S["emb_mm"], 1)
                if half == 0:
                    pe.wait_ge(S["rows_in"], 16 * 7)
                    pe.transpose(bank(7, 0, 75), rows[0:75, :], ident[0:75, 0:75]).then_inc(S["rows_mm"], 1)
            pe.wait_ge(S["attnw_in"], 16 * 5)
            pe.wait_ge(S["ffnw_in"], 16 * 6)

            def turn_norm(t):
                pe.wait_ge(S["n2_ready"], t + 1)
                for c in range(DC):
                    mm = pe.transpose(bank(0, c * P, (c + 1) * P), n2[:, c * P:(c + 1) * P], ident)
                mm.then_inc(S["n2_mm"], 1)

            def project(dst, lhsT, w, sem):
                for c in range(DC):
                    mm = pe.matmul(dst, lhsT[:, c * P:(c + 1) * P], w[:, c, :], start=(c == 0), stop=(c == DC - 1))
                mm.then_inc(S[sem], 1)

            def project_qk(t):
                project(bank(1), n2T, wqk_a, "qk_mm")

            def project_beta(t):
                pe.wait_ge(S["n2T_ready"], t + 1)
                project(bank(0, 256, 260), n2T, wb_a, "beta_mm")

            def turn_qk(t):
                pe.wait_ge(S["knorm_ready"], t + 1)
                for p in range(2):
                    mm = pe.transpose(bank(3, p * P, (p + 1) * P), qk[:, 256 + p * P:256 + (p + 1) * P], ident)
                mm.then_inc(S["kT_mm"], 1)
                pe.wait_ge(S["kb_ready"], t + 1)
                for p in range(2):
                    pe.transpose(bank(1, p * 256, p * 256 + P), kb[:, p * P:(p + 1) * P], ident)
                    mm = pe.transpose(bank(1, p * 256 + P, p * 256 + 256), qk[:, p * P:(p + 1) * P], ident)
                mm.then_inc(S["kqT_mm"], 1)

            def turn_power(t, src, wait, sem):
                pe.wait_ge(S[wait], t + 1)
                for h in range(H):
                    mm = pe.transpose(bank(3, h * P, (h + 1) * P), src[:, h * P:(h + 1) * P], ident)
                mm.then_inc(S[sem], 1)

            def heads(dst, width, lhsT, rhs, step, sem):
                for h in range(H):
                    mm = pe.matmul(dst[:, h * width:(h + 1) * width], lhsT[:, h * P:(h + 1) * P],
                                   rhs[:, h * step:h * step + width], start=True, stop=True)
                mm.then_inc(S[sem], 1)

            def key_products(t):
                for hp in range(2):
                    for par in range(2):
                        r = slice(64 * par, 64 * par + 64)
                        kq = kqT[r, hp * 256:hp * 256 + 256].rearrange("p (a k) -> p a k", a=2)
                        for j in range(P // W):
                            mm = pe.matmul(ps[W * j:W * j + W, 1 + par, hp * 2 * W:hp * 2 * W + 2 * W],
                                           kT[r, hp * P + W * j:hp * P + W * j + W], kq[:, :, W * j:W * j + W],
                                           start=True, stop=True)
                mm.then_inc(S["np_mm"], 1)
                for hp in range(2):
                    for par in range(2):
                        r = slice(64 * par, 64 * par + 64)
                        for j in range(P // W):
                            mm = pe.matmul(ps[W * j:W * j + W, 3 * par, hp * W:hp * W + W],
                                           kqT[r, hp * 256 + W * j:hp * 256 + W * j + W],
                                           kT[r, hp * P + W * j:hp * P + W * j + W], start=True, stop=True)
                mm.then_inc(S["m_mm"], 1)

            def slot(t, delta, attn, tail):
                nxt = delta and not is_last(t)
                if attn:
                    pe.wait_ge(S["on_ready"], t)
                    if delta:
                        pe.wait_ge(S["npc_ready"], t + 1)
                    for h in range(H):
                        mm = pe.transpose(bank(1, h * P, (h + 1) * P), on[:, h * P:(h + 1) * P], ident)
                    mm.then_inc(S["oT_mm"], 1)
                if delta:
                    pe.wait_ge(S["npc_ready"], t + 1)
                    pe.wait_ge(S["m_ready"], t + 1)
                    heads(bank(2), 2 * W, mf, nx[0], 2 * W, "nx1_mm")
                if attn:
                    pe.wait_ge(S["oT_ready"], t)
                    for h in range(H):
                        mm = pe.matmul(bank(5, 0, D), oT[:, h * P:(h + 1) * P], wo_a[:, h, :],
                                       start=(h == 0), stop=(h == H - 1))
                    mm.then_inc(S["wo_mm"], 1)
                if delta:
                    turn_power(t, n2f, "n2f_ready", "m2_mm")
                if tail:
                    pe.wait_ge(S["prob"], 3 * t - 3)
                    for c in range(4):
                        mm = pe.transpose(bank(7, c * P, (c + 1) * P), sm[:, c * P:(c + 1) * P], ident)
                    mm.then_inc(S["pT_mm"], 1)
                if delta:
                    pe.wait_ge(S["m2_ready"], t + 1)
                    heads(bank(2), 2 * W, m2f, nx[1], 2 * W, "nx2_mm")
                if tail:
                    pe.wait_ge(S["vbd_in"], 16 * 16 * (t - 1))
                    pe.wait_ge(S["pT_ready"], t - 1)
                    for hg in range(4):
                        for j in range(4):
                            col = hg // 2 * P + 32 * j
                            mm = pe.matmul(ps[64 * (hg % 2):64 * (hg % 2) + 64, 6, col:col + 32],
                                           vbd[:, j * 256 + hg * 64:j * 256 + hg * 64 + 64],
                                           pT[:, hg * P + 32 * j:hg * P + 32 * j + 32], start=True, stop=True)
                    mm.then_inc(S["pv_mm"], 1)
                if nxt:
                    turn_norm(t + 1)
                if attn:
                    pe.wait_ge(S["n3_ready"], t)
                    for c in range(DC):
                        mm = pe.transpose(bank(4, c * P, (c + 1) * P), n3[:, c * P:(c + 1) * P], ident)
                    mm.then_inc(S["n3_mm"], 1)
                if tail:
                    pe.wait_ge(S["aoT_ready"], t - 1)
                    project(bank(7, 0, D), aoT, wo_f, "awo_mm")
                if delta:
                    turn_power(t, n4f, "n4f_ready", "m4_mm")
                if attn:
                    pe.wait_ge(S["n3T_ready"], t)
                    project(bank(5), n3T, wqk_f, "aqk_mm")
                if delta:
                    pe.wait_ge(S["m4_ready"], t + 1)
                    heads(bank(2), 2 * W, m4f, nx[1], 2 * W, "nx3_mm")
                if attn:
                    project(bank(4, 256, 512), n3T, wv_f, "av_mm")
                if nxt:
                    project_beta(t + 1)
                    project_qk(t + 1)
                if delta:
                    turn_power(t, n8f, "n8f_ready", "m8_mm")
                if tail:
                    pe.wait_ge(S["x1n_ready"], t - 1)
                    for c in range(DC):
                        mm = pe.transpose(bank(7, 256 + c * P, 256 + (c + 1) * P), x1n[:, c * P:(c + 1) * P], ident)
                    mm.then_inc(S["x1T_mm"], 1)
                if delta:
                    pe.wait_ge(S["m8_ready"], t + 1)
                    heads(bank(2), W, m8f, nx[1][:, W:], 2 * W, "x4_mm")
                if attn:
                    pe.wait_ge(S["rope_ready"], t)
                    for c in range(4):
                        mm = pe.transpose(bank(5, c * P, (c + 1) * P), sm[:, c * P:(c + 1) * P], ident)
                    mm.then_inc(S["qkT_mm"], 1)
                if delta:
                    pe.wait_ge(S["xf_ready"], t + 1)
                    pe.wait_ge(S["y0_ready"], t + 1)
                    if nxt:
                        pe.wait_ge(S["beta_act"], t + 2)
                    for h in range(H):
                        g = h % 2 * 2 + h // 2
                        mm = pe.matmul(bank(0, h * P, (h + 1) * P), xf[:, g * P:(g + 1) * P], y[0][:, h * P:(h + 1) * P],
                                       start=True, stop=True)
                    mm.then_inc(S["o_mm"], 1)
                if nxt:
                    project(bank(6), n2T, wv_a, "v_mm")
                if attn:
                    pe.wait_ge(S["qT_ready"], t)
                    pe.wait_ge(S["kexp_ready"], t)
                    for g in range(2):
                        keys = kexp[:, g * 1024:(g + 1) * 1024].rearrange("p (h k) -> p h k", h=8)
                        for j in range(4):
                            mm = pe.matmul(ps[32 * j:32 * j + 32, 4, g * 256:g * 256 + 256],
                                           qT[:, g * P + 32 * j:g * P + 32 * j + 32],
                                           keys[:, :, 32 * j:32 * j + 32], start=True, stop=True)
                    mm.then_inc(S["score_mm"], 1)
                if nxt:
                    turn_qk(t + 1)
                if tail:
                    pe.wait_ge(S["x1T_ready"], t - 1)
                    pe.matmul(bank(7, 0, E), x1T[:, 0:P], wg_f[:, 0, :], start=True, stop=False)
                if nxt:
                    pe.wait_ge(S["on_ready"], t + 1)
                    pe.wait_ge(S["kT_ready"], t + 2)
                    pe.wait_ge(S["kqT_ready"], t + 2)
                if tail:
                    pe.matmul(bank(7, 0, E), x1T[:, P:D], wg_f[:, 1, :], start=False, stop=True).then_inc(S["gate_mm"], 1)
                if nxt:
                    key_products(t + 1)
            pe.wait_ge(S["h_ready"], NT)
            turn_norm(0)
            project_beta(0)
            project_qk(0)
            project(bank(6), n2T, wv_a, "v_mm")
            turn_qk(0)
            pe.wait_ge(S["kT_ready"], 1)
            pe.wait_ge(S["kqT_ready"], 1)
            key_products(0)
            run_slots(pe, slot)

            pe.wait_ge(S["routing_const_in"], 16)
            pe.wait_ge(S["logit_ready"], NT)
            pe.wait_ge(S["route"], CHOSEN)
            pe.matmul(bank(0, 0, 72), con[:, C_ONE:C_ONE + P], cum, start=True, stop=False, skip_group_check=True)
            pe.matmul(bank(0, 0, 64), con[:, C_UP:C_UP + P], chosen, start=False, stop=True,
                      skip_group_check=True).then_inc(S["count_mm"], 1)
            pe.wait_ge(S["route"], WEIGHED)
            for t in range(NT):
                mm = pe.transpose(ps[0:E, 1 + t // 4, t % 4 * P:t % 4 * P + P], comb[:, t * E:(t + 1) * E], ident)
            mm.then_inc(S["combT_mm"], 1)
            pe.wait_ge(S["combT_ready"], 1)
            for t in range(NT):
                mm = pe.matmul(bank(4 + t // 2, t % 2 * D, t % 2 * D + D), combT[:, t * P:(t + 1) * P], b2_f[:, :],
                               start=True, stop=True)
            mm.then_inc(S["b2_mm"], 1)
            for k, mapped in ((0, MAPPED0), (1, MAPPED1)):
                pe.wait_ge(S["route"], mapped)
                for t in range(NT):
                    n = k * NT + t
                    mm = pe.matmul(bank(3, 0, SLOT_TILES), onehot[k][:, t * P:(t + 1) * P],
                                   choice_col[:, n * SLOT_TILES:(n + 1) * SLOT_TILES],
                                   start=(n == 0), stop=(n == 2 * NT - 1))
            mm.then_inc(S["map_mm"], 1)

            pe.wait_ge(S["route"], ROUTED)
            pe.wait_ge(S["x1b_ready"], NT // 2)
            pe.wait_ge(S["w2lo_in"], 16 * (E // 2))
            pe.wait_ge(S["w2hi_in"], 16 * (E // 2))

            def turn_rows(t, u, wait_in, first):
                pe.wait_ge(S[f"slot_in{u}"], wait_in)
                if not first:
                    pe.wait_ge(S["xgT_ready"], t)
                for c in range(DC):
                    mm = pe.transpose(bank(7, c * P, (c + 1) * P), xg[u][:, c * P:(c + 1) * P], ident)
                mm.then_inc(S["xgT_mm"], 1)

            def up(t, u, first):
                pe.wait_ge(S["w1_staged"], t + 1)
                pe.wait_ge(S["xgT_ready"], t + 1)
                if not first:
                    pe.wait_ge(S["act_ready"], t - 1)
                for f in range(FC):
                    for c in range(DC):
                        mm = pe.matmul(bank(2 * u + f // 4, f % 4 * P, f % 4 * P + P),
                                       w1_stage[u][c][:, f * P:(f + 1) * P],
                                       xgT[u][:, c * P:(c + 1) * P], start=(c == 0), stop=(c == DC - 1))
                mm.then_inc(S["hT_mm"], 1)

            def down(t, u, e, first):
                pe.wait_ge(S["act_ready"], t + 1)
                if not first:
                    pe.wait_ge(S["ys_ready"], t)
                for f in range(FC):
                    mm = pe.matmul(bank(6, 0, D), gT[u][:, f * P:(f + 1) * P],
                                   w2[:, ds(e * (FC * D) + f * D, D)], start=(f == 0), stop=(f == FC - 1))
                mm.then_inc(S["down_mm"], 1)

            def expert(t):
                return pe.value_load(tilee[0:1, ds(t, 1)], min_val=0, max_val=E - 1)

            turn_rows(0, 0, 16, True)
            up(0, 0, True)
            turn_rows(1, 1, 16, False)
            up(1, 1, True)
            turn_rows(2, 0, 32, False)
            down(0, 0, expert(0), True)
            with pe.Fori(1, SLOT_TILES // 2) as i:
                up(2 * i, 0, False)
                turn_rows(2 * i + 1, 1, 16 * i + 16, False)
                down(2 * i - 1, 1, expert(2 * i - 1), False)
                up(2 * i + 1, 1, False)
                turn_rows(2 * i + 2, 0, 16 * i + 32, False)
                down(2 * i, 0, expert(2 * i), False)
            t = SLOT_TILES - 1
            up(t, 0, False)
            down(t - 1, 1, expert(t - 1), False)
            down(t, 0, expert(t), False)

            pe.wait_ge(S["x1b_ready"], NT)
            for t in range(NT):
                if t == 6:
                    pe.wait_ge(S["ys_ready"], SLOT_TILES)
                pe.matmul(bank(t, 0, D), ident, x1[:, t, :], start=True, stop=False)
            pe.wait_ge(S["diag_ready"], 3)
            for t in range(NT):
                pe.wait_ge(choices_in[t], 16)
                for k in range(2):
                    mm = pe.matmul(bank(t, 0, D), diag_of(k, t), yg[:, k, t, :], start=False, stop=(k == 1))
                mm.then_inc(S["combined_mm"], 1)

        @block.vector
        def _(dve):
            def split(half):
                dve.wait_ge(S[f"x_in{half}"], 48)
                for c in (0, 2):
                    x_split(dve.tensor_copy, half, c).then_inc(S[f"x_split{half}"], 1)

            def turned_patches(half):
                if half == 1:
                    dve.wait_ge(S["x_split0"], 3)
                for q in range(0, KC, 2):
                    dve.wait_ge(S["xT_mm"], KC * half + q + 1)
                    dve.tensor_copy(xT_out(half, q), xT_in(half, q)).then_inc(S["xT_even_ready"], 1)

            def embed(half):
                for tt in range(4):
                    t = 4 * half + tt
                    dve.wait_ge(S["emb_mm"], t + 1)
                    dve.tensor_tensor(hres[:, t, :], bank(t % 4, 0, D), tokb, ALU.add).then_inc(S["h_ready"], 1)
                    dve.wait_ge(S["h_ready"], t + 1)
                    dve.bn_stats(bst[t], hres[:, t, :]).then_inc(S["hstat_raw"], 1)
                    dve.wait_ge(S["hstat_raw"], t + 1)
                    dve.bn_aggr(mv1[:, 2 * t:2 * t + 2], bst[t]).then_inc(S["hstat_mv"], 1)
                a, b = 4 * half, 4 * half + 4
                dve.wait_ge(S["hstat_mv"], b)
                dve.tensor_scalar(ve1[:, a:b], mv1.rearrange("p (t k) -> p t k", k=2)[:, a:b, 1], EPS, None,
                                  ALU.add).then_inc(S["hstat_ready"], 1)

            def first_norm(half):
                dve.wait_ge(S["r1_ready"], half + 1)
                for t in range(4 * half, 4 * half + 4):
                    dve.tensor_scalar(x1[:, t, :], hres[:, t, :], mv1[:, 2 * t:2 * t + 1], r1[:, t:t + 1],
                                      ALU.subtract, ALU.mult).then_inc(S["n1_ready"], 1)
            split(0)
            turned_patches(0)
            for n in range(3):
                dve.wait_ge(S["wT_mm"], n + 1)
                dve.tensor_copy(tokwT[:, n * 512:(n + 1) * 512], bank(n)).then_inc(S["wT_ready"], 1)
            split(1)
            dve.wait_ge(S["bias_in"], 16 * 9)
            embed(0)
            turned_patches(1)
            first_norm(0)
            embed(1)
            first_norm(1)

            def centred_rows(t):
                sm_ = sm.rearrange("p (h k) -> p h k", h=MH)
                dve.wait_ge(S["score_mm"], t)
                dve.tensor_tensor(sm_, bank(4).rearrange("p (h k) -> p h k", h=MH),
                                  rep(con[:, C_KEYB:C_KEYB + 32][:, None, :], [P, MH, 32]), ALU.add).then_inc(S["centre"], 1)
                dve.wait_ge(S["centre"], 3 * t - 2)
                dve.tensor_reduce(mx, sm_, AX, ALU.max).then_inc(S["centre"], 1)
                dve.wait_ge(S["centre"], 3 * t - 1)
                dve.tensor_tensor(sm_, sm_, rep(mx[:, :, None], [P, MH, 32]), ALU.subtract).then_inc(S["centre"], 1)

            def probabilities(t):
                sm_ = sm.rearrange("p (h k) -> p h k", h=MH)
                dve.wait_ge(S["exp_ready"], t)
                dve.tensor_reduce(sums, sm_, AX, ALU.add).then_inc(S["prob"], 1)
                dve.wait_ge(S["prob"], 3 * t - 2)
                dve.reciprocal(recs, sums).then_inc(S["prob"], 1)
                dve.wait_ge(S["prob"], 3 * t - 1)
                dve.tensor_tensor(sm_, sm_, rep(recs[:, :, None], [P, MH, 32]), ALU.mult).then_inc(S["prob"], 1)

            def both(ap):
                ap = packed(ap)
                return ap[:, :, 0:W], ap[:, :, W:2 * W]

            def stationary(dst, src, sem):
                dve.tensor_tensor(dst.rearrange("p (h j c) -> p h j c", h=H, j=P // W), rep(src[:, :, None, :], [P, H, P // W, W]),
                                  rep(con[:, C_G:C_G + P // W][:, None, :, None], [P, H, P // W, W]), ALU.mult).then_inc(S[sem], 1)

            def qk_squares(t):
                dve.wait_ge(S["beta_act"], t + 1)
                dve.tensor_scalar(beta, th, 0.5, 0.5, ALU.mult, ALU.add).then_inc(S["beta_ready"], 1)
                dve.wait_ge(S["qk_act"], t + 1)
                dve.tensor_tensor(sq, qk, qk, ALU.mult).then_inc(S["ssq"], 1)
                dve.wait_ge(S["ssq"], 3 * t + 1)
                dve.tensor_reduce(ssq0, sq.rearrange("p (h d) -> p h d", h=8), AX, ALU.add).then_inc(S["ssq"], 1)
                dve.wait_ge(S["ssq"], 3 * t + 2)
                dve.tensor_scalar(ssq, ssq0, 1e-6, None, ALU.add).then_inc(S["ssq"], 1)

            def v_scaled(t):
                dve.wait_ge(S["v_act"], t + 1)
                dve.wait_ge(S["beta_ready"], t + 1)
                dve.tensor_tensor(heads4(y[0]), heads4(y[1]), rep(beta[:, :, None], [P, H, DV]),
                                  ALU.mult).then_inc(S["y0_ready"], 1)

            def qk_scaled(t):
                q, k = (qk[:, c * 256:(c + 1) * 256].rearrange("p (h d) -> p h d", h=H) for c in range(2))
                dve.wait_ge(S["rn_ready"], t + 1)
                dve.tensor_tensor(k, k, rep(rn[:, H:2 * H][:, :, None], [P, H, DK]), ALU.mult).then_inc(S["qnorm_ready"], 1)
                dve.scalar_tensor_tensor(q, q, DK ** -0.5, rep(rn[:, 0:H][:, :, None], [P, H, DK]),
                                         ALU.mult, ALU.mult).then_inc(S["knorm_ready"], 1)
                dve.wait_ge(S["qnorm_ready"], t + 1)
                dve.tensor_tensor(kb.rearrange("p (h d) -> p h d", h=H), k, rep(beta[:, :, None], [P, H, DK]),
                                  ALU.mult).then_inc(S["kb_ready"], 1)

            def grow(t, src, add, k, dst):
                dve.wait_ge(S[f"nx{k}_mm"], t + 1)
                n_, x_ = both(bank(2))
                dve.tensor_tensor(both(nx[1])[1], both(src)[1], x_, add)
                if k < 3:
                    dve.tensor_copy(both(nx[1])[0], n_)
                stationary(dst, n_, f"n{2 ** k}f_ready")

            def masked(t):
                dve.wait_ge(S["np_mm"], t + 1)
                dve.tensor_tensor(nx[0].rearrange("p (a g c) -> p a g c", a=2, g=2),
                                  ps[:, 1:3, 0:4 * W].rearrange("p a (g c) -> p a g c", g=2),
                                  rep(con[:, C_NP:C_NP + 2 * W][:, None, None, :], [P, 2, 2, 2 * W]),
                                  ALU.mult).then_inc(S["npc_ready"], 1)
                dve.wait_ge(S["m_mm"], t + 1)
                for par in range(2):
                    last = dve.tensor_tensor(
                        mf[:, par * 256:par * 256 + 256].rearrange("p (g j c) -> p g j c", g=2, j=P // W),
                        rep(bank(3 * par, 0, 2 * W).rearrange("p (g c) -> p g c", g=2)[:, :, None, :], [P, 2, P // W, W]),
                        rep(con[:, C_MF:C_MF + P].rearrange("p (j c) -> p j c", j=P // W)[:, None, :, :],
                            [P, 2, P // W, W]), ALU.mult)
                last.then_inc(S["m_ready"], 1)

            steps = [0]

            def link(ins):
                steps[0] += 1
                ins.then_inc(S["route"], 1)
                dve.wait_ge(S["route"], steps[0])

            def te(ap):
                return ap.rearrange("p (t e) -> p t e", e=E)

            def choose(a, b):
                n = b - a

                def part(ap):
                    return ap[:, a * E:b * E]
                top, total_ = lmax[:, a:b], lsum[:, a:b]
                link(dve.tensor_reduce(top, te(part(lg)), AX, ALU.max))
                link(dve.tensor_tensor(te(part(lg)), te(part(lg)), rep(top[:, :, None], [P, n, E]), ALU.subtract))
                dve.wait_ge(S["logit_exp"], 1 if a == 0 else 2)
                link(dve.tensor_reduce(total_, te(part(lg)), AX, ALU.add))
                link(dve.reciprocal(total_, total_))
                link(dve.tensor_tensor(te(part(prob)), te(part(lg)), rep(total_[:, :, None], [P, n, E]), ALU.mult))
                four = [P, n, E, E]
                mine, other = rep(te(part(prob))[:, :, :, None], four), rep(te(part(prob))[:, :, None, :], four)
                more, same = ahead[:, 0:n * E * E], tied[:, 0:n * E * E]
                link(dve.tensor_tensor(more.rearrange("p (t e j) -> p t e j", e=E, j=E), other, mine, ALU.is_gt))
                link(dve.tensor_tensor(same.rearrange("p (t e j) -> p t e j", e=E, j=E), other, mine, ALU.is_equal))
                link(dve.tensor_tensor(same.rearrange("p (t c) -> p t c", t=n), same.rearrange("p (t c) -> p t c", t=n),
                                       rep(con[:, C_LT:C_LT + 64][:, None, :], [P, n, 64]), ALU.mult))
                link(dve.tensor_tensor(more, more, same, ALU.add))
                link(dve.tensor_reduce(part(rank), more.rearrange("p (c j) -> p c j", j=E), AX, ALU.add))
                link(dve.tensor_scalar(part(sel0), part(rank), 0.5, None, ALU.is_lt))
                link(dve.tensor_scalar(part(chosen), part(rank), 1.5, None, ALU.is_lt))
                assert steps[0] % RANKED == 0

            def slot(t, delta, attn, tail):
                nxt = delta and not is_last(t)
                if not attn and not delta:
                    dve.wait_ge(S["routing_const_in"], 16)
                    dve.wait_ge(S["logit_ready"], NT - 1)
                    choose(0, NT - 1)
                if delta:
                    grow(t, nx[0], ALU.subtract, 1, n2f)
                    v_scaled(t)
                if attn:
                    dve.wait_ge(S["wo_mm"], t)
                    dve.tensor_tensor(h2, tile_of(hres, t - 1), bank(5, 0, D), ALU.add).then_inc(S["h2s_ready"], 1)
                    dve.wait_ge(S["h2s_ready"], t)
                    dve.bn_stats(bst[0], h2).then_inc(S["h2stat"], 1)
                    dve.wait_ge(S["h2stat"], 3 * t - 2)
                    dve.tensor_tensor(tile_of(hres, t - 1), tile_of(hres, t - 1), bank(5, 0, D), ALU.add).then_inc(S["h2_ready"], 1)
                    dve.bn_aggr(mv3, bst[0]).then_inc(S["h2stat"], 1)
                    dve.wait_ge(S["h2stat"], 3 * t - 1)
                    dve.tensor_scalar(ve3, mv3[:, 1:2], EPS, None, ALU.add).then_inc(S["h2stat"], 1)
                if attn:
                    dve.wait_ge(S["r3_ready"], t)
                    dve.tensor_scalar(n3, h2, mv3[:, 0:1], r3, ALU.subtract, ALU.mult).then_inc(S["n3_ready"], 1)
                if delta:
                    grow(t, nx[1], ALU.add, 2, n4f)
                if tail:
                    dve.wait_ge(S["awo_mm"], t - 1)
                    dve.wait_ge(S["n3b_ready"], t - 1)
                    dve.tensor_tensor(xa, bank(7, 0, D), n3b, ALU.add).then_inc(S["xa_ready"], 1)
                    dve.wait_ge(S["xa_ready"], t - 1)
                    dve.bn_stats(bst[1], xa).then_inc(S["xastat"], 1)
                    dve.wait_ge(S["xastat"], 3 * t - 5)
                    dve.memset(spare, 0.0)
                    dve.bn_aggr(mv4, bst[1]).then_inc(S["xastat"], 1)
                    dve.wait_ge(S["xastat"], 3 * t - 4)
                    dve.tensor_scalar(ve4, mv4[:, 1:2], EPS, None, ALU.add).then_inc(S["xastat"], 1)
                    dve.wait_ge(S["r4_ready"], t - 1)
                    dve.tensor_scalar(x1n, xa, mv4[:, 0:1], r4, ALU.subtract, ALU.mult).then_inc(S["x1n_ready"], 1)
                if attn:
                    dve.wait_ge(S["aqk_mm"], t)
                    dve.tensor_tensor(qkb, bank(5), bqk, ALU.add).then_inc(S["qkb_ready"], 1)
                if delta:
                    grow(t, nx[1], ALU.add, 3, n8f)
                if attn:
                    dve.wait_ge(S["qkb_ready"], t)
                    x, z = (v.rearrange("p (h s f) -> p h s f", s=2, f=8) for v in (qkb, tb))
                    for s in range(2):
                        last = dve.tensor_tensor(z[:, :, s, :], x[:, :, 1 - s, :],
                                                 rep(con[:, C_SIN + 8 * s:C_SIN + 8 * s + 8][:, None, :], [P, 32, 8]), ALU.mult)
                    last.then_inc(S["ropeb_ready"], 1)
                    dve.wait_ge(S["ropea_ready"], t)
                    dve.wait_ge(S["ropeb_ready"], t)
                    dve.tensor_tensor(sm, ta, tb, ALU.add).then_inc(S["rope_ready"], 1)
                if nxt:
                    qk_squares(t + 1)
                if delta:
                    dve.wait_ge(S["x4_mm"], t + 1)
                    dve.tensor_tensor(both(nx[1])[1], both(nx[1])[1], packed(bank(2, 0, H * W)), ALU.add).then_inc(S["x4_ready"], 1)
                    dve.wait_ge(S["x4_ready"], t + 1)
                    stationary(xf, both(nx[1])[1], "xf_ready")
                if attn:
                    dve.wait_ge(S["qT_ready"], t)
                    dve.tensor_tensor(kexp.rearrange("p (g h k) -> p g h k", g=2, h=8),
                                      rep(bank(5, 256, 512).rearrange("p (g k) -> p g k", g=2)[:, :, None, :], [P, 2, 8, P]),
                                      rep(con[:, C_HM:C_HM + 8][:, None, :, None], [P, 2, 8, P]),
                                      ALU.mult).then_inc(S["kexp_ready"], 1)
                if delta:
                    dve.wait_ge(S["oss_ready"], t + 1)
                    dve.tensor_scalar(orv, oss, 1.0 / DV, EPS, ALU.mult, ALU.add).then_inc(S["orv_ready"], 1)
                if nxt:
                    qk_scaled(t + 1)
                if tail:
                    dve.wait_ge(S["x1g_ready"], t - 1)
                    dve.tensor_tensor(tile_of(x1, t - 2), x1n, be1, ALU.add).then_inc(S["x1_ready"], 1)
                if delta:
                    dve.wait_ge(S["orms_ready"], t + 1)
                    dve.tensor_tensor(heads4(on), heads4(bank(0)), rep(orms[:, :, None], [P, H, DV]),
                                      ALU.mult).then_inc(S["on_ready"], 1)
                if attn:
                    centred_rows(t)
                if nxt:
                    masked(t + 1)
                if tail:
                    dve.wait_ge(S["gate_mm"], t - 1)
                    dve.tensor_tensor(lg[:, ds((t - 2) * E, E)], bank(7, 0, E), bg, ALU.add).then_inc(S["logit_ready"], 1)
                if attn:
                    probabilities(t)
            qk_squares(0)
            qk_scaled(0)
            masked(0)
            dve.wait_ge(S["hres_ready"], NT)
            run_slots(dve, slot)

            dve.wait_ge(S["logit_ready"], NT)
            choose(NT - 1, NT)
            src = chosen
            for n, dst in ((E, lead0), (2 * E, lead1), (4 * E, cum[:, E:E + 64])):
                if n == E:
                    dve.memset(cum[:, 0:E], 0.0).then_inc(S["route"], 1)
                    steps[0] += 1
                dve.tensor_copy(dst[:, 0:n], src[:, 0:n]).then_inc(S["route"], 1)
                steps[0] += 1
                link(dve.tensor_tensor(dst[:, n:64], src[:, n:64], src[:, 0:64 - n], ALU.add))
                src = dst
            assert steps[0] == CHOSEN
            dve.tensor_tensor(sel1, chosen, sel0, ALU.subtract).then_inc(S["route"], 1)
            steps[0] += 1
            link(dve.tensor_tensor(comb, prob, chosen, ALU.mult))
            link(dve.tensor_reduce(lsum, te(comb), AX, ALU.add))
            link(dve.reciprocal(lsum, lsum))
            link(dve.tensor_tensor(te(comb), te(comb), rep(lsum[:, :, None], [P, NT, E]), ALU.mult))
            assert steps[0] == WEIGHED
            dve.wait_ge(S["count_mm"], 1)
            link(dve.tensor_copy(total, bank(0, 64, 72)))
            link(dve.tensor_tensor(te(pick), rep(total[:, :, None], [P, E, 8]),
                                   rep(con[:, C_TH:C_TH + 8][:, None, :], [P, E, 8]), ALU.is_gt))
            link(dve.tensor_reduce(tiles, te(pick), AX, ALU.add))
            link(dve.tensor_tensor(te(pick), rep(tiles[:, None, :], [P, E, E]), te(con[:, C_LT:C_LT + 64]), ALU.mult))
            link(dve.tensor_reduce(begin, te(pick), AX, ALU.add))
            link(dve.scalar_tensor_tensor(te(place), rep(begin[:, None, :], [P, NT, E]), float(P),
                                          te(bank(0, 0, 64)), ALU.mult, ALU.add))
            for s, sel in enumerate((sel0, sel1)):
                link(dve.tensor_tensor(pick, place, sel, ALU.mult))
                link(dve.tensor_reduce(slots[:, s * NT:(s + 1) * NT], te(pick), AX, ALU.add))
            by_tile = [P, 2 * NT, SLOT_TILES]
            grid, cols_ = (v.rearrange("p (c j) -> p c j", j=SLOT_TILES) for v in (tile_ends, choice_col))
            link(dve.tensor_tensor(grid, rep(slots[:, :, None], by_tile),
                                   rep(con[:, C_SE:C_SE + SLOT_TILES][:, None, :], by_tile), ALU.is_ge))
            link(dve.tensor_reduce(slot_tile, grid, AX, ALU.add))
            link(dve.scalar_tensor_tensor(in_tile, slot_tile, -float(P), slots, ALU.mult, ALU.add))
            link(dve.tensor_tensor(cols_, rep(slot_tile[:, :, None], by_tile),
                                   rep(con[:, C_SL:C_SL + SLOT_TILES][:, None, :], by_tile), ALU.is_equal))
            link(dve.tensor_tensor(cols_, cols_, rep(con[:, C_CHO:C_CHO + 2 * NT][:, :, None], by_tile), ALU.mult))
            for k, mapped in ((0, MAPPED0), (1, MAPPED1)):
                dve.tensor_tensor(onehot[k].rearrange("p (t s) -> p t s", s=P),
                                  rep(in_tile[:, k * NT:(k + 1) * NT][:, :, None], [P, NT, P]),
                                  rep(con[:, C_IO:C_IO + P][:, None, :], [P, NT, P]), ALU.is_equal).then_inc(S["route"], 1)
                steps[0] += 1
                assert steps[0] == mapped, steps
            link(dve.tensor_tensor(end, begin, tiles, ALU.add))
            ends = tile_ends[:, 0:SLOT_TILES * E].rearrange("p (j e) -> p j e", e=E)
            link(dve.tensor_tensor(ends, rep(end[:, None, :], [P, SLOT_TILES, E]),
                                   rep(con[:, C_SL:C_SL + SLOT_TILES][:, :, None], [P, SLOT_TILES, E]), ALU.is_le))
            link(dve.tensor_reduce(owner, ends, AX, ALU.add))
            dve.tensor_scalar(tilee[:, :], owner, float(E - 1), None, ALU.min)
            dve.wait_ge(S["map_mm"], 1)
            dve.tensor_copy(choice, bank(3, 0, SLOT_TILES)).then_inc(S["route"], 1)
            steps[0] += 1
            link(dve.tensor_scalar(second, bank(3, 0, SLOT_TILES), float(TOK) + 0.5, -float(TOK), ALU.is_gt, ALU.mult))
            link(dve.tensor_tensor(second, second, choice, ALU.add))
            link(dve.tensor_scalar(slot_tok[:, :], second, -1.0, 0.0, ALU.add, ALU.max))
            assert steps[0] == ROUTED
            def stage(t, u, first):
                e = dve.value_load(tilee[0:1, ds(t, 1)], min_val=0, max_val=E - 1)
                if not first:
                    dve.wait_ge(S["hT_mm"], t - 1)
                for c in range(DC):
                    last = dve.tensor_copy(w1_stage[u][c], w1[:, ds(e * (DC * FF) + c * FF, FF)])
                last.then_inc(S["w1_staged"], 1)

            def rows_out(t, u):
                dve.wait_ge(S["xgT_mm"], t + 1)
                dve.tensor_copy(xgT[u], bank(7, 0, D)).then_inc(S["xgT_ready"], 1)

            def output_out(t, u, y_sent):
                dve.wait_ge(S["down_mm"], t + 1)
                if y_sent is not None:
                    dve.wait_ge(S[f"y_out{u}"], y_sent)
                dve.tensor_copy(ys[u], bank(6, 0, D)).then_inc(S["ys_ready"], 1)

            def second_bias(a, b):
                for t in range(a, b):
                    dve.tensor_tensor(x1[:, t, :], x1[:, t, :], bank(4 + t // 2, t % 2 * D, t % 2 * D + D),
                                      ALU.add).then_inc(S["x1b_ready"], 1)
            dve.wait_ge(S["w1_in"], 16 * E)
            stage(0, 0, True)
            dve.wait_ge(S["b2_mm"], 1)
            dve.wait_ge(S["x1_out"], 16 * NT)
            second_bias(NT // 2, NT)
            rows_out(0, 0)
            link(dve.tensor_scalar(second, choice, 0.5, None, ALU.is_lt))
            link(dve.tensor_tensor(second, second, con[:, C_FREE:C_FREE + SLOT_TILES], ALU.mult))
            link(dve.tensor_tensor(second, second, choice, ALU.add))
            link(dve.tensor_scalar(slot_row[:, :], second, -1.0, None, ALU.add))
            for s, sel in enumerate((sel0, sel1)):
                link(dve.tensor_tensor(pick, comb, sel, ALU.mult))
                link(dve.tensor_reduce(wsel[:, s * NT:(s + 1) * NT], te(pick), AX, ALU.add))
            assert steps[0] == WEIGHTS
            stage(1, 1, True)
            rows_out(1, 1)
            second_bias(0, NT // 2)
            stage(2, 0, False)
            rows_out(2, 0)
            stage(3, 1, False)
            output_out(0, 0, None)
            rows_out(3, 1)
            stage(4, 0, False)
            output_out(1, 1, None)
            with dve.Fori(2, SLOT_TILES // 2) as i:
                rows_out(2 * i, 0)
                stage(2 * i + 1, 1, False)
                output_out(2 * i - 2, 0, 16 * i - 16)
                rows_out(2 * i + 1, 1)
                stage(2 * i + 2, 0, False)
                output_out(2 * i - 1, 1, 16 * i - 16)
            t = SLOT_TILES - 1
            rows_out(t, 0)
            output_out(t - 2, 0, 16 * (t // 2 - 1))
            output_out(t - 1, 1, 16 * (t // 2 - 1))
            output_out(t, 0, 16 * (t // 2))

            n = [0]

            def step(ins):
                n[0] += 1
                ins.then_inc(S["tail"], 1)
                return n[0]

            for t in range(NT + 1):
                if t < NT:
                    dve.wait_ge(S["combined_mm"], t + 1)
                    new = step(dve.bn_stats(bst[t], bank(t, 0, D)))
                if t >= 1:
                    dve.wait_ge(S["tail"], scaled)
                    dve.wait_ge(S["hb_ready"], t)
                    dve.wait_ge(S["r5_ready"], t)
                    dve.scalar_tensor_tensor(fin[:, t - 1, :], x1[:, t - 1, :], r5[:, t - 1:t], hres[:, t - 1, :],
                                             ALU.mult, ALU.add).then_inc(S["fin_ready"], 1)
                if t < NT:
                    dve.wait_ge(S["tail"], new)
                    new = step(dve.bn_aggr(mv5[:, 2 * t:2 * t + 2], bst[t]))
                    dve.wait_ge(S["tail"], new)
                    dve.tensor_scalar(ve5[:, t:t + 1], mv5[:, 2 * t + 1:2 * t + 2], EPS, None,
                                      ALU.add).then_inc(S["ve5_ready"], 1)
                    scaled = step(dve.scalar_tensor_tensor(x1[:, t, :], bank(t, 0, D), mv5[:, 2 * t:2 * t + 1], g2,
                                                           ALU.subtract, ALU.mult))


INPUTS = ["x", "L0_tok_W", "L0_tok_b", "L0_attn_ln_w", "L0_attn_ln_b", "L0_attn_Wq", "L0_attn_Wk", "L0_attn_Wv",
          "L0_attn_Wb", "L0_attn_o_norm_w", "L0_attn_Wo", "L0_ffn_Wq", "L0_ffn_bq", "L0_ffn_Wk", "L0_ffn_bk",
          "L0_ffn_Wv", "L0_ffn_bv", "L0_ffn_Wo", "L0_ffn_bo", "L0_ffn_Wg", "L0_ffn_bg", "L0_ffn_W1", "L0_ffn_b1",
          "L0_ffn_W2", "L0_ffn_b2", "L0_ffn_g1", "L0_ffn_be1", "L0_ffn_g2", "L0_ffn_be2"]


def kernel(**inputs):
    import concourse.bacc as bacc
    from concourse.bass_utils import run_bass_kernel_spmd

    nc = bacc.Bacc("TRN2", target_bir_lowering=False, num_devices=1)
    arrays = {"in_" + name: np.ascontiguousarray(inputs[name]) for name in INPUTS}
    arrays["in_consts"] = constants()
    aps = {name[3:]: nc.dram_tensor(name, a.shape, F32, kind="ExternalInput").ap() for name, a in arrays.items()}
    out = nc.dram_tensor("out", (TOK, D), F32, kind="ExternalOutput").ap()
    tower(nc, aps, out)
    result = run_bass_kernel_spmd(nc, [arrays], core_ids=[0])
    return result.results[0]["out"].reshape(IMGS, SEQ, D)
```
